# Optimizing a Trainium2 kernel written in Bass

```python
import numpy as np
import jax
import jax.numpy as jnp

def _softmax(x, axis=-1):
    return jax.nn.softmax(x, axis=axis)

def _gelu(x):
    return jax.nn.gelu(x, approximate=True)

def _silu(x):
    return jax.nn.silu(x)

def _sigmoid(x):
    return jax.nn.sigmoid(x)

def _layernorm(x, axis=-1, eps=1e-05):
    m = jnp.mean(x, axis=axis, keepdims=True)
    v = jnp.var(x, axis=axis, keepdims=True)
    return (x - m) / jnp.sqrt(v + eps)

def _scatter_add(tgt, idx, src, axis=0):
    return tgt.at[idx].add(src)

def _segment_sum(src, seg, n):
    return jax.ops.segment_sum(src, seg, n)
kernel_name = 'mk_sandwich_d1_jaxref_r4_dc91ae'

def setup_inputs(seed: int=0):
    np.random.seed(seed)
    _w = jnp.asarray

    def _L0_attn_setup():
        import jax, jax.numpy as jnp
        import numpy as np
        B, L, D, S, K, FF = (2, 1024, 256, 16, 3, 672)
        EPS = 1e-06

        def rmsnorm(x, w):
            var = jnp.mean(x * x, axis=-1, keepdims=True)
            return x * jax.lax.rsqrt(var + EPS) * w
        key = jax.random.key(seed)
        ks = jax.random.split(key, 12)
        return {'u': jax.random.normal(ks[0], (B, L, D), jnp.float32), 'pre_norm_w': jnp.ones((D,), jnp.float32), 'in_proj_w': jax.random.normal(ks[1], (3 * D, D), jnp.float32) * D ** (-0.5), 'short_w': jax.random.normal(ks[2], (3 * D, 1, K), jnp.float32) * 0.3, 'short_b': jax.random.normal(ks[3], (3 * D,), jnp.float32) * 0.02, 'log_poles': -(jax.random.uniform(ks[4], (D, S, 1), jnp.float32) * 0.3 + 0.001), 'residues': jax.random.normal(ks[5], (D, S), jnp.float32) * S ** (-0.5), 'D_skip': jax.random.normal(ks[6], (D,), jnp.float32) * 0.02, 'out_proj_w': jax.random.normal(ks[7], (D, D), jnp.float32) * D ** (-0.5), 'post_norm_w': jnp.ones((D,), jnp.float32), 'l1_w': jax.random.normal(ks[8], (FF, D), jnp.float32) * D ** (-0.5), 'l2_w': jax.random.normal(ks[9], (FF, D), jnp.float32) * D ** (-0.5), 'l3_w': jax.random.normal(ks[10], (D, FF), jnp.float32) * FF ** (-0.5)}
    _L0_attn_in = _L0_attn_setup()

    def _L0_ffn_setup():
        import jax, jax.numpy as jnp
        import numpy as np
        LORA_DIM = 16
        LORA_TOKEN_INDEX = 1
        B, S, D, H = (4, 512, 256, 1024)
        key = jax.random.key(seed)
        ks = jax.random.split(key, 6)
        x = jax.random.normal(ks[0], (B, S, D), dtype=jnp.float32)
        W1 = jax.random.normal(ks[1], (H, D), dtype=jnp.float32) * 0.02
        b1 = jnp.zeros((H,), dtype=jnp.float32)
        W2 = jax.random.normal(ks[2], (D, H), dtype=jnp.float32) * 0.02
        b2 = jnp.zeros((D,), dtype=jnp.float32)
        scale = jnp.asarray(0.001, dtype=jnp.float32)
        return {'x': x, 'W1': W1, 'b1': b1, 'W2': W2, 'b2': b2, 'scale': scale}
    _L0_ffn_in = _L0_ffn_setup()
    _d = {'L0_attn_u': _L0_attn_in['u'], 'L0_attn_pre_norm_w': _L0_attn_in['pre_norm_w'], 'L0_attn_in_proj_w': _L0_attn_in['in_proj_w'], 'L0_attn_short_w': _L0_attn_in['short_w'], 'L0_attn_short_b': _L0_attn_in['short_b'], 'L0_attn_log_poles': _L0_attn_in['log_poles'], 'L0_attn_residues': _L0_attn_in['residues'], 'L0_attn_D_skip': _L0_attn_in['D_skip'], 'L0_attn_out_proj_w': _L0_attn_in['out_proj_w'], 'L0_attn_post_norm_w': _L0_attn_in['post_norm_w'], 'L0_attn_l1_w': _L0_attn_in['l1_w'], 'L0_attn_l2_w': _L0_attn_in['l2_w'], 'L0_attn_l3_w': _L0_attn_in['l3_w'], 'L0_ffn_W1': _L0_ffn_in['W1'], 'L0_ffn_b1': _L0_ffn_in['b1'], 'L0_ffn_W2': _L0_ffn_in['W2'], 'L0_ffn_b2': _L0_ffn_in['b2'], 'L0_ffn_scale': _L0_ffn_in['scale']}
    _x0 = _d['L0_attn_u']
    _d['L0_attn_u'] = jax.random.normal(jax.random.fold_in(jax.random.key(seed), 1), (2, 4096, 256), dtype=_x0.dtype)
    del _x0
    return _d

def reference(L0_attn_u, L0_attn_pre_norm_w, L0_attn_in_proj_w, L0_attn_short_w, L0_attn_short_b, L0_attn_log_poles, L0_attn_residues, L0_attn_D_skip, L0_attn_out_proj_w, L0_attn_post_norm_w, L0_attn_l1_w, L0_attn_l2_w, L0_attn_l3_w, L0_ffn_W1, L0_ffn_b1, L0_ffn_W2, L0_ffn_b2, L0_ffn_scale):

    def _L0_attn_ref(u, pre_norm_w, in_proj_w, short_w, short_b, log_poles, residues, D_skip, out_proj_w, post_norm_w, l1_w, l2_w, l3_w):
        import jax, jax.numpy as jnp
        import numpy as np
        B, L, D, S, K, FF = (2, 1024, 256, 16, 3, 672)
        EPS = 1e-06

        def rmsnorm(x, w):
            var = jnp.mean(x * x, axis=-1, keepdims=True)
            return x * jax.lax.rsqrt(var + EPS) * w
        Lc = u.shape[1]
        z = rmsnorm(u, pre_norm_w) @ in_proj_w.T
        zc = z.transpose(0, 2, 1)
        z_pre = jax.lax.conv_general_dilated(zc, short_w, window_strides=(1,), padding=[(K - 1, 0)], dimension_numbers=('NCH', 'OIH', 'NCH'), feature_group_count=3 * D)
        z_pre = z_pre + short_b[None, :, None]
        x2, x1, v = jnp.split(z_pre, 3, axis=1)
        t = jnp.arange(Lc, dtype=jnp.float32)
        h = jnp.sum(residues[:, :, None] * jnp.exp(log_poles * t[None, None, :]), axis=1)
        xv = x1 * v
        n = 2 * Lc
        Xf = jnp.fft.rfft(xv, n=n)
        Hf = jnp.fft.rfft(h, n=n)
        yconv = jnp.fft.irfft(Xf * Hf[None], n=n)[..., :Lc]
        y = (yconv + xv * D_skip[None, :, None]) * x2
        y = y.transpose(0, 2, 1)
        y = y @ out_proj_w.T + u
        zm = rmsnorm(y, post_norm_w)
        mlp = jax.nn.gelu(zm @ l1_w.T) * (zm @ l2_w.T) @ l3_w.T
        return y + mlp

    def _L0_ffn_ref(x, W1, b1, W2, b2, scale):
        import jax, jax.numpy as jnp
        import numpy as np
        LORA_DIM = 16
        LORA_TOKEN_INDEX = 1
        B, S, D, H = (4, 512, 256, 1024)
        Bx, Sx, Dx = x.shape
        Hx = W1.shape[0]
        lt = jax.lax.dynamic_slice_in_dim(x, LORA_TOKEN_INDEX, LORA_DIM, axis=1)
        even = lt[:, ::2, :]
        odd = lt[:, 1::2, :]
        m1 = (even[:, :4, :, None] * odd[:, :4, None, :]).reshape(Bx, Hx, Dx)
        m2 = (even[:, 4:, :, None] * odd[:, 4:, None, :]).reshape(Bx, Dx, Hx)
        h = jnp.einsum('bsd,hd->bsh', x, W1) + scale * jnp.einsum('bsd,bhd->bsh', x, m1) + b1
        h = jax.nn.gelu(h, approximate=False)
        out = jnp.einsum('bsh,oh->bso', h, W2) + scale * jnp.einsum('bsh,boh->bso', h, m2) + b2
        return out
    x = L0_attn_u
    x = x + _layernorm(_L0_attn_ref(_layernorm(x, axis=-1), L0_attn_pre_norm_w, L0_attn_in_proj_w, L0_attn_short_w, L0_attn_short_b, L0_attn_log_poles, L0_attn_residues, L0_attn_D_skip, L0_attn_out_proj_w, L0_attn_post_norm_w, L0_attn_l1_w, L0_attn_l2_w, L0_attn_l3_w), axis=-1)
    x = x + _layernorm(_L0_ffn_ref(_layernorm(x, axis=-1), L0_ffn_W1, L0_ffn_b1, L0_ffn_W2, L0_ffn_b2, L0_ffn_scale), axis=-1)
    return x

_drawn_inputs = setup_inputs


def setup_inputs(seed=0):
    import zlib

    import numpy as np

    out = dict(_drawn_inputs(seed))
    spreads = {'L0_attn_pre_norm_w': (1.0, 0.2),
     'L0_attn_post_norm_w': (1.0, 0.2),
     'L0_ffn_b1': (0.0, 0.1),
     'L0_ffn_b2': (0.0, 0.1)}
    factors = {'L0_attn_short_b': 3.536, 'L0_attn_D_skip': 33.006}
    for name, (base, spread) in spreads.items():
        noise = np.random.default_rng([zlib.crc32(name.encode()), seed]).standard_normal(out[name].shape)
        drawn = base * np.exp(spread * noise) if base else spread * noise
        out[name] = jnp.asarray(drawn.astype(out[name].dtype))
    for name, factor in factors.items():
        out[name] = (out[name] * factor).astype(out[name].dtype)
    return out
```

```python
from contextlib import ExitStack

import concourse.bass as bass
from concourse import mybir

ALU = mybir.AluOpType
ACT = mybir.ActivationFunctionType
F32 = mybir.dt.float32
F32R = mybir.dt.float32r

P = 128
B, L, D = 2, 4096, 256
TOKENS = B * L
KB = D // P
STATES = 16
TAPS = 3
ZB = 3 * D // P
CH = P
COLS = TOKENS // CH
BC = L // CH
FF, FM = 672, 112
FB = FF // FM
H = 1024
HB = H // P
EPS_LN, EPS_RMS = 1e-5, 1e-6

TA = 512
CA = TA // P
UA = TOKENS // TA
GC = P // STATES
GROUPS = D // GC
TC = 256
CC = TC // P
UC = TOKENS // TC
UCB = UC // B
LORA = 4
AHEAD = 2


def is_step(n):
    return isinstance(n, int)


def valid(n, units):
    return not is_step(n) or 0 <= n < units


def wait(eng, sem, value):
    if not is_step(value) or value > 0:
        eng.wait_ge(sem, value)


def aggregate_after(dve, vector, mark, sem, value):
    dve.wait_ge(sem, value)
    vector.memset(mark, 0.0)


def run_steps(eng, step, plan):
    for part in plan:
        if is_step(part):
            step(2 * part, 0, part)
            step(2 * part + 1, 1, part)
        else:
            with eng.Fori(*part) as k:
                step(2 * k, 0, k)
                step(2 * k + 1, 1, k)


def build(nc, x, pre_w, in_w, short_w, short_b, lp_chan, lp_group, lp_flat, res_chan, res_group,
          d_skip, out_w, post_w, l1_w, l2_w, l3_w, w1, b1, w2, b2, scale, out):
    x2_dram = nc.dram_tensor("x2_scratch", (P, KB, TOKENS), F32, kind="Internal").ap()
    taps_dram = nc.dram_tensor("taps_scratch", (D, 2 * CH), F32, kind="Internal").ap()
    lora_dram = nc.dram_tensor("lora_scratch", (4 * LORA, D), F32, kind="Internal").ap()
    half = P // 2
    with ExitStack() as whole:
        def sb(ctx, name, shape, dt=F32):
            return ctx.enter_context(nc.sbuf_tensor(name, shape, dt))

        def ps(ctx, name, shape):
            return ctx.enter_context(nc.psum_tensor(name, shape, F32))

        def sem(ctx, name):
            return ctx.enter_context(nc.semaphore(name))

        ident = sb(whole, "ident", [P, P])
        neg_half = sb(whole, "neg_half", [P, 2, CA])
        ln_scale = sb(whole, "ln_scale", [P, COLS])
        ln_mean = sb(whole, "ln_mean", [P, COLS])
        mark = sb(whole, "mark", [P, 1])
        seq = sb(whole, "seq", [P, D, COLS])
        wout = [sb(whole, f"wout_{s}", [P, KB, D], F32R) for s in "hl"]
        wl1 = [sb(whole, f"wl1_{s}", [P, KB, FF], F32R) for s in "hl"]
        wl2 = [sb(whole, f"wl2_{s}", [P, KB, FF], F32R) for s in "hl"]
        wl3 = [sb(whole, f"wl3_{s}", [FM, FB, D], F32R) for s in "hl"]

        phase_a(nc, whole, sb, ps, sem, locals())
        phase_b(nc, sb, ps, sem, locals())
        phase_c(nc, sb, ps, sem, locals())


def phase_a(nc, whole, sb, ps, sem, v):
    ident, neg_half, seq = v["ident"], v["neg_half"], v["seq"]
    ln_scale, ln_mean, mark = v["ln_scale"], v["ln_mean"], v["mark"]
    x2_dram, taps_dram = v["x2_dram"], v["taps_dram"]
    with ExitStack() as ctx:
        win = sb(ctx, "win", [P, KB, 3 * D])
        win_r = [sb(ctx, f"win_{s}", [P, KB, 3 * D], F32R) for s in "hl"]
        pre = sb(ctx, "pre", [P, KB])
        sw = sb(ctx, "sw", [P, ZB, TAPS])
        sbias = sb(ctx, "sbias", [P, ZB])
        lpc = sb(ctx, "lpc", [P, KB, STATES])
        rc = sb(ctx, "rc", [P, KB, STATES])
        dsk = sb(ctx, "dsk", [P, KB])
        back = sb(ctx, "back", [P, CH])
        pole_pow = sb(ctx, "pole_pow", [P, 2, CH])
        taps = sb(ctx, "taps", [P, KB, 2 * CH])
        zero_halo = sb(ctx, "zero_halo", [P, ZB, TAPS - 1])
        xa = sb(ctx, "xa", [P, 2, CA, D])
        stats = sb(ctx, "stats", [P, CA, 6])
        mv = sb(ctx, "mv", [P, 2, CA, 2])
        st = sb(ctx, "st", [P, 2, CA])
        minus = sb(ctx, "minus", [P, 2, CA])
        zn = sb(ctx, "zn", [P, CA, D])
        zt = [sb(ctx, f"zt_{s}", [P, 2, KB, TA], F32R) for s in "hl"]
        zbuf = sb(ctx, "zbuf", [P, 2, ZB, TA + TAPS - 1])
        conv = sb(ctx, "conv", [P, ZB, TA])
        xv = sb(ctx, "xv", [P, KB, TA])
        ps_t = ps(ctx, "ps_t", [P, KB, TA])
        ps_z = ps(ctx, "ps_z", [P, 3, TA])
        ps_x = ps(ctx, "ps_x", [P, CA, D])

        win_in = sem(ctx, "win_in")
        small_in = sem(ctx, "small_in")
        x_in = [sem(ctx, f"x_in{i}") for i in range(2)]
        x2_out = sem(ctx, "x2_out")
        taps_out = sem(ctx, "taps_out")
        consts = sem(ctx, "consts")
        tap_exp = sem(ctx, "tap_exp")
        tap_sum = sem(ctx, "tap_sum")
        taps_ready = sem(ctx, "taps_ready")
        win_fold = sem(ctx, "win_fold")
        stats_done = sem(ctx, "stats_done")
        args_done = sem(ctx, "args_done")
        st_done = sem(ctx, "st_done")
        zn_done = sem(ctx, "zn_done")
        zt_done = sem(ctx, "zt_done")
        zh_done = sem(ctx, "zh_done")
        zl_done = sem(ctx, "zl_done")
        z_mm = sem(ctx, "z_mm")
        halo_done = sem(ctx, "halo_done")
        z_copy = sem(ctx, "z_copy")
        conv_done = sem(ctx, "conv_done")
        xv_done = sem(ctx, "xv_done")
        xt_done = sem(ctx, "xt_done")
        xs_done = sem(ctx, "xs_done")
        ST = 4
        order = (2, 4, 3, 5, 0, 1)
        plan = (0, 1, (2, 4), 4, (5, 7), 7, 8)
        x_rows = v["x"].rearrange("(n c p) d -> n p c d", c=CA, p=P)

        block = ctx.enter_context(nc.Block())

        @block.sync
        def _(sp):
            sp.dma_start(xa[:, 0], x_rows[0]).then_inc(x_in[0], 16)
            for dst, src in ((lpc, v["lp_chan"]), (rc, v["res_chan"]), (dsk, v["d_skip"]),
                             (pre, v["pre_w"]), (sw, v["short_w"]), (sbias, v["short_b"])):
                sp.dma_start(dst[:], src).then_inc(small_in, 16)
            sp.dma_start(win[:], v["in_w"].rearrange("(k p) o -> p k o", p=P)).then_inc(win_in, 16)
            wait(sp, taps_ready, KB + 1)
            sp.dma_start(taps_dram.rearrange("(k p) t -> p k t", p=P), taps[:]).then_inc(taps_out, 16)

            def step(n, par, k):
                if valid(n + 1, UA):
                    wait(sp, zn_done, CA * n)
                    sp.dma_start(xa[:, 1 - par], x_rows[bass.ds(n + 1, 1)].rearrange("n p c d -> (n p) c d")
                                 ).then_inc(x_in[1 - par], 16)
                if valid(n - 1, UA):
                    wait(sp, conv_done, 2 * ZB * n)
                    sp.dma_start(x2_dram[:, :, bass.ds((n - 1) * TA, TA)], conv[:, 0:KB, :]
                                 ).then_inc(x2_out, 16)

            run_steps(sp, step, plan)
            sp.wait_ge(x2_out, 16 * UA)
            sp.wait_ge(taps_out, 16)

        @block.gpsimd
        def _(pool):
            nc.gpsimd.memset(ident[:], 1.0).then_inc(consts, 1)
            nc.gpsimd.memset(neg_half[:], -0.5).then_inc(consts, 1)
            nc.gpsimd.memset(zero_halo[:], 0.0).then_inc(consts, 1)
            nc.gpsimd.iota(back[:], [[-1, CH]], base=CH - 1, channel_multiplier=0,
                           allow_small_or_imprecise_dtypes=True).then_inc(consts, 1)
            pool.wait_ge(consts, 4)
            nc.gpsimd.affine_select(ident[:], ident[:], [[-1, P]], ALU.is_equal, 0.0, base=0,
                                    channel_multiplier=1).then_inc(consts, 1)

            def row_scales(n, par):
                pool.wait_ge(args_done, 3 * (n + 1))
                nc.gpsimd.tensor_tensor(st[:], st[:], neg_half[:], ALU.pow).then_inc(st_done, 1)
                pool.wait_ge(st_done, ST * n + 1)
                wait(pool, zt_done, n)
                nc.gpsimd.tensor_tensor(minus[:, 1], minus[:, 0], st[:, 1], ALU.mult
                                        ).then_inc(st_done, 1)
                pool.wait_ge(st_done, ST * n + 2)
                nc.gpsimd.tensor_copy(ln_scale[:, bass.ds(n * CA, CA)], st[:, 0]).then_inc(st_done, 1)
                nc.gpsimd.tensor_copy(ln_mean[:, bass.ds(n * CA, CA)], mv[:, par, :, 0]).then_inc(st_done, 1)
                for c in range(CA):
                    nc.gpsimd.tensor_scalar(zn[:, c], xa[:, par, c], st[:, 1, c:c + 1],
                                            minus[:, 1, c:c + 1], ALU.mult, ALU.add
                                            ).then_inc(zn_done, 1)

            row_scales(0, 0)

            def step(n, par, k):
                if valid(n + 1, UA):
                    row_scales(n + 1, 1 - par)
                if valid(n - 1, UA):
                    wait(pool, xt_done, n - 1)
                    for j in range(KB):
                        pool.wait_ge(conv_done, 2 * ZB * (n - 1) + 4 * (j + 1))
                        nc.gpsimd.tensor_tensor(xv[:, j], conv[:, 2 + j], conv[:, 4 + j], ALU.mult
                                                ).then_inc(xv_done, 1)

            run_steps(pool, step, plan)

        @block.scalar
        def _(act):
            act.wait_ge(small_in, 16 * 6)
            act.wait_ge(consts, 5)
            for i in range(KB * STATES):
                wait(act, tap_sum, i - 1)
                nc.scalar.activation(pole_pow[:, i % 2], back[:], ACT.Exp,
                                     scale=lpc[:, i // STATES, i % STATES:i % STATES + 1]
                                     ).then_inc(tap_exp, 1)

            def step(n, par, k):
                if valid(n - 2, UA):
                    act.wait_ge(xt_done, n - 1)
                    nc.scalar.activation(seq[:, :, bass.ds((n - 2) * CA, CA)].rearrange("p h c -> p c h"),
                                         ps_x[:], ACT.Copy).then_inc(xs_done, 1)
                if valid(n, UA):
                    act.wait_ge(zt_done, n + 1)
                    wait(act, z_mm, ZB * (n - 1))
                    nc.scalar.activation(zt[0][:, par], ps_t[:], ACT.Copy).then_inc(zh_done, 1)
                u = n - 1
                if valid(u, UA):
                    first = is_step(n) and u % (UA // B) == 0
                    wait(act, conv_done, 2 * ZB * (u - 1))
                    halo = zero_halo[:] if first else zbuf[:, par, :, TA:]
                    wait(act, z_copy, 2 * ZB * u)
                    nc.scalar.activation(zbuf[:, 1 - par, :, 0:TAPS - 1], halo, ACT.Copy
                                         ).then_inc(halo_done, 1)
                for i in range(ZB):
                    if valid(u, UA):
                        m = order[i]
                        act.wait_ge(z_mm, ZB * u + i + 1)
                        nc.scalar.activation(zbuf[:, 1 - par, m, TAPS - 1:], ps_z[:, i % 3], ACT.Copy
                                             ).then_inc(z_copy, 1)
                        if i == 0:
                            wait(act, xv_done, KB * u)
                        if i == 4:
                            wait(act, x2_out, 16 * u)
                        nc.scalar.activation(conv[:, m], ps_z[:, i % 3], ACT.Identity,
                                             scale=sw[:, m, 2:3], bias=sbias[:, m:m + 1]
                                             ).then_inc(z_copy, 1)

            run_steps(act, step, plan)

        @block.vector
        def _(dve):
            nc.vector.memset(taps[:], 0.0).then_inc(taps_ready, 1)

            def row_stats(n, par, k):
                dve.wait_ge(x_in[par], 16 * (k + 1))
                wait(dve, st_done, ST * (n - 1))
                for c in range(CA):
                    nc.vector.bn_stats(stats[:, c], xa[:, par, c]).then_inc(stats_done, 1)
                aggregate_after(dve, nc.vector, mark[:], stats_done, 2 * CA * n + CA)
                for c in range(CA):
                    nc.vector.bn_aggr(mv[:, par, c], stats[:, c]).then_inc(stats_done, 1)
                dve.wait_ge(stats_done, 2 * CA * n + 2 * CA)
                wait(dve, st_done, ST * n)
                wait(dve, zn_done, CA * n)
                nc.vector.tensor_scalar(st[:, 0], mv[:, par, :, 1], EPS_LN, None, ALU.add
                                        ).then_inc(args_done, 1)
                nc.vector.tensor_scalar(st[:, 1], mv[:, par, :, 1], 1.0 + EPS_RMS, EPS_RMS * EPS_LN,
                                        ALU.mult, ALU.add).then_inc(args_done, 1)
                nc.vector.tensor_scalar(minus[:, 0], mv[:, par, :, 0], -1.0, None, ALU.mult
                                        ).then_inc(args_done, 1)

            row_stats(0, 0, 0)
            dve.wait_ge(small_in, 16 * 6)
            dve.wait_ge(win_in, 16)
            for k in range(KB):
                nc.vector.tensor_scalar(win[:, k], win[:, k], pre[:, k:k + 1], None, ALU.mult
                                        ).then_inc(win_fold, 1)
            dve.wait_ge(win_fold, KB)
            nc.vector.tensor_copy(win_r[0][:], win[:]).then_inc(win_fold, 1)
            dve.wait_ge(win_fold, KB + 1)
            nc.vector.tensor_tensor(win_r[1][:], win[:], win_r[0][:].bitcast(F32), ALU.subtract
                                    ).then_inc(win_fold, 1)

            dve.wait_ge(taps_ready, 1)
            for i in range(KB * STATES):
                kb, s = divmod(i, STATES)
                dve.wait_ge(tap_exp, i + 1)
                wait(dve, tap_sum, i)
                nc.vector.scalar_tensor_tensor(taps[:, kb, 0:CH], pole_pow[:, i % 2], rc[:, kb, s:s + 1],
                                               taps[:, kb, 0:CH], ALU.mult, ALU.add).then_inc(tap_sum, 1)
            dve.wait_ge(tap_sum, KB * STATES)
            for k in range(KB):
                nc.vector.tensor_tensor(taps[:, k, CH - 1:CH], taps[:, k, CH - 1:CH], dsk[:, k:k + 1],
                                        ALU.add).then_inc(taps_ready, 1)

            def step(n, par, k):
                if valid(n, UA):
                    dve.wait_ge(zh_done, n + 1)
                    nc.vector.tensor_tensor(zt[1][:, par], ps_t[:], zt[0][:, par].bitcast(F32),
                                            ALU.subtract).then_inc(zl_done, 1)
                u = n - 1
                if valid(n + 1, UA):
                    row_stats(n + 1, 1 - par, k + par)
                if valid(u, UA):
                    dve.wait_ge(halo_done, n)
                    for i in range(0, ZB, 2):
                        for tap, (j, m) in ((t, (j, order[j])) for t in (1, 0) for j in (i, i + 1)):
                            if tap:
                                dve.wait_ge(z_copy, 2 * ZB * u + 2 * j + 2)
                            else:
                                dve.wait_ge(conv_done, 2 * ZB * u + i + j + 1)
                            nc.vector.scalar_tensor_tensor(conv[:, m], zbuf[:, 1 - par, m, tap:TA + tap],
                                                           sw[:, m, tap:tap + 1], conv[:, m],
                                                           ALU.mult, ALU.add).then_inc(conv_done, 1)

            run_steps(dve, step, plan)

        @block.tensor
        def _(pe):
            pe.wait_ge(consts, 5)

            def step(n, par, k):
                if valid(n, UA):
                    pe.wait_ge(zn_done, CA * (n + 1))
                    wait(pe, zl_done, n)
                    for b in range(KB):
                        for c in range(CA):
                            mm = nc.tensor.transpose(ps_t[:, b, c * P:(c + 1) * P],
                                                     zn[:, c, b * P:(b + 1) * P], ident[:])
                    mm.then_inc(zt_done, 1)
                if valid(n - 2, UA):
                    pe.wait_ge(xv_done, KB * (n - 1))
                    wait(pe, xs_done, n - 2)
                    for c in range(CA):
                        for b in range(KB):
                            mm = nc.tensor.transpose(ps_x[:, c, b * P:(b + 1) * P],
                                                     xv[:, b, c * P:(c + 1) * P], ident[:])
                    mm.then_inc(xt_done, 1)
                u = n - 1
                if valid(u, UA):
                    if is_step(n) and u == 0:
                        pe.wait_ge(win_fold, KB + 2)
                    pe.wait_ge(zl_done, u + 1)
                    for i in range(ZB):
                        m = order[i]
                        wait(pe, z_copy, 2 * (ZB * u + i - 2))
                        passes = [(a, b, kk) for a, b in ((0, 0), (0, 1), (1, 0)) for kk in range(KB)]
                        for j, (a, b, kk) in enumerate(passes):
                            mm = nc.tensor.matmul(ps_z[:, i % 3], win_r[a][:, kk, m * P:(m + 1) * P],
                                                  zt[b][:, 1 - par, kk], start=(j == 0),
                                                  stop=(j == len(passes) - 1))
                        mm.then_inc(z_mm, 1)

            run_steps(pe, step, plan)


def phase_b(nc, sb, ps, sem, v):
    seq, taps_dram = v["seq"], v["taps_dram"]
    with ExitStack() as ctx:
        lpb = sb(ctx, "lpb", [P, D * STATES])
        lpg = sb(ctx, "lpg", [P, GROUPS])
        rg = sb(ctx, "rg", [P, GROUPS])
        pole_chunk = sb(ctx, "pole_chunk", [P, GROUPS])
        to_end = sb(ctx, "to_end", [P, 1])
        ahead = sb(ctx, "ahead", [P, CH])
        own = sb(ctx, "own", [P, 2 * GC, BC])
        later = sb(ctx, "later", [P, 2 * GC, BC])
        collect = sb(ctx, "collect", [P, 2, P])
        spread = sb(ctx, "spread", [P, 2, CH])
        decay = sb(ctx, "decay", [P, 2, 2 * GC * BC])
        inflow = sb(ctx, "inflow", [P, 2, 2 * GC, BC])
        state = sb(ctx, "state", [P, 2, 2 * GC * BC])
        toep = sb(ctx, "toep", [P, 2, GC, CH])
        raw = sb(ctx, "raw", [P, KB, FF])
        post = sb(ctx, "post", [P, KB])
        ps_s = [ps(ctx, f"ps_s{i}", [P, 2 * GC, BC]) for i in range(2)]
        ps_y = [ps(ctx, f"ps_y{i}", [P, 2 * GC * BC]) for i in range(2)]

        poles_in = sem(ctx, "poles_in")
        toep_in = [sem(ctx, f"toep_in{i}") for i in range(2)]
        raw_in = sem(ctx, "raw_in")
        split = sem(ctx, "split")
        bconst = sem(ctx, "bconst")
        pole_done = sem(ctx, "pole_done")
        collect_done = sem(ctx, "collect_done")
        spread_done = sem(ctx, "spread_done")
        decay_done = sem(ctx, "decay_done")
        s_mm = sem(ctx, "s_mm")
        toep_mm = sem(ctx, "toep_mm")
        y_mm = sem(ctx, "y_mm")
        inflow_done = sem(ctx, "inflow_done")
        scan_done = sem(ctx, "scan_done")
        y_done = sem(ctx, "y_done")
        plan = (0, (1, GROUPS // 2 - 1), GROUPS // 2 - 1)
        folded = ((v["l1_w"], v["wl1"]), (v["l2_w"], v["wl2"]))

        block = ctx.enter_context(nc.Block())

        @block.sync
        def _(sp):
            sp.dma_start(lpg[:], v["lp_group"]).then_inc(poles_in, 16)
            sp.dma_start(rg[:], v["res_group"]).then_inc(poles_in, 16)
            lp_flat = v["lp_flat"]
            sp.dma_start(lpb[:], bass.AP(lp_flat.tensor, 0, [[0, P], [1, D * STATES]])
                         ).then_inc(poles_in, 16)

            def load(g, par):
                src = bass.AP(taps_dram.tensor, 2 * CH * GC * g, [[1, P], [2 * CH, GC], [1, CH]])
                wait(sp, toep_mm, g - 1)
                sp.dma_start(toep[:, par], src).then_inc(toep_in[par], 16)

            load(0, 0)

            def step(g, par, k):
                if valid(g + 1, GROUPS):
                    load(g + 1, 1 - par)

            run_steps(sp, step, plan)

        @block.gpsimd
        def _(pool):
            nc.gpsimd.iota(to_end[:], [[0, 1]], base=CH - 1, channel_multiplier=-1,
                           allow_small_or_imprecise_dtypes=True).then_inc(bconst, 1)
            nc.gpsimd.iota(ahead[:], [[-1, CH]], base=CH, channel_multiplier=0,
                           allow_small_or_imprecise_dtypes=True).then_inc(bconst, 1)
            nc.gpsimd.memset(own[:], 1.0).then_inc(bconst, 1)
            nc.gpsimd.memset(later[:], 1.0).then_inc(bconst, 1)
            nc.gpsimd.memset(inflow[:], 0.0).then_inc(bconst, 1)
            pool.wait_ge(bconst, 5)
            nc.gpsimd.memset(later[:, :, 0:1], 0.0).then_inc(bconst, 1)
            nc.gpsimd.affine_select(own[:], own[:], [[-STATES, GC], [0, 2 * BC]], ALU.is_ge, 0.0,
                                    base=0, channel_multiplier=1).then_inc(bconst, 1)
            pool.wait_ge(bconst, 7)
            nc.gpsimd.affine_select(own[:], own[:], [[STATES, GC], [0, 2 * BC]], ALU.is_ge, 0.0,
                                    base=STATES - 1, channel_multiplier=-1).then_inc(bconst, 1)

            wout, wl3 = v["wout"], v["wl3"]
            raw_out = raw[:, :, 0:D]
            raw_l3 = raw[0:FM].rearrange("p k f -> p (k f)")
            count, loads = 0, 0
            pool.dma_start(post[:], v["post_w"]).then_inc(raw_in, 16)
            loads += 16
            pool.wait_ge(raw_in, loads)
            for src, dst in folded:
                pool.dma_start(raw[:], src.rearrange("(k p) f -> p k f", p=P)).then_inc(raw_in, 16)
                loads += 16
                pool.wait_ge(raw_in, loads)
                for kk in range(KB):
                    nc.gpsimd.tensor_scalar(raw[:, kk], raw[:, kk], post[:, kk:kk + 1], 1.0,
                                            ALU.mult, ALU.mult).then_inc(split, 1)
                count += KB
                pool.wait_ge(split, count)
                nc.gpsimd.tensor_copy(dst[0][:], raw[:]).then_inc(split, 1)
                count += 1
                pool.wait_ge(split, count)
                nc.gpsimd.tensor_tensor(dst[1][:], raw[:], dst[0][:].bitcast(F32), ALU.subtract
                                        ).then_inc(split, 1)
                count += 1
                pool.wait_ge(split, count)
            pieces = [(v["out_w"].rearrange("(k p) o -> p k o", p=P), raw_out,
                       wout[0][:], wout[1][:])]
            half_l3 = FB // 2
            for h in range(2):
                span = slice(h * half_l3, (h + 1) * half_l3)
                pieces.append((v["l3_w"].rearrange("(m p) o -> p m o", p=FM)[:, span],
                               raw_l3[:, 0:half_l3 * D].rearrange("p (m o) -> p m o", m=half_l3),
                               wl3[0][:, span], wl3[1][:, span]))
            for src, stage, high, low in pieces:
                pool.dma_start(stage, src).then_inc(raw_in, 16)
                loads += 16
                pool.wait_ge(raw_in, loads)
                nc.gpsimd.tensor_copy(high, stage).then_inc(split, 1)
                count += 1
                pool.wait_ge(split, count)
                nc.gpsimd.tensor_tensor(low, stage, high.bitcast(F32), ALU.subtract).then_inc(split, 1)
                count += 1
                pool.wait_ge(split, count)

        @block.scalar
        def _(act):
            act.wait_ge(poles_in, 48)
            act.wait_ge(bconst, 8)
            nc.scalar.activation(pole_chunk[:], lpg[:], ACT.Exp, scale=float(CH)).then_inc(pole_done, 1)
            act.wait_ge(pole_done, 1)

            def powers(g, par):
                wait(act, s_mm, g - 1)
                nc.scalar.activation(collect[:, par], lpb[:, bass.ds(g * P, P)], ACT.Exp,
                                     scale=to_end[:, 0:1]).then_inc(collect_done, 1)
                wait(act, scan_done, g - 1)
                nc.scalar.activation(decay[:, par], later[:].rearrange("p c j -> p (c j)"), ACT.Copy,
                                     scale=pole_chunk[:, bass.ds(g, 1)]).then_inc(decay_done, 1)
                wait(act, y_mm, g - 1)
                nc.scalar.activation(spread[:, par], ahead[:], ACT.Exp, scale=lpg[:, bass.ds(g, 1)]
                                     ).then_inc(spread_done, 1)

            powers(0, 0)

            def take(g, par):
                act.wait_ge(y_mm, g + 1)
                nc.scalar.activation(seq[:, bass.ds(g * GC, GC), :], ps_y[par][:], ACT.Copy
                                     ).then_inc(y_done, 1)

            def step(g, par, k):
                if valid(g + 1, GROUPS):
                    powers(g + 1, 1 - par)
                if valid(g - 1, GROUPS):
                    take(g - 1, 1 - par)

            run_steps(act, step, plan)
            take(GROUPS - 1, 1)

        @block.vector
        def _(dve):
            dve.wait_ge(poles_in, 48)
            dve.wait_ge(bconst, 8)

            def step(g, par, k):
                dve.wait_ge(s_mm, g + 1)
                wait(dve, scan_done, g - 1)
                nc.vector.scalar_tensor_tensor(inflow[:, par, :, 1:BC], ps_s[par][:, :, 0:BC - 1],
                                               rg[:, bass.ds(g, 1)], own[:, :, 0:BC - 1],
                                               ALU.mult, ALU.mult).then_inc(inflow_done, 1)
                dve.wait_ge(inflow_done, g + 1)
                dve.wait_ge(decay_done, g + 1)
                wait(dve, y_mm, g - 1)
                nc.vector.tensor_tensor_scan(state[:, par], decay[:, par],
                                             inflow[:, par].rearrange("p c j -> p (c j)"), 0.0,
                                             ALU.mult, ALU.add).then_inc(scan_done, 1)

            run_steps(dve, step, plan)

        @block.tensor
        def _(pe):
            def states_of(g, par):
                pe.wait_ge(collect_done, g + 1)
                wait(pe, inflow_done, g - 1)
                nc.tensor.matmul(ps_s[par][:].rearrange("p c j -> p (c j)"), collect[:, par],
                                 seq[:, bass.ds(g * GC, GC), :].rearrange("p h c -> p (h c)"),
                                 start=True, stop=True).then_inc(s_mm, 1)

            states_of(0, 0)

            def step(g, par, k):
                if valid(g + 1, GROUPS):
                    states_of(g + 1, 1 - par)
                pe.wait_ge(toep_in[par], 16 * (k + 1))
                wait(pe, y_done, g - 1)
                for c in range(GC):
                    mm = nc.tensor.matmul(ps_y[par][:, c * COLS:(c + 1) * COLS], toep[:, par, c],
                                          seq[:, bass.ds(g * GC + c, 1), :].rearrange("p h c -> p (h c)"),
                                          start=(c == 0), stop=False, skip_group_check=True)
                mm.then_inc(toep_mm, 1)
                pe.wait_ge(spread_done, g + 1)
                pe.wait_ge(scan_done, g + 1)
                nc.tensor.matmul(ps_y[par][:], spread[:, par], state[:, par], start=False, stop=True,
                                 skip_group_check=True).then_inc(y_mm, 1)

            run_steps(pe, step, plan)


def phase_c(nc, sb, ps, sem, v):
    ident, neg_half, seq = v["ident"], v["neg_half"], v["seq"]
    ln_scale, ln_mean, mark = v["ln_scale"], v["ln_mean"], v["mark"]
    wout, wl1, wl2, wl3 = v["wout"], v["wl1"], v["wl2"], v["wl3"]
    x2_dram, lora_dram = v["x2_dram"], v["lora_dram"]
    last = UC + AHEAD
    plan = (0, 1, (2, UCB // 2), UCB // 2, (UCB // 2 + 1, UC // 2 - 1), UC // 2 - 1, UC // 2)
    PASSES = ((0, 0), (0, 1), (1, 0))
    T3_AT = FB // 2
    with ExitStack() as ctx:
        we1 = [sb(ctx, f"we1_{s}", [P, KB, H], F32R) for s in "hl"]
        we2 = [sb(ctx, f"we2_{s}", [P, HB, D], F32R) for s in "hl"]
        b1s = sb(ctx, "b1s", [P, HB])
        b2s = sb(ctx, "b2s", [P, CC, D])
        scale_s = sb(ctx, "scale_s", [P, 1])
        xs = sb(ctx, "xs", [P, 2, CC, D])
        x2s = sb(ctx, "x2s", [P, KB, TC])
        ys = sb(ctx, "ys", [P, CC, D])
        yf = sb(ctx, "yf", [P, KB, TC])
        yt = [sb(ctx, f"yt_{s}", [P, KB, TC], F32R) for s in "hl"]
        yrow = sb(ctx, "yrow", [P, 2, CC, D])
        square = sb(ctx, "square", [P, D])
        rows = sb(ctx, "rows", [P, CC, D])
        zt = [sb(ctx, f"mt_{s}", [P, KB, TC], F32R) for s in "hl"]
        xt = [sb(ctx, f"xt_{s}", [P, KB, TC], F32R) for s in "hl"]
        gate = sb(ctx, "gate", [FM, 2, TC])
        prod = sb(ctx, "prod", [FM, 2, TC])
        pt = [sb(ctx, f"pt_{s}", [FM, FB, TC], F32R) for s in "hl"]
        x1 = sb(ctx, "x1", [P, 2, CC, D])
        hid = sb(ctx, "hid", [P, 2, TC])
        with ExitStack() as weights_made:
            even = sb(weights_made, "even", [P, 2 * LORA, D])
            base = sb(weights_made, "base", [P, 2, H])
        ht = [sb(ctx, f"ht_{s}", [P, HB, TC], F32R) for s in "hl"]
        frow = sb(ctx, "frow", [P, CC, D])
        orow = sb(ctx, "orow", [P, CC, D])
        odd = sb(ctx, "odd", [P, KB, 2 * LORA])
        bn = sb(ctx, "bn", [P, 3, CC, 6])
        mva = sb(ctx, "mva", [P, CC, 2])
        mvx = sb(ctx, "mvx", [P, CC, 2])
        mvf = sb(ctx, "mvf", [P, CC, 2])
        sc = sb(ctx, "sc", [P, 4, CC])
        sums = sb(ctx, "sums", [P, CC])
        ps_y = ps(ctx, "ps_yt", [P, KB, TC])
        ps_t = ps(ctx, "ps_rt", [P, KB, TC])
        ps_o = ps(ctx, "ps_o", [P, CC, D])
        ps_m = ps(ctx, "ps_m", [P, CC, D])
        ps_w = ps(ctx, "ps_w", [P, CC, D])
        ring = [ps(ctx, f"ps_ring{i}", [P, 2, TC]) for i in range(3)]

        x_in = [sem(ctx, f"cx_in{i}") for i in range(2)]
        base_in = [sem(ctx, f"base_in{i}") for i in range(KB)]
        names = """x2_in rows_out consts_in y_copied yt_mm yf_done yh_done yl_done o_mm yrow_u yrow_done
                   squared rms_arg rms_done zm_done zt_mm zh_done zl_done ml_mm gate_done prod_done
                   ph_done pl_done m_mm a_done a_stat a_var a_scale x1_hat x1_done x_stat x_var x_scale
                   xn_done xt_mm xh_done xl_done h_mm hid_done hh_done hl_even hl_odd w2_mm f_done
                   f_stat f_var f_scale f_norm out_done lora_out even_in odd_done weight_add
                   weight_high weight_low1 weight_low2"""
        S = {n: sem(ctx, "c_" + n) for n in names.split()}

        x_rows = v["x"].rearrange("(n c p) d -> n p c d", c=CC, p=P)
        out_rows = v["out"].rearrange("(n c p) d -> n p c d", c=CC, p=P)
        w1_pieces = [v["w1"].rearrange("(k p) h -> k p h", p=P)[k] for k in range(KB)]
        w2_pieces = [v["w2"].rearrange("(r j p) o -> j p r o", j=KB, p=P)[j] for j in range(KB)]
        PIECES = 2 * KB

        def row_unit(t, n):
            return t[bass.ds(n, 1)].rearrange("n p c d -> (n p) c d")

        def piece(i):
            if i < KB:
                return base[:, i], we1[0][:, i], we1[1][:, i]
            view = [w[:].rearrange("p (r j) o -> p j r o", j=KB)[:, i - KB] for w in we2]
            return base[:, i - KB].rearrange("p (r o) -> p r o", o=D), view[0], view[1]

        def makes_weights(n):
            return is_step(n) and 0 <= n - 1 < UC and (n - 1) % UCB == 0

        block = ctx.enter_context(nc.Block())

        @block.sync
        def _(sp):
            sp.dma_start(x2s[:], x2_dram[:, :, 0:TC]).then_inc(S["x2_in"], 16)
            sp.dma_start(xs[:, 0], x_rows[0]).then_inc(x_in[0], 16)
            sp.dma_start(b1s[:], v["b1"]).then_inc(S["consts_in"], 16)
            for c in range(CC):
                sp.dma_start(b2s[:, c], bass.AP(v["b2"].tensor, 0, [[0, P], [1, D]])
                             ).then_inc(S["consts_in"], 16)
            sp.dma_start(scale_s[:], bass.AP(v["scale"].tensor, 0, [[0, P], [1, 1]])
                         ).then_inc(S["consts_in"], 16)

            def load_piece(made, i):
                if i >= KB:
                    sp.wait_ge(S["weight_low1"], KB * made + i - KB + 1)
                if i < KB:
                    sp.dma_start(base[:, i], w1_pieces[i]).then_inc(base_in[i], 16)
                else:
                    sp.dma_start(base[:, i - KB].rearrange("p (r o) -> p r o", o=D), w2_pieces[i - KB]
                                 ).then_inc(base_in[i - KB], 16)

            def step(n, par, k):
                if valid(n + 1, UC):
                    sp.wait_ge(S["yf_done"], n + 1)
                    sp.dma_start(x2s[:], x2_dram[:, :, bass.ds((n + 1) * TC, TC)]).then_inc(S["x2_in"], 16)
                    wait(sp, S["x1_done"], n)
                    sp.dma_start(xs[:, 1 - par], row_unit(x_rows, n + 1)).then_inc(x_in[1 - par], 16)
                if makes_weights(n):
                    made = (n - 1) // UCB
                    wait(sp, S["w2_mm"], n - 1)
                    load_piece(made, 0)
                    load_piece(made, 1)
                    sp.wait_ge(S["xn_done"], CC * n)
                    sp.dma_start(lora_dram, rows[1:1 + 4 * LORA, 0, :]).then_inc(S["lora_out"], 16)
                    sp.wait_ge(S["lora_out"], 16 * (made + 1))
                    sp.dma_start(even[:], bass.AP(lora_dram.tensor, 0, [[0, P], [2 * D, 2 * LORA], [1, D]])
                                 ).then_inc(S["even_in"], 16)
                    load_piece(made, 2)
                    load_piece(made, 3)
                if valid(n - 2, UC):
                    sp.wait_ge(S["out_done"], n - 1)
                    sp.dma_start(row_unit(out_rows, n - 2), orow[:]).then_inc(S["rows_out"], 16)

            run_steps(sp, step, plan)
            sp.wait_ge(S["rows_out"], 16 * UC)

        @block.gpsimd
        def _(pool):
            def copy_y(n):
                wait(pool, S["yt_mm"], n)
                nc.gpsimd.tensor_copy(ys[:], seq[:, :, bass.ds(n * CC, CC)].rearrange("p h c -> p c h")
                                      ).then_inc(S["y_copied"], 1)

            def inverse_root(var, to, done, n):
                pool.wait_ge(S[var], n + 1)
                nc.gpsimd.tensor_tensor(sc[:, to], sc[:, to], neg_half[:, 0, 0:CC], ALU.pow
                                        ).then_inc(S[done], 1)

            copy_y(0)

            def step(n, par, k):
                if valid(n - 1, UC):
                    inverse_root("a_var", 0, "a_scale", n - 1)
                if valid(n, UC):
                    inverse_root("rms_arg", 3, "rms_done", n)
                if valid(n - 1, UC):
                    inverse_root("x_var", 1, "x_scale", n - 1)
                if valid(n + 1, UC):
                    copy_y(n + 1)
                if valid(n - 2, UC):
                    inverse_root("f_var", 2, "f_scale", n - 2)
                    pool.wait_ge(S["f_norm"], CC * (n - 1))
                    wait(pool, S["rows_out"], 16 * (n - 2))
                    nc.gpsimd.tensor_tensor(orow[:], frow[:], x1[:, par], ALU.add
                                            ).then_inc(S["out_done"], 1)
                if makes_weights(n):
                    made = (n - 1) // UCB
                    pool.wait_ge(S["weight_high"], PIECES * made + PIECES)
                    src, high, low = piece(PIECES - 1)
                    nc.gpsimd.tensor_tensor(low, src, high.bitcast(F32), ALU.subtract
                                            ).then_inc(S["weight_low2"], 1)
                    pool.wait_ge(S["weight_low2"], KB * (made + 1))
                if valid(n - 1, UC):
                    for m in range(0, HB, 2):
                        pool.wait_ge(S["hh_done"], HB * (n - 1) + m + 1)
                        nc.gpsimd.tensor_tensor(ht[1][:, m], hid[:, m % 2], ht[0][:, m].bitcast(F32),
                                                ALU.subtract).then_inc(S["hl_even"], 1)

            run_steps(pool, step, plan)

        @block.scalar
        def _(act):
            act.wait_ge(S["consts_in"], 16 * (CC + 2))

            def step(n, par, k):
                if valid(n, UC):
                    act.wait_ge(S["yrow_done"], n + 1)
                    wait(act, S["rms_arg"], n)
                    for c in range(CC):
                        if c > 0:
                            act.wait_ge(S["squared"], CC * n + c)
                        nc.scalar.activation(square[:], yrow[:, par, c], ACT.Square,
                                             accum_out=sums[:, c:c + 1]).then_inc(S["squared"], 1)
                    act.wait_ge(S["rms_done"], n + 1)
                    wait(act, S["xt_mm"], n - 1)
                    for c in range(CC):
                        nc.scalar.activation(rows[:, c], yrow[:, par, c], ACT.Copy,
                                             scale=sc[:, 3, c:c + 1]).then_inc(S["zm_done"], 1)
                    act.wait_ge(S["zt_mm"], n + 1)
                    wait(act, S["ml_mm"], FB * n)
                    nc.scalar.activation(zt[0][:], ps_t[:], ACT.Copy).then_inc(S["zh_done"], 1)

                def mlp_gate(m):
                    act.wait_ge(S["ml_mm"], FB * n + m + 1)
                    wait(act, S["prod_done"], FB * n + m - 1)
                    nc.scalar.activation(gate[:, m % 2], ring[m % 3][0:FM, 0], ACT.Gelu_apprx_tanh
                                         ).then_inc(S["gate_done"], 1)

                if valid(n, UC):
                    for m in range(T3_AT):
                        mlp_gate(m)
                if valid(n - 1, UC):
                    act.wait_ge(S["xt_mm"], n)
                    wait(act, S["h_mm"], HB * (n - 1))
                    nc.scalar.activation(xt[0][:], ps_t[:], ACT.Copy).then_inc(S["xh_done"], 1)
                if valid(n, UC):
                    for m in range(T3_AT, FB):
                        mlp_gate(m)
                if makes_weights(n):
                    made = (n - 1) // UCB
                    wait(act, S["h_mm"], HB * (n - 1))
                    wait(act, S["w2_mm"], n - 1)
                    for i in range(PIECES):
                        act.wait_ge(S["weight_add"], 2 * LORA * made * KB + LORA * (i + 1))
                        src, high, low = piece(i)
                        nc.scalar.activation(high, src, ACT.Copy).then_inc(S["weight_high"], 1)
                if valid(n - 1, UC):
                    wait(act, S["w2_mm"], n - 1)
                    for m in range(HB):
                        b = HB * (n - 1) + m
                        act.wait_ge(S["h_mm"], b + 1)
                        if m % 2:
                            wait(act, S["hl_odd"], (b - 1) // 2 if is_step(n) else HB // 2 * (n - 1) + m // 2)
                        else:
                            wait(act, S["hl_even"], b // 2 if is_step(n) else HB // 2 * (n - 1) + m // 2)
                        nc.scalar.activation(hid[:, m % 2], ring[m % 3][:, 0], ACT.Gelu,
                                             bias=b1s[:, m:m + 1]).then_inc(S["hid_done"], 1)

            run_steps(act, step, plan)

        @block.vector
        def _(dve):
            dve.wait_ge(S["consts_in"], 16 * (CC + 2))

            def stats_of(src, kind, mv, stat, n):
                for c in range(CC):
                    nc.vector.bn_stats(bn[:, kind, c], src[:, c]).then_inc(S[stat], 1)
                aggregate_after(dve, nc.vector, mark[:], S[stat], 2 * CC * n + CC)
                for c in range(CC):
                    nc.vector.bn_aggr(mv[:, c], bn[:, kind, c]).then_inc(S[stat], 1)

            def split_low(low, src, high, done):
                nc.vector.tensor_tensor(low, src, high.bitcast(F32), ALU.subtract).then_inc(S[done], 1)

            def add_eps(kind, mv, stat, var, n):
                dve.wait_ge(S[stat], 2 * CC * (n + 1))
                nc.vector.tensor_scalar(sc[:, kind], mv[:, :, 1], EPS_LN, None, ALU.add
                                        ).then_inc(S[var], 1)

            def step(n, par, k):
                old = 1 - par
                u = n - 1
                if valid(n, UC):
                    dve.wait_ge(S["yt_mm"], n + 1)
                    dve.wait_ge(S["x2_in"], 16 * (n + 1))
                    wait(dve, S["yl_done"], n)
                    back = ps_y[:].rearrange("p b (c t) -> p (b c) t", t=CH)[:, :, ::-1]
                    nc.vector.tensor_tensor(yf[:].rearrange("p b (c t) -> p (b c) t", t=CH), back,
                                            x2s[:].rearrange("p b (c t) -> p (b c) t", t=CH), ALU.mult
                                            ).then_inc(S["yf_done"], 1)
                    dve.wait_ge(S["yf_done"], n + 1)
                    wait(dve, S["o_mm"], n)
                    nc.vector.tensor_copy(yt[0][:], yf[:]).then_inc(S["yh_done"], 1)
                    dve.wait_ge(S["yh_done"], n + 1)
                    split_low(yt[1][:], yf[:], yt[0][:], "yl_done")
                if valid(n, UC):
                    dve.wait_ge(x_in[par], 16 * (k + 1))
                    wait(dve, S["x1_hat"], CC * (n - 1))
                    for c in range(CC):
                        nc.vector.tensor_scalar(yrow[:, par, c], xs[:, par, c],
                                                ln_mean[:, bass.ds(n * CC + c, 1)],
                                                ln_scale[:, bass.ds(n * CC + c, 1)],
                                                ALU.subtract, ALU.mult).then_inc(S["yrow_u"], 1)
                if valid(u, UC):
                    dve.wait_ge(S["m_mm"], u + 1)
                    wait(dve, S["zm_done"], CC * (u + 1))
                    nc.vector.tensor_tensor(yrow[:, old], ps_m[:], yrow[:, old], ALU.add
                                            ).then_inc(S["a_done"], 1)
                if valid(n, UC):
                    dve.wait_ge(S["yrow_u"], CC * (n + 1))
                    dve.wait_ge(S["o_mm"], n + 1)
                    nc.vector.tensor_tensor(yrow[:, par], ps_o[:], yrow[:, par], ALU.add
                                            ).then_inc(S["yrow_done"], 1)
                if valid(u, UC):
                    dve.wait_ge(S["a_done"], u + 1)
                    wait(dve, S["x1_hat"], CC * u)
                    stats_of(yrow[:, old], 0, mva, "a_stat", u)
                    add_eps(0, mva, "a_stat", "a_var", u)
                if valid(n, UC):
                    dve.wait_ge(S["squared"], CC * (n + 1))
                    wait(dve, S["zm_done"], CC * n)
                    nc.vector.tensor_scalar(sc[:, 3], sums[:], 1.0 / D, EPS_RMS, ALU.mult, ALU.add
                                            ).then_inc(S["rms_arg"], 1)
                if valid(u, UC):
                    dve.wait_ge(S["a_scale"], u + 1)
                    wait(dve, S["out_done"], u - 1)
                    for c in range(CC):
                        nc.vector.tensor_scalar(x1[:, old, c], yrow[:, old, c], mva[:, c, 0:1],
                                                sc[:, 0, c:c + 1], ALU.subtract, ALU.mult
                                                ).then_inc(S["x1_hat"], 1)
                    dve.wait_ge(S["x1_hat"], CC * (u + 1))
                    nc.vector.tensor_tensor(x1[:, old], x1[:, old], xs[:, old], ALU.add
                                            ).then_inc(S["x1_done"], 1)
                if valid(u, UC):
                    dve.wait_ge(S["x1_done"], u + 1)
                    wait(dve, S["xn_done"], CC * u)
                    stats_of(x1[:, old], 1, mvx, "x_stat", u)
                    add_eps(1, mvx, "x_stat", "x_var", u)
                if valid(n, UC):
                    dve.wait_ge(S["zh_done"], n + 1)
                    split_low(zt[1][:], ps_t[:], zt[0][:], "zl_done")
                if valid(u, UC):
                    dve.wait_ge(S["x_scale"], u + 1)
                    if valid(n, UC):
                        dve.wait_ge(S["zt_mm"], n + 1)
                    else:
                        wait(dve, S["xt_mm"], u)
                    for c in range(CC):
                        nc.vector.tensor_scalar(rows[:, c], x1[:, old, c], mvx[:, c, 0:1],
                                                sc[:, 1, c:c + 1], ALU.subtract, ALU.mult
                                                ).then_inc(S["xn_done"], 1)
                if valid(n - 2, UC):
                    w = n - 2
                    dve.wait_ge(S["w2_mm"], w + 1)
                    wait(dve, S["out_done"], w)
                    nc.vector.tensor_tensor(frow[:], ps_w[:], b2s[:], ALU.add).then_inc(S["f_done"], 1)
                    dve.wait_ge(S["f_done"], w + 1)
                    wait(dve, S["f_norm"], CC * w)
                    stats_of(frow[:], 2, mvf, "f_stat", w)
                    add_eps(2, mvf, "f_stat", "f_var", w)

                def mlp_product(m):
                    b = FB * n + m
                    dve.wait_ge(S["gate_done"], b + 1)
                    wait(dve, S["pl_done"], b - 1)
                    nc.vector.tensor_tensor(prod[:, m % 2], ring[m % 3][0:FM, 1], gate[:, m % 2], ALU.mult
                                            ).then_inc(S["prod_done"], 1)
                    dve.wait_ge(S["prod_done"], b + 1)
                    if m == 0:
                        wait(dve, S["m_mm"], n)
                    nc.vector.tensor_copy(pt[0][:, m], prod[:, m % 2]).then_inc(S["ph_done"], 1)
                    dve.wait_ge(S["ph_done"], b + 1)
                    split_low(pt[1][:, m], prod[:, m % 2], pt[0][:, m], "pl_done")

                if valid(n, UC):
                    for m in range(T3_AT):
                        mlp_product(m)
                if valid(u, UC):
                    dve.wait_ge(S["xh_done"], u + 1)
                    split_low(xt[1][:], ps_t[:], xt[0][:], "xl_done")
                if valid(n - 2, UC):
                    w = n - 2
                    dve.wait_ge(S["f_scale"], w + 1)
                    for c in range(CC):
                        nc.vector.tensor_scalar(frow[:, c], frow[:, c], mvf[:, c, 0:1],
                                                sc[:, 2, c:c + 1], ALU.subtract, ALU.mult
                                                ).then_inc(S["f_norm"], 1)
                if valid(n, UC):
                    for m in range(T3_AT, FB):
                        mlp_product(m)
                if makes_weights(n):
                    made = (n - 1) // UCB
                    scaled_odd(made)
                    add_rank_one(made, range(KB))
                    for i in range(KB):
                        dve.wait_ge(S["weight_high"], PIECES * made + i + 1)
                        src, high, low = piece(i)
                        split_low(low, src, high, "weight_low1")
                    add_rank_one(made, range(KB, PIECES))
                    dve.wait_ge(S["weight_high"], PIECES * made + KB + 1)
                    src, high, low = piece(KB)
                    split_low(low, src, high, "weight_low2")
                    dve.wait_ge(S["weight_low2"], KB * (made + 1))
                if valid(u, UC):
                    for m in range(HB):
                        b = HB * u + m
                        dve.wait_ge(S["hid_done"], b + 1)
                        if m == 0:
                            wait(dve, S["w2_mm"], u)
                        nc.vector.tensor_copy(ht[0][:, m], hid[:, m % 2]).then_inc(S["hh_done"], 1)
                        if m % 2:
                            dve.wait_ge(S["hh_done"], b + 1)
                            split_low(ht[1][:, m], hid[:, m % 2], ht[0][:, m], "hl_odd")

            def scaled_odd(made):
                dve.wait_ge(S["xl_done"], UCB * made + 1)
                cols = [t[:, :, 2:2 + 4 * LORA:2].bitcast(F32) for t in xt]
                nc.vector.tensor_tensor(odd[:], cols[0], cols[1], ALU.add).then_inc(S["odd_done"], 1)
                dve.wait_ge(S["odd_done"], 2 * made + 1)
                nc.vector.tensor_scalar(odd[:], odd[:], scale_s[:, 0:1], None, ALU.mult
                                        ).then_inc(S["odd_done"], 1)
                dve.wait_ge(S["odd_done"], 2 * made + 2)
                dve.wait_ge(S["even_in"], 16 * (made + 1))

            def add_rank_one(made, pieces):
                for i in pieces:
                    dve.wait_ge(base_in[i % KB], 16 * (2 * made + i // KB + 1))
                    for q in range(LORA):
                        if i < KB:
                            row = even[:, q]
                            at = base[:, i, q * D:(q + 1) * D]
                            col = odd[:, i, q:q + 1]
                        else:
                            row = even[:, LORA + q].rearrange("p (a r) -> p r a", r=LORA)
                            at = base[:, i - KB].rearrange("p (r o) -> p r o", o=D)[
                                :, :, q * (D // LORA):(q + 1) * (D // LORA)]
                            col = odd[:, i - KB, LORA + q:LORA + q + 1]
                        nc.vector.scalar_tensor_tensor(at, row, col, at, ALU.mult, ALU.add
                                                       ).then_inc(S["weight_add"], 1)

            run_steps(dve, step, plan)

        @block.tensor
        def _(pe):
            def product(out, lhs, rhs, blocks, only=None):
                todo = [(a, b, kk) for a, b in PASSES for kk in only or range(blocks)]
                opens = only is None or only[0] == 0
                closes = only is None or only[-1] == blocks - 1
                for j, (a, b, kk) in enumerate(todo):
                    mm = nc.tensor.matmul(out, lhs(a, kk), rhs(b, kk), start=(opens and j == 0),
                                          stop=(closes and j == len(todo) - 1))
                return mm

            def chunk(c):
                return slice(c * P, (c + 1) * P)

            def transpose_unit(dst, src):
                for b in range(KB):
                    for c in range(CC):
                        mm = nc.tensor.transpose(dst[:, b, chunk(c)], src[:, c, b * P:(b + 1) * P], ident[:])
                return mm

            def mlp_block(n, m):
                if m >= 3:
                    pe.wait_ge(S["prod_done"], FB * n + m - 2)
                else:
                    wait(pe, S["hid_done"], HB * (n - 1) - (0 if m else 1))
                if m == 0:
                    pe.wait_ge(S["zl_done"], n + 1)
                bank = ring[m % 3]
                for side, w in enumerate((wl1, wl2)):
                    mm = product(bank[0:FM, side], lambda a, kk: w[a][:, kk, m * FM:(m + 1) * FM],
                                 lambda b, kk: zt[b][:, kk], KB)
                mm.then_inc(S["ml_mm"], 1)

            def ffn_down(c, only=None):
                return product(ps_w[:, c], lambda a, m: ht[a][:, m, chunk(c)],
                               lambda b, m: we2[b][:, m], HB, only)

            def step(n, par, k):
                u, w = n - 1, n - 2
                if valid(n, UC):
                    pe.wait_ge(S["y_copied"], n + 1)
                    wait(pe, S["yf_done"], n)
                    transpose_unit(ps_y, ys).then_inc(S["yt_mm"], 1)
                if valid(u, UC):
                    pe.wait_ge(S["pl_done"], FB * (u + 1))
                    wait(pe, S["a_done"], u)
                    for c in range(CC):
                        mm = product(ps_m[:, c], lambda a, m: pt[a][:, m, chunk(c)],
                                     lambda b, m: wl3[b][:, m], FB)
                    mm.then_inc(S["m_mm"], 1)
                if valid(n, UC):
                    pe.wait_ge(S["yl_done"], n + 1)
                    wait(pe, S["yrow_done"], n)
                    for c in range(CC):
                        mm = product(ps_o[:, c], lambda a, kk: yt[a][:, kk, chunk(c)],
                                     lambda b, kk: wout[b][:, kk], KB)
                    mm.then_inc(S["o_mm"], 1)
                if valid(w, UC):
                    pe.wait_ge(S["hl_even"], HB // 2 * (w + 1))
                    pe.wait_ge(S["hl_odd"], HB // 2 * (w + 1))
                    wait(pe, S["f_done"], w)
                    if is_step(n) and w % UCB == 0:
                        pe.wait_ge(S["weight_low2"], KB * (w // UCB + 1))
                    ffn_down(0)
                    ffn_down(1, range(HB // 2))
                if valid(n, UC):
                    pe.wait_ge(S["zm_done"], CC * (n + 1))
                    wait(pe, S["xl_done"], u)
                    transpose_unit(ps_t, rows).then_inc(S["zt_mm"], 1)
                if valid(w, UC):
                    ffn_down(1, range(HB // 2, HB)).then_inc(S["w2_mm"], 1)
                if valid(n, UC):
                    for m in range(T3_AT):
                        mlp_block(n, m)
                if valid(u, UC):
                    pe.wait_ge(S["xn_done"], CC * (u + 1))
                    if valid(n, UC):
                        pe.wait_ge(S["zl_done"], n + 1)
                    else:
                        wait(pe, S["xl_done"], u)
                    transpose_unit(ps_t, rows).then_inc(S["xt_mm"], 1)
                if valid(n, UC):
                    for m in range(T3_AT, FB):
                        mlp_block(n, m)
                if valid(u, UC):
                    pe.wait_ge(S["xl_done"], u + 1)
                    if makes_weights(n):
                        pe.wait_ge(S["weight_low1"], KB * ((n - 1) // UCB + 1))
                    for m in range(HB):
                        if m >= 3:
                            pe.wait_ge(S["hid_done"], HB * u + m - 2)
                        elif valid(n, UC):
                            pe.wait_ge(S["prod_done"], FB * n + FB - 2 + m)
                        else:
                            pe.wait_ge(S["hid_done"], HB * u)
                        product(ring[m % 3][:, 0], lambda a, kk: we1[a][:, kk, m * P:(m + 1) * P],
                                lambda b, kk: xt[b][:, kk], KB).then_inc(S["h_mm"], 1)

            run_steps(pe, step, plan)


def arrays(inputs):
    import numpy as np

    def get(name):
        return np.asarray(inputs["L0_" + name])

    def by_partition(a, p=P):
        a = a.reshape((a.shape[0] // p, p) + a.shape[1:])
        return np.ascontiguousarray(np.moveaxis(a, 0, 1))

    poles = get("attn_log_poles").reshape(D, STATES)
    residues = get("attn_residues")
    laid = {
        "x": get("attn_u").reshape(TOKENS, D),
        "pre_w": by_partition(get("attn_pre_norm_w")),
        "in_w": get("attn_in_proj_w").T,
        "short_w": by_partition(get("attn_short_w").reshape(3 * D, TAPS)),
        "short_b": by_partition(get("attn_short_b")),
        "lp_chan": by_partition(poles),
        "lp_group": poles.reshape(GROUPS, P).T,
        "lp_flat": poles.reshape(1, D * STATES),
        "res_chan": by_partition(residues),
        "res_group": residues.reshape(GROUPS, P).T,
        "d_skip": by_partition(get("attn_D_skip")),
        "out_w": get("attn_out_proj_w").T,
        "post_w": by_partition(get("attn_post_norm_w")),
        "l1_w": get("attn_l1_w").T,
        "l2_w": get("attn_l2_w").T,
        "l3_w": get("attn_l3_w").T,
        "w1": get("ffn_W1").T,
        "b1": by_partition(get("ffn_b1")),
        "w2": get("ffn_W2").T,
        "b2": get("ffn_b2").reshape(1, D),
        "scale": get("ffn_scale").reshape(1, 1),
    }
    return {k: np.ascontiguousarray(a) for k, a in laid.items()}


def kernel(**inputs):
    import numpy as np
    import concourse.bacc as bacc
    from concourse.bass_utils import run_bass_kernel_spmd

    nc = bacc.Bacc("TRN2", target_bir_lowering=False, num_devices=1)
    laid = arrays(inputs)
    args = [nc.dram_tensor(f"in_{name}", a.shape, mybir.dt.from_np(a.dtype), kind="ExternalInput").ap()
            for name, a in laid.items()]
    out = nc.dram_tensor("out", (TOKENS, D), F32, kind="ExternalOutput").ap()
    build(nc, *args, out)
    ran = run_bass_kernel_spmd(nc, [{f"in_{name}": a for name, a in laid.items()}], core_ids=[0])
    return np.asarray(ran.results[0]["out"]).reshape(B, L, D)
```

```python
from contextlib import ExitStack

import concourse.bass as bass
from concourse import mybir

ALU = mybir.AluOpType
ACT = mybir.ActivationFunctionType
F32 = mybir.dt.float32
F32R = mybir.dt.float32r

P = 128
B, L, D = 2, 4096, 256
TOKENS = B * L
KB = D // P
STATES = 16
TAPS = 3
ZB = 3 * D // P
CH = P
COLS = TOKENS // CH
BC = L // CH
FF = 672
FULL, REST = FF // P, FF % P
FB = FULL + 1
H = 1024
HB = H // P
EPS_LN, EPS_RMS = 1e-5, 1e-6

TA = 512
CA = TA // P
UA = TOKENS // TA
GC = P // STATES
GROUPS = D // GC
TC = 256
CC = TC // P
UC = TOKENS // TC
UCB = UC // B
LORA = 4
AHEAD = 2


def is_step(n):
    return isinstance(n, int)


def valid(n, units):
    return not is_step(n) or 0 <= n < units


def wait(eng, sem, value):
    if not is_step(value) or value > 0:
        eng.wait_ge(sem, value)


def aggregate_after(dve, vector, mark, sem, value):
    dve.wait_ge(sem, value)
    vector.memset(mark, 0.0)


def run_steps(eng, step, plan):
    for part in plan:
        if is_step(part):
            step(2 * part, 0, part)
            step(2 * part + 1, 1, part)
        else:
            with eng.Fori(*part) as k:
                step(2 * k, 0, k)
                step(2 * k + 1, 1, k)


def build(nc, x, pre_w, in_w, short_w, short_b, lp_chan, lp_group, lp_flat, res_chan, res_group,
          d_skip, out_w, post_w, l1_w, l2_w, l3_w, w1, b1, w2, b2, scale, out):
    x2_dram = nc.dram_tensor("x2_scratch", (P, KB, TOKENS), F32, kind="Internal").ap()
    taps_dram = nc.dram_tensor("taps_scratch", (D, 2 * CH), F32, kind="Internal").ap()
    lora_dram = nc.dram_tensor("lora_scratch", (4 * LORA, D), F32, kind="Internal").ap()
    half = P // 2
    with ExitStack() as whole:
        def sb(ctx, name, shape, dt=F32):
            return ctx.enter_context(nc.sbuf_tensor(name, shape, dt))

        def ps(ctx, name, shape):
            return ctx.enter_context(nc.psum_tensor(name, shape, F32))

        def sem(ctx, name):
            return ctx.enter_context(nc.semaphore(name))

        ident = sb(whole, "ident", [P, P])
        neg_half = sb(whole, "neg_half", [P, 2, CA])
        ln_scale = sb(whole, "ln_scale", [P, COLS])
        ln_mean = sb(whole, "ln_mean", [P, COLS])
        mark = sb(whole, "mark", [P, 1])
        seq = sb(whole, "seq", [P, D, COLS])
        wout = [sb(whole, f"wout_{s}", [P, KB, D], F32R) for s in "hl"]
        wl1 = [sb(whole, f"wl1_{s}", [P, KB, FULL * P], F32R) for s in "hl"]
        wl2 = [sb(whole, f"wl2_{s}", [P, KB, FULL * P], F32R) for s in "hl"]
        wrest = [sb(whole, f"wrest_{s}", [P, KB, 2 * REST], F32R) for s in "hl"]
        wl3 = [sb(whole, f"wl3_{s}", [P, FULL, D], F32R) for s in "hl"]
        wstack = sb(whole, "wstack", [3 * REST, D], F32R)

        phase_a(nc, whole, sb, ps, sem, locals())
        phase_b(nc, sb, ps, sem, locals())
        phase_c(nc, sb, ps, sem, locals())


def phase_a(nc, whole, sb, ps, sem, v):
    ident, neg_half, seq = v["ident"], v["neg_half"], v["seq"]
    ln_scale, ln_mean, mark = v["ln_scale"], v["ln_mean"], v["mark"]
    x2_dram, taps_dram = v["x2_dram"], v["taps_dram"]
    POWERS = 8
    with ExitStack() as ctx:
        win = sb(ctx, "win", [P, KB, 3 * D])
        win_r = [sb(ctx, f"win_{s}", [P, KB, 3 * D], F32R) for s in "hl"]
        pre = sb(ctx, "pre", [P, KB])
        sw = sb(ctx, "sw", [P, ZB, TAPS])
        sbias = sb(ctx, "sbias", [P, ZB])
        lpc = sb(ctx, "lpc", [P, KB, STATES])
        rc = sb(ctx, "rc", [P, KB, STATES])
        dsk = sb(ctx, "dsk", [P, KB])
        back = sb(ctx, "back", [P, CH])
        pole_pow = sb(ctx, "pole_pow", [P, POWERS, CH])
        taps = sb(ctx, "taps", [P, KB, 2 * CH])
        zero_halo = sb(ctx, "zero_halo", [P, ZB, TAPS - 1])
        xa = sb(ctx, "xa", [P, 2, CA, D])
        stats = sb(ctx, "stats", [P, CA, 6])
        mv = sb(ctx, "mv", [P, 2, CA, 2])
        st = sb(ctx, "st", [P, 2, CA])
        minus = sb(ctx, "minus", [P, 2, CA])
        zn = sb(ctx, "zn", [P, CA, D])
        zt = [sb(ctx, f"zt_{s}", [P, 2, KB, TA], F32R) for s in "hl"]
        zbuf = sb(ctx, "zbuf", [P, 2, ZB, TA + TAPS - 1])
        conv = sb(ctx, "conv", [P, ZB, TA])
        x2_tap = sb(ctx, "x2_tap", [P, KB, TA])
        xv = sb(ctx, "xv", [P, KB, TA])
        ps_t = ps(ctx, "ps_t", [P, KB, TA])
        ps_z = ps(ctx, "ps_z", [P, 3, TA])
        ps_x = ps(ctx, "ps_x", [P, CA, D])

        win_in = sem(ctx, "win_in")
        small_in = sem(ctx, "small_in")
        x_in = [sem(ctx, f"x_in{i}") for i in range(2)]
        x2_out = sem(ctx, "x2_out")
        taps_out = sem(ctx, "taps_out")
        consts = sem(ctx, "consts")
        tap_exp = sem(ctx, "tap_exp")
        tap_sum = sem(ctx, "tap_sum")
        taps_ready = sem(ctx, "taps_ready")
        win_fold = sem(ctx, "win_fold")
        stats_done = sem(ctx, "stats_done")
        args_done = sem(ctx, "args_done")
        st_done = sem(ctx, "st_done")
        zn_done = sem(ctx, "zn_done")
        zt_done = sem(ctx, "zt_done")
        zh_done = sem(ctx, "zh_done")
        zl_done = sem(ctx, "zl_done")
        z_mm = sem(ctx, "z_mm")
        halo_done = sem(ctx, "halo_done")
        z_copy = sem(ctx, "z_copy")
        conv_done = sem(ctx, "conv_done")
        x2_prod = sem(ctx, "x2_prod")
        x2_done = sem(ctx, "x2_done")
        xv_done = sem(ctx, "xv_done")
        xt_done = sem(ctx, "xt_done")
        xs_done = sem(ctx, "xs_done")
        ST = 4
        TX_AT = 2
        DT = 2 * ZB - KB
        order = (2, 4, 3, 5, 0, 1)
        plan = (0, 1, (2, 4), 4, (5, 7), 7, 8)
        x_rows = v["x"].rearrange("(n c p) d -> n p c d", c=CA, p=P)

        block = ctx.enter_context(nc.Block())

        @block.sync
        def _(sp):
            sp.dma_start(xa[:, 0], x_rows[0]).then_inc(x_in[0], 16)
            for dst, src in ((lpc, v["lp_chan"]), (rc, v["res_chan"]), (dsk, v["d_skip"]),
                             (pre, v["pre_w"]), (sw, v["short_w"]), (sbias, v["short_b"])):
                sp.dma_start(dst[:], src).then_inc(small_in, 16)
            sp.dma_start(win[:], v["in_w"].rearrange("(k p) o -> p k o", p=P)).then_inc(win_in, 16)

            def step(n, par, k):
                if valid(n + 1, UA):
                    wait(sp, zn_done, CA * n)
                    sp.dma_start(xa[:, 1 - par], x_rows[bass.ds(n + 1, 1)].rearrange("n p c d -> (n p) c d")
                                 ).then_inc(x_in[1 - par], 16)

            run_steps(sp, step, plan)
            sp.wait_ge(taps_ready, KB + 1)
            sp.dma_start(taps_dram.rearrange("(k p) t -> p k t", p=P), taps[:]).then_inc(taps_out, 16)
            sp.wait_ge(x2_out, 16 * UA)
            sp.wait_ge(taps_out, 16)

        @block.gpsimd
        def _(pool):
            nc.gpsimd.memset(ident[:], 1.0).then_inc(consts, 1)
            nc.gpsimd.memset(neg_half[:], -0.5).then_inc(consts, 1)
            nc.gpsimd.memset(zero_halo[:], 0.0).then_inc(consts, 1)
            nc.gpsimd.iota(back[:], [[-1, CH]], base=CH - 1, channel_multiplier=0,
                           allow_small_or_imprecise_dtypes=True).then_inc(consts, 1)
            pool.wait_ge(consts, 4)
            nc.gpsimd.affine_select(ident[:], ident[:], [[-1, P]], ALU.is_equal, 0.0, base=0,
                                    channel_multiplier=1).then_inc(consts, 1)

            def row_scales(n, par):
                pool.wait_ge(args_done, 3 * (n + 1))
                nc.gpsimd.tensor_tensor(st[:], st[:], neg_half[:], ALU.pow).then_inc(st_done, 1)
                pool.wait_ge(st_done, ST * n + 1)
                wait(pool, zt_done, n)
                nc.gpsimd.tensor_tensor(minus[:, 1], minus[:, 0], st[:, 1], ALU.mult
                                        ).then_inc(st_done, 1)
                pool.wait_ge(st_done, ST * n + 2)
                nc.gpsimd.tensor_copy(ln_scale[:, bass.ds(n * CA, CA)], st[:, 0]).then_inc(st_done, 1)
                nc.gpsimd.tensor_copy(ln_mean[:, bass.ds(n * CA, CA)], mv[:, par, :, 0]).then_inc(st_done, 1)
                for c in range(CA):
                    nc.gpsimd.tensor_scalar(zn[:, c], xa[:, par, c], st[:, 1, c:c + 1],
                                            minus[:, 1, c:c + 1], ALU.mult, ALU.add
                                            ).then_inc(zn_done, 1)

            row_scales(0, 0)

            def step(n, par, k):
                if valid(n + 1, UA):
                    row_scales(n + 1, 1 - par)
                if valid(n - 1, UA):
                    wait(pool, xt_done, n - 1)
                    for j in range(KB):
                        pool.wait_ge(conv_done, DT * (n - 1) + 4 * (j + 1))
                        nc.gpsimd.tensor_tensor(xv[:, j], conv[:, 2 + j], conv[:, 4 + j], ALU.mult
                                                ).then_inc(xv_done, 1)
                    pool.wait_ge(conv_done, DT * n)
                    pool.wait_ge(x2_prod, KB * n)
                    for j in range(KB):
                        nc.gpsimd.tensor_tensor(conv[:, j], conv[:, j], x2_tap[:, j], ALU.add
                                                ).then_inc(x2_done, 1)

            run_steps(pool, step, plan)

        @block.scalar
        def _(act):
            act.wait_ge(small_in, 16 * 6)
            act.wait_ge(consts, 5)

            def powers(steps):
                for i in steps:
                    wait(act, tap_sum, i - POWERS + 1)
                    s, kb = divmod(i, KB)
                    nc.scalar.activation(pole_pow[:, i % POWERS], back[:], ACT.Exp,
                                         scale=lpc[:, kb, s:s + 1]).then_inc(tap_exp, 1)

            powers(range(POWERS))

            def gate_rows(n):
                act.wait_ge(xt_done, n + 1)
                nc.scalar.activation(seq[:, :, bass.ds(n * CA, CA)].rearrange("p h c -> p c h"),
                                     ps_x[:], ACT.Copy).then_inc(xs_done, 1)

            def step(n, par, k):
                if valid(n, UA):
                    act.wait_ge(zt_done, n + 1)
                    wait(act, z_mm, ZB * (n - 1))
                    nc.scalar.activation(zt[0][:, par], ps_t[:], ACT.Copy).then_inc(zh_done, 1)
                if is_step(n) and n == 0:
                    powers(range(POWERS, KB * STATES))
                u = n - 1
                if valid(u, UA):
                    first = is_step(n) and u % (UA // B) == 0
                    wait(act, conv_done, DT * (u - 1))
                    wait(act, x2_prod, KB * (u - 1))
                    halo = zero_halo[:] if first else zbuf[:, par, :, TA:]
                    wait(act, z_copy, 2 * ZB * u)
                    nc.scalar.activation(zbuf[:, 1 - par, :, 0:TAPS - 1], halo, ACT.Copy
                                         ).then_inc(halo_done, 1)
                for i in range(ZB):
                    if valid(u - 1, UA) and i == 3:
                        gate_rows(u - 1)
                    if valid(u, UA):
                        m = order[i]
                        act.wait_ge(z_mm, ZB * u + i + 1)
                        nc.scalar.activation(zbuf[:, 1 - par, m, TAPS - 1:], ps_z[:, i % 3], ACT.Copy
                                             ).then_inc(z_copy, 1)
                        if i == 0:
                            wait(act, xv_done, KB * u)
                        if i == 4:
                            wait(act, x2_out, 16 * u)
                        nc.scalar.activation(conv[:, m], ps_z[:, i % 3], ACT.Identity,
                                             scale=sw[:, m, 2:3], bias=sbias[:, m:m + 1]
                                             ).then_inc(z_copy, 1)
                    if valid(u, UA) and i == ZB - 1:
                        for j in range(KB):
                            act.wait_ge(z_copy, 2 * (ZB * u + i + j))
                            nc.scalar.activation(x2_tap[:, j], zbuf[:, 1 - par, j, 0:TA], ACT.Copy,
                                                 scale=sw[:, j, 0:1]).then_inc(x2_prod, 1)
                    if valid(u - 1, UA) and i == 1:
                        act.wait_ge(x2_done, KB * u)
                        act.dma_start(x2_dram[:, :, bass.ds((u - 1) * TA, TA)], conv[:, 0:KB, :]
                                      ).then_inc(x2_out, 16)

            run_steps(act, step, plan)

        @block.vector
        def _(dve):
            nc.vector.memset(taps[:], 0.0).then_inc(taps_ready, 1)

            def row_stats(n, par, k):
                dve.wait_ge(x_in[par], 16 * (k + 1))
                wait(dve, st_done, ST * (n - 1))
                for c in range(CA):
                    nc.vector.bn_stats(stats[:, c], xa[:, par, c]).then_inc(stats_done, 1)
                aggregate_after(dve, nc.vector, mark[:], stats_done, 2 * CA * n + CA)
                for c in range(CA):
                    nc.vector.bn_aggr(mv[:, par, c], stats[:, c]).then_inc(stats_done, 1)
                dve.wait_ge(stats_done, 2 * CA * n + 2 * CA)
                wait(dve, st_done, ST * n)
                wait(dve, zn_done, CA * n)
                nc.vector.tensor_scalar(st[:, 0], mv[:, par, :, 1], EPS_LN, None, ALU.add
                                        ).then_inc(args_done, 1)
                nc.vector.tensor_scalar(st[:, 1], mv[:, par, :, 1], 1.0 + EPS_RMS, EPS_RMS * EPS_LN,
                                        ALU.mult, ALU.add).then_inc(args_done, 1)
                nc.vector.tensor_scalar(minus[:, 0], mv[:, par, :, 0], -1.0, None, ALU.mult
                                        ).then_inc(args_done, 1)

            row_stats(0, 0, 0)
            dve.wait_ge(small_in, 16 * 6)
            dve.wait_ge(win_in, 16)
            for k in range(KB):
                nc.vector.tensor_scalar(win[:, k], win[:, k], pre[:, k:k + 1], None, ALU.mult
                                        ).then_inc(win_fold, 1)
            dve.wait_ge(win_fold, KB)
            nc.vector.tensor_copy(win_r[0][:], win[:]).then_inc(win_fold, 1)
            dve.wait_ge(win_fold, KB + 1)
            nc.vector.tensor_tensor(win_r[1][:], win[:], win_r[0][:].bitcast(F32), ALU.subtract
                                    ).then_inc(win_fold, 1)

            def long_taps():
                dve.wait_ge(taps_ready, 1)
                for i in range(KB * STATES):
                    s, kb = divmod(i, KB)
                    dve.wait_ge(tap_exp, i + 1)
                    wait(dve, tap_sum, i - KB + 1)
                    nc.vector.scalar_tensor_tensor(taps[:, kb, 0:CH], pole_pow[:, i % POWERS],
                                                   rc[:, kb, s:s + 1], taps[:, kb, 0:CH],
                                                   ALU.mult, ALU.add).then_inc(tap_sum, 1)
                dve.wait_ge(tap_sum, KB * STATES)
                for k in range(KB):
                    nc.vector.tensor_tensor(taps[:, k, CH - 1:CH], taps[:, k, CH - 1:CH],
                                            dsk[:, k:k + 1], ALU.add).then_inc(taps_ready, 1)

            def step(n, par, k):
                start = is_step(n) and n == 0
                if start:
                    row_stats(1, 1, 0)
                if valid(n, UA):
                    dve.wait_ge(zh_done, n + 1)
                    nc.vector.tensor_tensor(zt[1][:, par], ps_t[:], zt[0][:, par].bitcast(F32),
                                            ALU.subtract).then_inc(zl_done, 1)
                u = n - 1
                if start:
                    long_taps()
                elif valid(n + 1, UA):
                    row_stats(n + 1, 1 - par, k + par)
                if valid(u, UA):
                    dve.wait_ge(halo_done, n)
                    for i in range(0, ZB, 2):
                        for tap, (j, m) in ((t, (j, order[j])) for t in ((1, 0) if i < 2 * KB else (1,))
                                            for j in (i, i + 1)):
                            if tap:
                                dve.wait_ge(z_copy, 2 * ZB * u + 2 * j + 2)
                            else:
                                dve.wait_ge(conv_done, DT * u + i + j + 1)
                            nc.vector.scalar_tensor_tensor(conv[:, m], zbuf[:, 1 - par, m, tap:TA + tap],
                                                           sw[:, m, tap:tap + 1], conv[:, m],
                                                           ALU.mult, ALU.add).then_inc(conv_done, 1)

            run_steps(dve, step, plan)

        @block.tensor
        def _(pe):
            pe.wait_ge(consts, 5)

            def turn_rows(n):
                pe.wait_ge(zn_done, CA * (n + 1))
                wait(pe, zl_done, n)
                for b in range(KB):
                    for c in range(CA):
                        mm = nc.tensor.transpose(ps_t[:, b, c * P:(c + 1) * P],
                                                 zn[:, c, b * P:(b + 1) * P], ident[:])
                mm.then_inc(zt_done, 1)

            def step(n, par, k):
                rows_late = is_step(n) and n == 1
                if valid(n, UA) and not rows_late:
                    turn_rows(n)
                u = n - 1
                if valid(u, UA):
                    if is_step(n) and u == 0:
                        pe.wait_ge(win_fold, KB + 2)
                    pe.wait_ge(zl_done, u + 1)
                for i in range(ZB):
                    if rows_late and i == TX_AT:
                        turn_rows(n)
                    if valid(u - 1, UA) and i == TX_AT:
                        pe.wait_ge(xv_done, KB * u)
                        wait(pe, xs_done, u - 1)
                        for c in range(CA):
                            for b in range(KB):
                                mm = nc.tensor.transpose(ps_x[:, c, b * P:(b + 1) * P],
                                                         xv[:, b, c * P:(c + 1) * P], ident[:])
                        mm.then_inc(xt_done, 1)
                    if valid(u, UA):
                        m = order[i]
                        wait(pe, z_copy, 2 * (ZB * u + i - 2))
                        passes = [(a, b, kk) for a, b in ((0, 0), (0, 1), (1, 0)) for kk in range(KB)]
                        for j, (a, b, kk) in enumerate(passes):
                            mm = nc.tensor.matmul(ps_z[:, i % 3], win_r[a][:, kk, m * P:(m + 1) * P],
                                                  zt[b][:, 1 - par, kk], start=(j == 0),
                                                  stop=(j == len(passes) - 1))
                        mm.then_inc(z_mm, 1)

            run_steps(pe, step, plan)


def phase_b(nc, sb, ps, sem, v):
    seq, taps_dram = v["seq"], v["taps_dram"]
    with ExitStack() as ctx:
        lpb = sb(ctx, "lpb", [P, D * STATES])
        lpg = sb(ctx, "lpg", [P, GROUPS])
        rg = sb(ctx, "rg", [P, GROUPS])
        pole_chunk = sb(ctx, "pole_chunk", [P, GROUPS])
        to_end = sb(ctx, "to_end", [P, 1])
        ahead = sb(ctx, "ahead", [P, CH])
        own = sb(ctx, "own", [P, 2 * GC, BC])
        later = sb(ctx, "later", [P, 2 * GC, BC])
        collect = sb(ctx, "collect", [P, 2, P])
        spread = sb(ctx, "spread", [P, 2, CH])
        decay = sb(ctx, "decay", [P, 2, 2 * GC * BC])
        inflow = sb(ctx, "inflow", [P, 2, 2 * GC, BC])
        state = sb(ctx, "state", [P, 2, 2 * GC * BC])
        toep = sb(ctx, "toep", [P, 2, GC, CH])
        raw = sb(ctx, "raw", [P, KB, FF])
        post = sb(ctx, "post", [P, KB])
        ps_s = [ps(ctx, f"ps_s{i}", [P, 2 * GC, BC]) for i in range(2)]
        ps_y = [ps(ctx, f"ps_y{i}", [P, 2 * GC * BC]) for i in range(2)]

        poles_in = sem(ctx, "poles_in")
        rest_in = sem(ctx, "rest_in")
        toep_in = [sem(ctx, f"toep_in{i}") for i in range(2)]
        raw_in = sem(ctx, "raw_in")
        split = sem(ctx, "split")
        bconst = sem(ctx, "bconst")
        pole_done = sem(ctx, "pole_done")
        collect_done = sem(ctx, "collect_done")
        spread_done = sem(ctx, "spread_done")
        decay_done = sem(ctx, "decay_done")
        s_mm = sem(ctx, "s_mm")
        toep_mm = sem(ctx, "toep_mm")
        y_mm = sem(ctx, "y_mm")
        inflow_done = sem(ctx, "inflow_done")
        scan_done = sem(ctx, "scan_done")
        y_done = sem(ctx, "y_done")
        plan = (0, (1, GROUPS // 2 - 1), GROUPS // 2 - 1)
        FIRST = 3 * P
        folded = ((v["l2_w"], v["wl2"], 0), (v["l1_w"], v["wl1"], REST))

        block = ctx.enter_context(nc.Block())

        @block.sync
        def _(sp):
            sp.dma_start(lpg[:], v["lp_group"]).then_inc(poles_in, 16)
            sp.dma_start(rg[:], v["res_group"]).then_inc(poles_in, 16)
            lp_flat = v["lp_flat"]
            sp.dma_start(lpb[:, 0:FIRST], bass.AP(lp_flat.tensor, 0, [[0, P], [1, FIRST]])
                         ).then_inc(poles_in, 16)

            def load(g, par):
                src = bass.AP(taps_dram.tensor, 2 * CH * GC * g, [[1, P], [2 * CH, GC], [1, CH]])
                wait(sp, toep_mm, g - 1)
                sp.dma_start(toep[:, par], src).then_inc(toep_in[par], 16)

            load(0, 0)
            load(1, 1)
            sp.dma_start(lpb[:, FIRST:], bass.AP(lp_flat.tensor, FIRST, [[0, P], [1, D * STATES - FIRST]])
                         ).then_inc(rest_in, 16)

            def step(g, par, k):
                if not (is_step(g) and g == 0) and valid(g + 1, GROUPS):
                    load(g + 1, 1 - par)

            run_steps(sp, step, plan)

        @block.gpsimd
        def _(pool):
            nc.gpsimd.iota(to_end[:], [[0, 1]], base=CH - 1, channel_multiplier=-1,
                           allow_small_or_imprecise_dtypes=True).then_inc(bconst, 1)
            nc.gpsimd.iota(ahead[:], [[-1, CH]], base=CH, channel_multiplier=0,
                           allow_small_or_imprecise_dtypes=True).then_inc(bconst, 1)
            nc.gpsimd.memset(own[:], 1.0).then_inc(bconst, 1)
            nc.gpsimd.memset(later[:], 1.0).then_inc(bconst, 1)
            nc.gpsimd.memset(inflow[:], 0.0).then_inc(bconst, 1)
            pool.wait_ge(bconst, 5)
            nc.gpsimd.memset(later[:, :, 0:1], 0.0).then_inc(bconst, 1)
            nc.gpsimd.affine_select(own[:], own[:], [[-STATES, GC], [0, 2 * BC]], ALU.is_ge, 0.0,
                                    base=0, channel_multiplier=1).then_inc(bconst, 1)
            pool.wait_ge(bconst, 7)
            nc.gpsimd.affine_select(own[:], own[:], [[STATES, GC], [0, 2 * BC]], ALU.is_ge, 0.0,
                                    base=STATES - 1, channel_multiplier=-1).then_inc(bconst, 1)

            wout, wl3, wrest, wstack = v["wout"], v["wl3"], v["wrest"], v["wstack"]
            raw_out = raw[:, :, 0:D]
            raw_l3 = raw[:].rearrange("p k f -> p (k f)")[:, 0:FULL * D].rearrange("p (m o) -> p m o", o=D)
            raw_stack = raw[0:3 * REST, 0, 0:D]
            count, loads = 0, 0
            pool.dma_start(post[:], v["post_w"]).then_inc(raw_in, 16)
            loads += 16
            pool.wait_ge(raw_in, loads)
            for src, dst, at in folded:
                pool.dma_start(raw[:], src.rearrange("(k p) f -> p k f", p=P)).then_inc(raw_in, 16)
                loads += 16
                pool.wait_ge(raw_in, loads)
                for kk in range(KB):
                    nc.gpsimd.tensor_scalar(raw[:, kk], raw[:, kk], post[:, kk:kk + 1], 1.0,
                                            ALU.mult, ALU.mult).then_inc(split, 1)
                count += KB
                pool.wait_ge(split, count)
                parts = ((raw[:, :, 0:FULL * P], [w[:] for w in dst]),
                         (raw[:, :, FULL * P:], [w[:, :, at:at + REST] for w in wrest]))
                for piece, (high, low) in parts:
                    nc.gpsimd.tensor_copy(high, piece).then_inc(split, 1)
                    count += 1
                    pool.wait_ge(split, count)
                    nc.gpsimd.tensor_tensor(low, piece, high.bitcast(F32), ALU.subtract
                                            ).then_inc(split, 1)
                    count += 1
                pool.wait_ge(split, count)
            pieces = [(v["out_w"].rearrange("(k p) o -> p k o", p=P), raw_out,
                       wout[0][:], wout[1][:])]
            pieces.append((v["l3_w"][0:FULL * P].rearrange("(m p) o -> p m o", p=P), raw_l3,
                           wl3[0][:], wl3[1][:]))
            for src, stage, high, low in pieces:
                pool.dma_start(stage, src).then_inc(raw_in, 16)
                loads += 16
                pool.wait_ge(raw_in, loads)
                nc.gpsimd.tensor_copy(high, stage).then_inc(split, 1)
                count += 1
                pool.wait_ge(split, count)
                nc.gpsimd.tensor_tensor(low, stage, high.bitcast(F32), ALU.subtract).then_inc(split, 1)
                count += 1
                pool.wait_ge(split, count)

            for q in range(3):
                pool.dma_start(raw_stack[q * REST:(q + 1) * REST], v["l3_w"][FULL * P:]
                               ).then_inc(raw_in, 16)
                loads += 16
            pool.wait_ge(raw_in, loads)
            nc.gpsimd.tensor_copy(wstack[:], raw_stack).then_inc(split, 1)
            count += 1
            pool.wait_ge(split, count)
            mid = slice(REST, 2 * REST)
            nc.gpsimd.tensor_tensor(wstack[mid], raw_stack[mid], wstack[mid].bitcast(F32), ALU.subtract
                                    ).then_inc(split, 1)
            count += 1
            pool.wait_ge(split, count)

        @block.scalar
        def _(act):
            act.wait_ge(poles_in, 48)
            act.wait_ge(bconst, 8)
            nc.scalar.activation(pole_chunk[:], lpg[:], ACT.Exp, scale=float(CH)).then_inc(pole_done, 1)
            act.wait_ge(pole_done, 1)

            def powers(g, par):
                if not is_step(g) or (g + 1) * P > FIRST:
                    act.wait_ge(rest_in, 16)
                wait(act, s_mm, g - 1)
                nc.scalar.activation(collect[:, par], lpb[:, bass.ds(g * P, P)], ACT.Exp,
                                     scale=to_end[:, 0:1]).then_inc(collect_done, 1)
                wait(act, scan_done, g - 1)
                nc.scalar.activation(decay[:, par], later[:].rearrange("p c j -> p (c j)"), ACT.Copy,
                                     scale=pole_chunk[:, bass.ds(g, 1)]).then_inc(decay_done, 1)
                wait(act, y_mm, g - 1)
                nc.scalar.activation(spread[:, par], ahead[:], ACT.Exp, scale=lpg[:, bass.ds(g, 1)]
                                     ).then_inc(spread_done, 1)

            powers(0, 0)

            def take(g, par):
                act.wait_ge(y_mm, g + 1)
                nc.scalar.activation(seq[:, bass.ds(g * GC, GC), :], ps_y[par][:], ACT.Copy
                                     ).then_inc(y_done, 1)

            def step(g, par, k):
                if valid(g + 1, GROUPS):
                    powers(g + 1, 1 - par)
                if valid(g - 1, GROUPS):
                    take(g - 1, 1 - par)

            run_steps(act, step, plan)
            take(GROUPS - 1, 1)

        @block.vector
        def _(dve):
            dve.wait_ge(poles_in, 48)
            dve.wait_ge(bconst, 8)

            def step(g, par, k):
                dve.wait_ge(s_mm, g + 1)
                wait(dve, scan_done, g - 1)
                nc.vector.scalar_tensor_tensor(inflow[:, par, :, 1:BC], ps_s[par][:, :, 0:BC - 1],
                                               rg[:, bass.ds(g, 1)], own[:, :, 0:BC - 1],
                                               ALU.mult, ALU.mult).then_inc(inflow_done, 1)
                dve.wait_ge(inflow_done, g + 1)
                dve.wait_ge(decay_done, g + 1)
                wait(dve, y_mm, g - 1)
                nc.vector.tensor_tensor_scan(state[:, par], decay[:, par],
                                             inflow[:, par].rearrange("p c j -> p (c j)"), 0.0,
                                             ALU.mult, ALU.add).then_inc(scan_done, 1)

            run_steps(dve, step, plan)

        @block.tensor
        def _(pe):
            def states_of(g, par):
                pe.wait_ge(collect_done, g + 1)
                wait(pe, inflow_done, g - 1)
                nc.tensor.matmul(ps_s[par][:].rearrange("p c j -> p (c j)"), collect[:, par],
                                 seq[:, bass.ds(g * GC, GC), :].rearrange("p h c -> p (h c)"),
                                 start=True, stop=True).then_inc(s_mm, 1)

            states_of(0, 0)

            def step(g, par, k):
                if valid(g + 1, GROUPS):
                    states_of(g + 1, 1 - par)
                pe.wait_ge(toep_in[par], 16 * (k + 1))
                wait(pe, y_done, g - 1)
                for c in range(GC):
                    mm = nc.tensor.matmul(ps_y[par][:, c * COLS:(c + 1) * COLS], toep[:, par, c],
                                          seq[:, bass.ds(g * GC + c, 1), :].rearrange("p h c -> p (h c)"),
                                          start=(c == 0), stop=False, skip_group_check=True)
                mm.then_inc(toep_mm, 1)
                pe.wait_ge(spread_done, g + 1)
                pe.wait_ge(scan_done, g + 1)
                nc.tensor.matmul(ps_y[par][:], spread[:, par], state[:, par], start=False, stop=True,
                                 skip_group_check=True).then_inc(y_mm, 1)

            run_steps(pe, step, plan)


def phase_c(nc, sb, ps, sem, v):
    ident, neg_half, seq = v["ident"], v["neg_half"], v["seq"]
    ln_scale, ln_mean, mark = v["ln_scale"], v["ln_mean"], v["mark"]
    wout, wl1, wl2, wl3 = v["wout"], v["wl1"], v["wl2"], v["wl3"]
    wrest, wstack = v["wrest"], v["wstack"]
    x2_dram, lora_dram = v["x2_dram"], v["lora_dram"]
    last = UC + AHEAD
    plan = (0, 1, (2, UCB // 2), UCB // 2, (UCB // 2 + 1, UC // 2 - 1), UC // 2 - 1, UC // 2)
    PASSES = ((0, 0), (0, 1), (1, 0))
    PASSES_T = ((0, 0), (1, 0), (0, 1))
    ACT_HIGHS = FB - 2
    T3_AT = FB // 2
    RING = 4
    HIDS = 3
    with ExitStack() as ctx:
        we1 = [sb(ctx, f"we1_{s}", [P, KB, H], F32R) for s in "hl"]
        we2 = [sb(ctx, f"we2_{s}", [P, HB, D], F32R) for s in "hl"]
        b1s = sb(ctx, "b1s", [P, HB])
        b2s = sb(ctx, "b2s", [P, CC, D])
        scale_s = sb(ctx, "scale_s", [P, 1])
        xs = sb(ctx, "xs", [P, 2, CC, D])
        x2s = sb(ctx, "x2s", [P, KB, TC])
        ys = sb(ctx, "ys", [P, CC, D])
        yf = sb(ctx, "yf", [P, KB, TC])
        yt = [sb(ctx, f"yt_{s}", [P, KB, TC], F32R) for s in "hl"]
        yrow = sb(ctx, "yrow", [P, 2, CC, D])
        rows = sb(ctx, "rows", [P, CC, D])
        zt = [sb(ctx, f"mt_{s}", [P, KB, TC], F32R) for s in "hl"]
        xt = [sb(ctx, f"xt_{s}", [P, KB, TC], F32R) for s in "hl"]
        gate = sb(ctx, "gate", [P, 2, TC])
        prod = sb(ctx, "prod", [P, 2, TC])
        pt = [sb(ctx, f"pt_{s}", [P, FULL, TC], F32R) for s in "hl"]
        pstack = sb(ctx, "pstack", [3 * REST, TC], F32R)
        x1 = sb(ctx, "x1", [P, 2, CC, D])
        hid = sb(ctx, "hid", [P, HIDS, TC])
        with ExitStack() as weights_made:
            even = sb(weights_made, "even", [P, 2 * LORA, D])
            base = sb(weights_made, "base", [P, 2, H])
        ht = [sb(ctx, f"ht_{s}", [P, HB, TC], F32R) for s in "hl"]
        frow = sb(ctx, "frow", [P, CC, D])
        orow = sb(ctx, "orow", [P, CC, D])
        odd = sb(ctx, "odd", [P, KB, 2 * LORA])
        bn = sb(ctx, "bn", [P, 3, CC, 6])
        mva = sb(ctx, "mva", [P, CC, 2])
        mvx = sb(ctx, "mvx", [P, CC, 2])
        mvf = sb(ctx, "mvf", [P, CC, 2])
        sc = sb(ctx, "sc", [P, 4, CC])
        sums = sb(ctx, "sums", [P, CC])
        mark_act = sb(ctx, "mark_act", [P, 1])
        ps_t = ps(ctx, "ps_rt", [P, KB, TC])
        ps_o = ps(ctx, "ps_o", [P, CC, D])
        ps_m = ps(ctx, "ps_m", [P, CC, D])
        ps_w = ps(ctx, "ps_w", [P, CC, D])
        ring = [ps(ctx, f"ps_ring{i}", [P, 2, TC]) for i in range(RING)]

        x_in = [sem(ctx, f"cx_in{i}") for i in range(2)]
        base_in = [sem(ctx, f"base_in{i}") for i in range(KB)]
        names = """x2_in rows_out consts_in y_copied yt_mm yf_done yh_done yl_done o_mm yrow_u yrow_done
                   squared rms_arg rms_done zm_done zt_mm zh_done zl_done ml_mm gate_done prod_done
                   ph_done high_here pl_done stacked m_mm a_done a_stat a_var a_scale x1_hat x1_done x_stat x_var x_scale
                   xn_done xt_mm xh_done xl_done h_mm hid_done hh_done hl_even hl_odd w2_mm f_done
                   f_stat f_var f_scale f_norm out_done lora_out even_in odd_done weight_add
                   weight_high weight_low1 weight_low2"""
        S = {n: sem(ctx, "c_" + n) for n in names.split()}

        x_rows = v["x"].rearrange("(n c p) d -> n p c d", c=CC, p=P)
        out_rows = v["out"].rearrange("(n c p) d -> n p c d", c=CC, p=P)
        w1_pieces = [v["w1"].rearrange("(k p) h -> k p h", p=P)[k] for k in range(KB)]
        w2_pieces = [v["w2"].rearrange("(r j p) o -> j p r o", j=KB, p=P)[j] for j in range(KB)]
        PIECES = 2 * KB

        def row_unit(t, n):
            return t[bass.ds(n, 1)].rearrange("n p c d -> (n p) c d")

        def piece(i):
            if i < KB:
                return base[:, i], we1[0][:, i], we1[1][:, i]
            view = [w[:].rearrange("p (r j) o -> p j r o", j=KB)[:, i - KB] for w in we2]
            return base[:, i - KB].rearrange("p (r o) -> p r o", o=D), view[0], view[1]

        def product_views(m):
            if m < FULL:
                return pt[0][:, m], prod[:, m % 2], pt[1][:, m]
            return pstack[0:REST], prod[0:REST, m % 2], pstack[2 * REST:]

        def makes_weights(n):
            return is_step(n) and 0 <= n - 1 < UC and (n - 1) % UCB == 0

        block = ctx.enter_context(nc.Block())

        @block.sync
        def _(sp):
            sp.dma_start(x2s[:], x2_dram[:, :, 0:TC]).then_inc(S["x2_in"], 16)
            sp.dma_start(xs[:, 0], x_rows[0]).then_inc(x_in[0], 16)
            sp.dma_start(b1s[:], v["b1"]).then_inc(S["consts_in"], 16)
            for c in range(CC):
                sp.dma_start(b2s[:, c], bass.AP(v["b2"].tensor, 0, [[0, P], [1, D]])
                             ).then_inc(S["consts_in"], 16)
            sp.dma_start(scale_s[:], bass.AP(v["scale"].tensor, 0, [[0, P], [1, 1]])
                         ).then_inc(S["consts_in"], 16)

            def load_piece(made, i):
                if i >= KB:
                    sp.wait_ge(S["weight_low1"], KB * made + i - KB + 1)
                if i < KB:
                    sp.dma_start(base[:, i], w1_pieces[i]).then_inc(base_in[i], 16)
                else:
                    sp.dma_start(base[:, i - KB].rearrange("p (r o) -> p r o", o=D), w2_pieces[i - KB]
                                 ).then_inc(base_in[i - KB], 16)

            def store(n):
                sp.wait_ge(S["out_done"], n + 1)
                sp.dma_start(row_unit(out_rows, n), orow[:]).then_inc(S["rows_out"], 16)

            def step(n, par, k):
                if valid(n + 1, UC):
                    sp.wait_ge(S["yf_done"], n + 1)
                    sp.dma_start(x2s[:], x2_dram[:, :, bass.ds((n + 1) * TC, TC)]).then_inc(S["x2_in"], 16)
                if valid(n - 3, UC):
                    store(n - 3)
                if valid(n + 1, UC):
                    wait(sp, S["x1_done"], n)
                    sp.dma_start(xs[:, 1 - par], row_unit(x_rows, n + 1)).then_inc(x_in[1 - par], 16)
                if makes_weights(n):
                    made = (n - 1) // UCB
                    wait(sp, S["w2_mm"], n - 1)
                    load_piece(made, 0)
                    load_piece(made, 1)
                    sp.wait_ge(S["xn_done"], CC * n)
                    sp.dma_start(lora_dram, rows[1:1 + 4 * LORA, 0, :]).then_inc(S["lora_out"], 16)
                    sp.wait_ge(S["lora_out"], 16 * (made + 1))
                    sp.dma_start(even[:], bass.AP(lora_dram.tensor, 0, [[0, P], [2 * D, 2 * LORA], [1, D]])
                                 ).then_inc(S["even_in"], 16)
                    load_piece(made, 2)
                    load_piece(made, 3)

            run_steps(sp, step, plan)
            store(UC - 1)
            sp.wait_ge(S["rows_out"], 16 * UC)

        @block.gpsimd
        def _(pool):
            def copy_y(n):
                wait(pool, S["yt_mm"], n)
                nc.gpsimd.tensor_copy(ys[:], seq[:, :, bass.ds(n * CC, CC)].rearrange("p h c -> p c h")
                                      ).then_inc(S["y_copied"], 1)

            def inverse_root(var, to, done, n):
                pool.wait_ge(S[var], n + 1)
                nc.gpsimd.tensor_tensor(sc[:, to], sc[:, to], neg_half[:, 0, 0:CC], ALU.pow
                                        ).then_inc(S[done], 1)

            copy_y(0)

            def add_out(n, par):
                pool.wait_ge(S["f_norm"], CC * (n + 1))
                wait(pool, S["rows_out"], 16 * n)
                nc.gpsimd.tensor_tensor(orow[:], frow[:], x1[:, par], ALU.add).then_inc(S["out_done"], 1)

            def step(n, par, k):
                if valid(n - 3, UC):
                    add_out(n - 3, 1 - par)
                if valid(n, UC):
                    inverse_root("rms_arg", 3, "rms_done", n)
                if valid(n - 1, UC):
                    inverse_root("a_var", 0, "a_scale", n - 1)
                if valid(n - 1, UC):
                    inverse_root("x_var", 1, "x_scale", n - 1)
                if valid(n + 1, UC):
                    copy_y(n + 1)
                if valid(n - 2, UC):
                    inverse_root("f_var", 2, "f_scale", n - 2)
                if makes_weights(n):
                    made = (n - 1) // UCB
                    pool.wait_ge(S["weight_high"], PIECES * made + PIECES)
                    src, high, low = piece(PIECES - 1)
                    nc.gpsimd.tensor_tensor(low, src, high.bitcast(F32), ALU.subtract
                                            ).then_inc(S["weight_low2"], 1)
                    pool.wait_ge(S["weight_low2"], KB * (made + 1))
                if valid(n - 1, UC):
                    for m in range(0, HB, 2):
                        pool.wait_ge(S["hh_done"], HB * (n - 1) + m + 1)
                        nc.gpsimd.tensor_tensor(ht[1][:, m], hid[:, m % HIDS], ht[0][:, m].bitcast(F32),
                                                ALU.subtract).then_inc(S["hl_even"], 1)

            run_steps(pool, step, plan)
            add_out(UC - 1, (UC - 1) % 2)

        @block.scalar
        def _(act):
            act.wait_ge(S["consts_in"], 16 * (CC + 2))

            def load_table(function):
                nc.scalar.activation(mark_act[:], neg_half[:, 0, 0:1], function)

            def step(n, par, k):
                if valid(n, UC):
                    act.wait_ge(S["yrow_done"], n + 1)
                    wait(act, S["rms_arg"], n)
                    wait(act, S["xt_mm"], n - 1)
                    for c in range(CC):
                        nc.scalar.activation(rows[:, c], yrow[:, par, c], ACT.Square,
                                             accum_out=sums[:, c:c + 1]).then_inc(S["squared"], 1)
                    act.wait_ge(S["rms_done"], n + 1)
                    for c in range(CC):
                        nc.scalar.activation(rows[:, c], yrow[:, par, c], ACT.Copy,
                                             scale=sc[:, 3, c:c + 1]).then_inc(S["zm_done"], 1)
                    act.wait_ge(S["zt_mm"], n + 1)
                    wait(act, S["ml_mm"], FB * n)
                    nc.scalar.activation(zt[0][:], ps_t[:], ACT.Copy).then_inc(S["zh_done"], 1)
                    load_table(ACT.Gelu_apprx_tanh)

                def product_high(m):
                    act.wait_ge(S["prod_done"], FB * n + m + 1)
                    if m == 0:
                        wait(act, S["m_mm"], n)
                    high, src = product_views(m)[:2]
                    nc.scalar.activation(high, src, ACT.Copy).then_inc(S["ph_done"], 1)

                def mlp_gate(m):
                    act.wait_ge(S["ml_mm"], FB * n + m + 1)
                    wait(act, S["prod_done"], FB * n + m - 1)
                    rows_of = slice(0, P) if m < FULL else slice(REST, 2 * REST)
                    nc.scalar.activation(gate[rows_of, m % 2], ring[m % RING][rows_of, 0],
                                         ACT.Gelu_apprx_tanh).then_inc(S["gate_done"], 1)
                    if m == FB - 1:
                        load_table(ACT.Gelu)
                    elif m > 0:
                        product_high(m - 1)

                if valid(n, UC):
                    for m in range(T3_AT):
                        mlp_gate(m)
                if valid(n - 1, UC):
                    act.wait_ge(S["xt_mm"], n)
                    wait(act, S["h_mm"], HB * (n - 1))
                    nc.scalar.activation(xt[0][:], ps_t[:], ACT.Copy).then_inc(S["xh_done"], 1)
                if valid(n, UC):
                    for m in range(T3_AT, FB):
                        mlp_gate(m)
                if makes_weights(n):
                    made = (n - 1) // UCB
                    wait(act, S["h_mm"], HB * (n - 1))
                    wait(act, S["w2_mm"], n - 1)
                    for i in range(PIECES):
                        act.wait_ge(S["weight_add"], 2 * LORA * made * KB + LORA * (i + 1))
                        src, high, low = piece(i)
                        nc.scalar.activation(high, src, ACT.Copy).then_inc(S["weight_high"], 1)
                if valid(n - 1, UC):
                    wait(act, S["w2_mm"], n - 1)
                    for m in range(HB):
                        b = HB * (n - 1) + m
                        act.wait_ge(S["h_mm"], b + 1)
                        half = HB // 2 * (n - 1)
                        if m < HIDS:
                            wait(act, S["hl_even"], half)
                            wait(act, S["hl_odd"], half)
                        else:
                            act.wait_ge(S["hl_odd" if (m - HIDS) % 2 else "hl_even"],
                                        half + (m - HIDS) // 2 + 1)
                        nc.scalar.activation(hid[:, m % HIDS], ring[(m + 2) % RING][:, 0], ACT.Gelu,
                                             bias=b1s[:, m:m + 1]).then_inc(S["hid_done"], 1)

            run_steps(act, step, plan)

        @block.vector
        def _(dve):
            dve.wait_ge(S["consts_in"], 16 * (CC + 2))

            def measure(src, kind, stat):
                for c in range(CC):
                    nc.vector.bn_stats(bn[:, kind, c], src[:, c]).then_inc(S[stat], 1)

            def aggregate(kind, mv, stat, var, n):
                aggregate_after(dve, nc.vector, mark[:], S[stat], 2 * CC * n + CC)
                for c in range(CC):
                    nc.vector.bn_aggr(mv[:, c], bn[:, kind, c]).then_inc(S[stat], 1)
                dve.wait_ge(S[stat], 2 * CC * (n + 1))
                nc.vector.tensor_scalar(sc[:, kind], mv[:, :, 1], EPS_LN, None, ALU.add
                                        ).then_inc(S[var], 1)

            def split_low(low, src, high, done):
                nc.vector.tensor_tensor(low, src, high.bitcast(F32), ALU.subtract).then_inc(S[done], 1)

            def gate_y(n, part):
                if part == 0:
                    dve.wait_ge(S["yt_mm"], n + 1)
                    dve.wait_ge(S["x2_in"], 16 * (n + 1))
                    wait(dve, S["yl_done"], n)
                    back = ps_t[:].rearrange("p b (c t) -> p (b c) t", t=CH)[:, :, ::-1]
                    nc.vector.tensor_tensor(yf[:].rearrange("p b (c t) -> p (b c) t", t=CH), back,
                                            x2s[:].rearrange("p b (c t) -> p (b c) t", t=CH), ALU.mult
                                            ).then_inc(S["yf_done"], 1)
                elif part == 1:
                    dve.wait_ge(S["yf_done"], n + 1)
                    wait(dve, S["o_mm"], n)
                    nc.vector.tensor_copy(yt[0][:], yf[:]).then_inc(S["yh_done"], 1)
                else:
                    dve.wait_ge(S["yh_done"], n + 1)
                    split_low(yt[1][:], yf[:], yt[0][:], "yl_done")

            def normalize_f(n):
                dve.wait_ge(S["f_scale"], n + 1)
                for c in range(CC):
                    nc.vector.tensor_scalar(frow[:, c], frow[:, c], mvf[:, c, 0:1], sc[:, 2, c:c + 1],
                                            ALU.subtract, ALU.mult).then_inc(S["f_norm"], 1)

            def step(n, par, k):
                if valid(n - 3, UC):
                    normalize_f(n - 3)
                old = 1 - par
                u = n - 1
                if valid(n, UC):
                    dve.wait_ge(x_in[par], 16 * (k + 1))
                    wait(dve, S["x1_hat"], CC * (n - 1))
                    for c in range(CC):
                        nc.vector.tensor_scalar(yrow[:, par, c], xs[:, par, c],
                                                ln_mean[:, bass.ds(n * CC + c, 1)],
                                                ln_scale[:, bass.ds(n * CC + c, 1)],
                                                ALU.subtract, ALU.mult).then_inc(S["yrow_u"], 1)
                if valid(u, UC):
                    dve.wait_ge(S["m_mm"], u + 1)
                    wait(dve, S["zm_done"], CC * (u + 1))
                    nc.vector.tensor_tensor(yrow[:, old], ps_m[:], yrow[:, old], ALU.add
                                            ).then_inc(S["a_done"], 1)
                if valid(n, UC):
                    dve.wait_ge(S["yrow_u"], CC * (n + 1))
                    dve.wait_ge(S["o_mm"], n + 1)
                    nc.vector.tensor_tensor(yrow[:, par], ps_o[:], yrow[:, par], ALU.add
                                            ).then_inc(S["yrow_done"], 1)
                if valid(u, UC):
                    dve.wait_ge(S["a_done"], u + 1)
                    wait(dve, S["x1_hat"], CC * u)
                    measure(yrow[:, old], 0, "a_stat")
                if valid(n, UC):
                    dve.wait_ge(S["squared"], CC * (n + 1))
                    wait(dve, S["zm_done"], CC * n)
                    nc.vector.tensor_scalar(sc[:, 3], sums[:], 1.0 / D, EPS_RMS, ALU.mult, ALU.add
                                            ).then_inc(S["rms_arg"], 1)
                if valid(u, UC):
                    aggregate(0, mva, "a_stat", "a_var", u)
                if valid(u, UC):
                    dve.wait_ge(S["a_scale"], u + 1)
                    wait(dve, S["out_done"], u - 1)
                    for c in range(CC):
                        nc.vector.tensor_scalar(x1[:, old, c], yrow[:, old, c], mva[:, c, 0:1],
                                                sc[:, 0, c:c + 1], ALU.subtract, ALU.mult
                                                ).then_inc(S["x1_hat"], 1)
                    dve.wait_ge(S["x1_hat"], CC * (u + 1))
                    nc.vector.tensor_tensor(x1[:, old], x1[:, old], xs[:, old], ALU.add
                                            ).then_inc(S["x1_done"], 1)
                if valid(n, UC):
                    dve.wait_ge(S["zh_done"], n + 1)
                    split_low(zt[1][:], ps_t[:], zt[0][:], "zl_done")
                if valid(u, UC):
                    dve.wait_ge(S["x1_done"], u + 1)
                    wait(dve, S["xn_done"], CC * u)
                    measure(x1[:, old], 1, "x_stat")
                if valid(u, UC):
                    aggregate(1, mvx, "x_stat", "x_var", u)
                if valid(u, UC):
                    dve.wait_ge(S["x_scale"], u + 1)
                    if valid(n, UC):
                        dve.wait_ge(S["zt_mm"], n + 1)
                    else:
                        wait(dve, S["xt_mm"], u)
                    for c in range(CC):
                        nc.vector.tensor_scalar(rows[:, c], x1[:, old, c], mvx[:, c, 0:1],
                                                sc[:, 1, c:c + 1], ALU.subtract, ALU.mult
                                                ).then_inc(S["xn_done"], 1)
                if valid(n - 2, UC):
                    w = n - 2
                    dve.wait_ge(S["w2_mm"], w + 1)
                    wait(dve, S["out_done"], w)
                    nc.vector.tensor_tensor(frow[:], ps_w[:], b2s[:], ALU.add).then_inc(S["f_done"], 1)
                    dve.wait_ge(S["f_done"], w + 1)
                    wait(dve, S["f_norm"], CC * w)
                    measure(frow[:], 2, "f_stat")
                    aggregate(2, mvf, "f_stat", "f_var", w)

                def mlp_product(m):
                    b = FB * n + m
                    dve.wait_ge(S["gate_done"], b + 1)
                    wait(dve, S["pl_done"], b - 1)
                    if m < FULL:
                        value, gated = ring[m % RING][:, 1], gate[:, m % 2]
                    else:
                        value, gated = ring[m % RING][0:REST, 0], gate[REST:2 * REST, m % 2]
                    nc.vector.tensor_tensor(product_views(m)[1], value, gated, ALU.mult
                                            ).then_inc(S["prod_done"], 1)
                    if m > 0:
                        product_low(m - 1)
                    if m == FB - 1:
                        product_low(m)

                def product_low(m):
                    high, src, low = product_views(m)
                    if m < ACT_HIGHS:
                        dve.wait_ge(S["ph_done"], ACT_HIGHS * n + m + 1)
                    else:
                        dve.wait_ge(S["prod_done"], FB * n + m + 1)
                        nc.vector.tensor_copy(high, src).then_inc(S["high_here"], 1)
                        dve.wait_ge(S["high_here"], (FB - ACT_HIGHS) * n + m - ACT_HIGHS + 1)
                    if m == FULL:
                        nc.vector.tensor_copy(pstack[REST:2 * REST], src).then_inc(S["stacked"], 1)
                    split_low(low, src, high, "pl_done")

                if valid(n, UC):
                    for m in range(T3_AT):
                        mlp_product(m)
                if valid(u, UC):
                    dve.wait_ge(S["xh_done"], u + 1)
                    split_low(xt[1][:], ps_t[:], xt[0][:], "xl_done")
                if valid(n, UC):
                    for m in range(T3_AT, FB):
                        mlp_product(m)
                if valid(n + 1, UC) and not valid(u, UC):
                    for part in range(3):
                        gate_y(n + 1, part)
                if makes_weights(n):
                    made = (n - 1) // UCB
                    scaled_odd(made)
                    add_rank_one(made, range(KB))
                    for i in range(KB):
                        dve.wait_ge(S["weight_high"], PIECES * made + i + 1)
                        src, high, low = piece(i)
                        split_low(low, src, high, "weight_low1")
                    add_rank_one(made, range(KB, PIECES))
                    dve.wait_ge(S["weight_high"], PIECES * made + KB + 1)
                    src, high, low = piece(KB)
                    split_low(low, src, high, "weight_low2")
                    dve.wait_ge(S["weight_low2"], KB * (made + 1))
                if valid(u, UC):
                    for m in range(HB):
                        b = HB * u + m
                        dve.wait_ge(S["hid_done"], b + 1)
                        if m == 0:
                            wait(dve, S["w2_mm"], u)
                        nc.vector.tensor_copy(ht[0][:, m], hid[:, m % HIDS]).then_inc(S["hh_done"], 1)
                        if m % 2:
                            dve.wait_ge(S["hh_done"], b + 1)
                            split_low(ht[1][:, m], hid[:, m % HIDS], ht[0][:, m], "hl_odd")
                        if valid(n + 1, UC) and m in (1, 3, 5):
                            gate_y(n + 1, m // 2)

            def scaled_odd(made):
                dve.wait_ge(S["xl_done"], UCB * made + 1)
                cols = [t[:, :, 2:2 + 4 * LORA:2].bitcast(F32) for t in xt]
                nc.vector.tensor_tensor(odd[:], cols[0], cols[1], ALU.add).then_inc(S["odd_done"], 1)
                dve.wait_ge(S["odd_done"], 2 * made + 1)
                nc.vector.tensor_scalar(odd[:], odd[:], scale_s[:, 0:1], None, ALU.mult
                                        ).then_inc(S["odd_done"], 1)
                dve.wait_ge(S["odd_done"], 2 * made + 2)
                dve.wait_ge(S["even_in"], 16 * (made + 1))

            def add_rank_one(made, pieces):
                for i in pieces:
                    dve.wait_ge(base_in[i % KB], 16 * (2 * made + i // KB + 1))
                    for q in range(LORA):
                        if i < KB:
                            row = even[:, q]
                            at = base[:, i, q * D:(q + 1) * D]
                            col = odd[:, i, q:q + 1]
                        else:
                            row = even[:, LORA + q].rearrange("p (a r) -> p r a", r=LORA)
                            at = base[:, i - KB].rearrange("p (r o) -> p r o", o=D)[
                                :, :, q * (D // LORA):(q + 1) * (D // LORA)]
                            col = odd[:, i - KB, LORA + q:LORA + q + 1]
                        nc.vector.scalar_tensor_tensor(at, row, col, at, ALU.mult, ALU.add
                                                       ).then_inc(S["weight_add"], 1)

            for part in range(3):
                gate_y(0, part)
            run_steps(dve, step, plan)
            normalize_f(UC - 1)

        @block.tensor
        def _(pe):
            def product(out, lhs, rhs, blocks, only=None, closed=True, passes=PASSES, low_ready=None):
                todo = [(a, b, kk) for a, b in passes for kk in only or range(blocks)]
                opens = only is None or only[0] == 0
                closes = closed and (only is None or only[-1] == blocks - 1)
                for j, (a, b, kk) in enumerate(todo):
                    if low_ready and j == len(todo) - blocks:
                        pe.wait_ge(*low_ready)
                    mm = nc.tensor.matmul(out, lhs(a, kk), rhs(b, kk), start=(opens and j == 0),
                                          stop=(closes and j == len(todo) - 1))
                return mm

            def chunk(c):
                return slice(c * P, (c + 1) * P)

            def transpose_unit(dst, src):
                for b in range(KB):
                    for c in range(CC):
                        mm = nc.tensor.transpose(dst[:, b, chunk(c)], src[:, c, b * P:(b + 1) * P], ident[:])
                return mm

            def mlp_block(n, m):
                if m >= RING:
                    pe.wait_ge(S["prod_done"], FB * n + m - RING + 1)
                else:
                    wait(pe, S["hid_done"], HB * (n - 1) - (0 if m else 1))
                if m == 0:
                    pe.wait_ge(S["zh_done"], n + 1)
                bank = ring[m % RING]
                if m < FULL:
                    for side, w in enumerate((wl1, wl2)):
                        mm = product(bank[:, side], lambda a, kk: w[a][:, kk, m * P:(m + 1) * P],
                                     lambda b, kk: zt[b][:, kk], KB, passes=PASSES_T,
                                     low_ready=(S["zl_done"], n + 1) if m == side == 0 else None)
                else:
                    mm = product(bank[0:2 * REST, 0], lambda a, kk: wrest[a][:, kk],
                                 lambda b, kk: zt[b][:, kk], KB)
                mm.then_inc(S["ml_mm"], 1)

            def ffn_down(c, only=None):
                return product(ps_w[:, c], lambda a, m: ht[a][:, m, chunk(c)],
                               lambda b, m: we2[b][:, m], HB, only)

            def turn_y(n):
                pe.wait_ge(S["y_copied"], n + 1)
                transpose_unit(ps_t, ys).then_inc(S["yt_mm"], 1)

            def step(n, par, k):
                u, w = n - 1, n - 2
                if valid(u, UC):
                    pe.wait_ge(S["pl_done"], FB * (u + 1))
                    wait(pe, S["a_done"], u)
                    pe.wait_ge(S["stacked"], u + 1)
                    for c in range(CC):
                        product(ps_m[:, c], lambda a, m: pt[a][:, m, chunk(c)],
                                lambda b, m: wl3[b][:, m], FULL, closed=False)
                        mm = nc.tensor.matmul(ps_m[:, c], pstack[:, chunk(c)], wstack[:],
                                              start=False, stop=True)
                    mm.then_inc(S["m_mm"], 1)
                if valid(n, UC):
                    pe.wait_ge(S["yl_done"], n + 1)
                    wait(pe, S["yrow_done"], n)
                    for c in range(CC):
                        mm = product(ps_o[:, c], lambda a, kk: yt[a][:, kk, chunk(c)],
                                     lambda b, kk: wout[b][:, kk], KB)
                    mm.then_inc(S["o_mm"], 1)
                if valid(w, UC):
                    pe.wait_ge(S["hl_even"], HB // 2 * (w + 1))
                    pe.wait_ge(S["hl_odd"], HB // 2 * (w + 1))
                    wait(pe, S["f_done"], w)
                    if is_step(n) and w % UCB == 0:
                        pe.wait_ge(S["weight_low2"], KB * (w // UCB + 1))
                    ffn_down(0)
                    ffn_down(1, range(HB // 2))
                if valid(n, UC):
                    pe.wait_ge(S["zm_done"], CC * (n + 1))
                    pe.wait_ge(S["yf_done"], n + 1)
                    transpose_unit(ps_t, rows).then_inc(S["zt_mm"], 1)
                if valid(w, UC):
                    ffn_down(1, range(HB // 2, HB)).then_inc(S["w2_mm"], 1)
                if valid(n, UC):
                    for m in range(T3_AT):
                        mlp_block(n, m)
                if valid(u, UC):
                    pe.wait_ge(S["xn_done"], CC * (u + 1))
                    if valid(n, UC):
                        pe.wait_ge(S["zl_done"], n + 1)
                    else:
                        wait(pe, S["xl_done"], u)
                    transpose_unit(ps_t, rows).then_inc(S["xt_mm"], 1)
                if valid(n, UC):
                    for m in range(T3_AT, FB):
                        mlp_block(n, m)
                if valid(n + 1, UC):
                    if valid(u, UC):
                        pe.wait_ge(S["xl_done"], u + 1)
                    else:
                        pe.wait_ge(S["zl_done"], n + 1)
                    turn_y(n + 1)
                if valid(u, UC):
                    pe.wait_ge(S["xl_done"], u + 1)
                    if makes_weights(n):
                        pe.wait_ge(S["weight_low1"], KB * ((n - 1) // UCB + 1))
                    for m in range(HB):
                        if m >= RING:
                            pe.wait_ge(S["hid_done"], HB * u + m - RING + 1)
                        elif valid(n, UC):
                            pe.wait_ge(S["prod_done"], FB * n + FB - RING + m + 1)
                        else:
                            pe.wait_ge(S["hid_done"], HB * u)
                        product(ring[(m + 2) % RING][:, 0], lambda a, kk: we1[a][:, kk, m * P:(m + 1) * P],
                                lambda b, kk: xt[b][:, kk], KB).then_inc(S["h_mm"], 1)

            turn_y(0)
            run_steps(pe, step, plan)


def arrays(inputs):
    import numpy as np

    def get(name):
        return np.asarray(inputs["L0_" + name])

    def by_partition(a, p=P):
        a = a.reshape((a.shape[0] // p, p) + a.shape[1:])
        return np.ascontiguousarray(np.moveaxis(a, 0, 1))

    poles = get("attn_log_poles").reshape(D, STATES)
    residues = get("attn_residues")
    laid = {
        "x": get("attn_u").reshape(TOKENS, D),
        "pre_w": by_partition(get("attn_pre_norm_w")),
        "in_w": get("attn_in_proj_w").T,
        "short_w": by_partition(get("attn_short_w").reshape(3 * D, TAPS)),
        "short_b": by_partition(get("attn_short_b")),
        "lp_chan": by_partition(poles),
        "lp_group": poles.reshape(GROUPS, P).T,
        "lp_flat": poles.reshape(1, D * STATES),
        "res_chan": by_partition(residues),
        "res_group": residues.reshape(GROUPS, P).T,
        "d_skip": by_partition(get("attn_D_skip")),
        "out_w": get("attn_out_proj_w").T,
        "post_w": by_partition(get("attn_post_norm_w")),
        "l1_w": get("attn_l1_w").T,
        "l2_w": get("attn_l2_w").T,
        "l3_w": get("attn_l3_w").T,
        "w1": get("ffn_W1").T,
        "b1": by_partition(get("ffn_b1")),
        "w2": get("ffn_W2").T,
        "b2": get("ffn_b2").reshape(1, D),
        "scale": get("ffn_scale").reshape(1, 1),
    }
    return {k: np.ascontiguousarray(a) for k, a in laid.items()}


def kernel(**inputs):
    import numpy as np
    import concourse.bacc as bacc
    from concourse.bass_utils import run_bass_kernel_spmd

    nc = bacc.Bacc("TRN2", target_bir_lowering=False, num_devices=1)
    laid = arrays(inputs)
    args = [nc.dram_tensor(f"in_{name}", a.shape, mybir.dt.from_np(a.dtype), kind="ExternalInput").ap()
            for name, a in laid.items()]
    out = nc.dram_tensor("out", (TOKENS, D), F32, kind="ExternalOutput").ap()
    build(nc, *args, out)
    ran = run_bass_kernel_spmd(nc, [{f"in_{name}": a for name, a in laid.items()}], core_ids=[0])
    return np.asarray(ran.results[0]["out"]).reshape(B, L, D)
```

```python
from contextlib import ExitStack

import concourse.bass as bass
from concourse import mybir

ALU = mybir.AluOpType
ACT = mybir.ActivationFunctionType
F32 = mybir.dt.float32
F32R = mybir.dt.float32r

P = 128
B, L, D = 2, 4096, 256
TOKENS = B * L
KB = D // P
STATES = 16
TAPS = 3
ZB = 3 * D // P
CH = P
COLS = TOKENS // CH
BC = L // CH
FF = 672
FULL, REST = FF // P, FF % P
FB = FULL + 1
H = 1024
HB = H // P
EPS_LN, EPS_RMS = 1e-5, 1e-6

TA = 512
CA = TA // P
UA = TOKENS // TA
GC = P // STATES
GROUPS = D // GC
FIRST = 3
TC = 256
CC = TC // P
UC = TOKENS // TC
UCB = UC // B
LORA = 4


def is_step(n):
    return isinstance(n, int)


def valid(n, units):
    return not is_step(n) or 0 <= n < units


def wait(eng, sem, value):
    if not is_step(value) or value > 0:
        eng.wait_ge(sem, value)


def aggregate_after(dve, vector, mark, sem, value):
    dve.wait_ge(sem, value)
    vector.memset(mark, 0.0)


def run_steps(eng, step, plan):
    for part in plan:
        if is_step(part):
            step(2 * part, 0, part)
            step(2 * part + 1, 1, part)
        else:
            with eng.Fori(*part) as k:
                step(2 * k, 0, k)
                step(2 * k + 1, 1, k)


def build(nc, x, pre_w, in_w, short_w, short_b, lp_chan, lp_group, lp_flat, res_chan, res_group,
          d_skip, out_w, post_w, l1_w, l2_w, l3_w, w1, b1, w2, b2, scale, out):
    x2_dram = nc.dram_tensor("x2_scratch", (P, KB, TOKENS), F32, kind="Internal").ap()
    taps_dram = nc.dram_tensor("taps_scratch", (D, 2 * CH), F32, kind="Internal").ap()
    lora_dram = nc.dram_tensor("lora_scratch", (4 * LORA, D), F32, kind="Internal").ap()
    with ExitStack() as whole:
        def sb(ctx, name, shape, dt=F32):
            return ctx.enter_context(nc.sbuf_tensor(name, shape, dt))

        def ps(ctx, name, shape):
            return ctx.enter_context(nc.psum_tensor(name, shape, F32))

        def sem(ctx, name):
            return ctx.enter_context(nc.semaphore(name))

        ident = sb(whole, "ident", [P, P])
        neg_half = sb(whole, "neg_half", [P, 2, CA])
        ln_scale = sb(whole, "ln_scale", [P, COLS])
        ln_mean = sb(whole, "ln_mean", [P, COLS])
        x2s = sb(whole, "x2s", [P, KB, TC])
        x2_in = sem(whole, "x2_in")
        mark = sb(whole, "mark", [P, 1])
        seq = sb(whole, "seq", [P, D, COLS])
        wout = [sb(whole, f"wout_{s}", [P, KB, D], F32R) for s in "hl"]
        wl1 = [sb(whole, f"wl1_{s}", [P, KB, FULL * P], F32R) for s in "hl"]
        wl2 = [sb(whole, f"wl2_{s}", [P, KB, FULL * P], F32R) for s in "hl"]
        wrest = [sb(whole, f"wrest_{s}", [P, KB, 2 * REST], F32R) for s in "hl"]
        wl3 = [sb(whole, f"wl3_{s}", [P, FULL, D], F32R) for s in "hl"]
        wstack = sb(whole, "wstack", [3 * REST, D], F32R)

        with ExitStack() as early:
            lpg = sb(early, "lpg", [P, GROUPS])
            rg = sb(early, "rg", [P, GROUPS])
            lpb_first = sb(early, "lpb_first", [P, FIRST * P])
            to_end = sb(early, "to_end", [P, 1])
            ahead = sb(early, "ahead", [P, CH])
            own = sb(early, "own", [P, 2 * GC, BC])
            later = sb(early, "later", [P, 2 * GC, BC])
            x2_out = [sem(early, f"x2_out{i}") for i in range(2)]
            poles_in = sem(early, "poles_in")
            bconst = sem(early, "bconst")
            phase_a(nc, whole, sb, ps, sem, locals())
            phase_b(nc, sb, ps, sem, locals())
        phase_c(nc, sb, ps, sem, locals())


def phase_a(nc, whole, sb, ps, sem, v):
    ident, neg_half, seq = v["ident"], v["neg_half"], v["seq"]
    ln_scale, ln_mean, mark = v["ln_scale"], v["ln_mean"], v["mark"]
    x2_dram, taps_dram = v["x2_dram"], v["taps_dram"]
    POWERS = 8
    with ExitStack() as ctx:
        win_high = sb(ctx, "win_h", [P, KB, 3 * D], F32R)
        with ExitStack() as unsplit:
            win = sb(unsplit, "win", [P, KB, 3 * D])
        win_r = [win_high, sb(ctx, "win_l", [P, KB, 3 * D], F32R)]
        pre = sb(ctx, "pre", [P, KB])
        sw = sb(ctx, "sw", [P, ZB, TAPS])
        sbias = sb(ctx, "sbias", [P, ZB])
        lpc = sb(ctx, "lpc", [P, KB, STATES])
        rc = sb(ctx, "rc", [P, KB, STATES])
        dsk = sb(ctx, "dsk", [P, KB])
        back = sb(ctx, "back", [P, CH])
        pole_pow = sb(ctx, "pole_pow", [P, POWERS, CH])
        taps = sb(ctx, "taps", [P, KB, 2 * CH])
        zero_halo = sb(ctx, "zero_halo", [P, ZB, TAPS - 1])
        xa = sb(ctx, "xa", [P, 2, CA, D])
        stats = sb(ctx, "stats", [P, CA, 6])
        mv = sb(ctx, "mv", [P, 2, CA, 2])
        st = sb(ctx, "st", [P, 2, CA])
        minus = sb(ctx, "minus", [P, 2, CA])
        zn = sb(ctx, "zn", [P, CA, D])
        zt = [sb(ctx, f"zt_{s}", [P, 2, KB, TA], F32R) for s in "hl"]
        zbuf = sb(ctx, "zbuf", [P, 2, ZB, TA + TAPS - 1])
        conv = sb(ctx, "conv", [P, ZB - KB, TA])
        x2c = sb(ctx, "x2c", [P, 2, KB, TA])
        x2_tap = sb(ctx, "x2_tap", [P, KB, TA])
        xv = sb(ctx, "xv", [P, KB, TA])
        ps_t = ps(ctx, "ps_t", [P, KB, TA])
        ps_z = ps(ctx, "ps_z", [P, 3, TA])
        ps_x = ps(ctx, "ps_x", [P, CA, D])

        win_in = sem(ctx, "win_in")
        small_in = sem(ctx, "small_in")
        x_in = [sem(ctx, f"x_in{i}") for i in range(2)]
        x2_out = v["x2_out"]
        taps_out = sem(ctx, "taps_out")
        consts = sem(ctx, "consts")
        tap_exp = sem(ctx, "tap_exp")
        tap_sum = sem(ctx, "tap_sum")
        taps_ready = sem(ctx, "taps_ready")
        win_fold = sem(ctx, "win_fold")
        stats_done = sem(ctx, "stats_done")
        args_done = sem(ctx, "args_done")
        st_done = sem(ctx, "st_done")
        zn_done = sem(ctx, "zn_done")
        zt_done = sem(ctx, "zt_done")
        zh_done = sem(ctx, "zh_done")
        zl_done = sem(ctx, "zl_done")
        z_mm = sem(ctx, "z_mm")
        halo_done = sem(ctx, "halo_done")
        z_copy = sem(ctx, "z_copy")
        conv_done = sem(ctx, "conv_done")
        x2_prod = sem(ctx, "x2_prod")
        x2_done = sem(ctx, "x2_done")
        xv_done = sem(ctx, "xv_done")
        xt_done = sem(ctx, "xt_done")
        xs_done = sem(ctx, "xs_done")
        ST = 4
        TX_AT = 2
        DT = 2 * ZB - KB
        order = (2, 4, 3, 5, 0, 1)
        plan = (0, 1, (2, 4), 4, (5, 7), 7, 8)
        x_rows = v["x"].rearrange("(n c p) d -> n p c d", c=CA, p=P)

        def conv_of(m, par):
            return x2c[:, par, m] if m < KB else conv[:, m - KB]

        block = ctx.enter_context(nc.Block())

        @block.sync
        def _(sp):
            def xa_load(n, other):
                wait(sp, zn_done, CA * (n - 1))
                sp.dma_start(xa[:, 1 - other], x_rows[bass.ds(n, 1)].rearrange("n p c d -> (n p) c d")
                             ).then_inc(x_in[1 - other], 16)

            sp.dma_start(xa[:, 0], x_rows[0]).then_inc(x_in[0], 16)
            for dst, src in ((lpc, v["lp_chan"]), (rc, v["res_chan"]), (dsk, v["d_skip"]),
                             (pre, v["pre_w"]), (sw, v["short_w"]), (sbias, v["short_b"])):
                sp.dma_start(dst[:], src).then_inc(small_in, 16)
            sp.dma_start(win[:], v["in_w"].rearrange("(k p) o -> p k o", p=P)).then_inc(win_in, 16)
            xa_load(1, 0)
            sp.dma_start(v["lpg"][:], v["lp_group"]).then_inc(v["poles_in"], 16)
            sp.dma_start(v["rg"][:], v["res_group"]).then_inc(v["poles_in"], 16)
            sp.dma_start(v["lpb_first"][:], bass.AP(v["lp_flat"].tensor, 0, [[0, P], [1, FIRST * P]])
                         ).then_inc(v["poles_in"], 16)

            def step(n, par, k):
                if valid(n + 1, UA) and not (is_step(n) and n == 0):
                    xa_load(n + 1, par)

            run_steps(sp, step, plan)
            sp.wait_ge(taps_ready, KB + 1)
            sp.dma_start(taps_dram.rearrange("(k p) t -> p k t", p=P), taps[:]).then_inc(taps_out, 16)
            sp.wait_ge(taps_out, 16)

        @block.gpsimd
        def _(pool):
            nc.gpsimd.memset(ident[:], 1.0).then_inc(consts, 1)
            nc.gpsimd.memset(neg_half[:], -0.5).then_inc(consts, 1)
            nc.gpsimd.memset(zero_halo[:], 0.0).then_inc(consts, 1)
            nc.gpsimd.iota(back[:], [[-1, CH]], base=CH - 1, channel_multiplier=0,
                           allow_small_or_imprecise_dtypes=True).then_inc(consts, 1)
            pool.wait_ge(consts, 4)
            nc.gpsimd.affine_select(ident[:], ident[:], [[-1, P]], ALU.is_equal, 0.0, base=0,
                                    channel_multiplier=1).then_inc(consts, 1)

            nc.gpsimd.iota(v["to_end"][:], [[0, 1]], base=CH - 1, channel_multiplier=-1,
                           allow_small_or_imprecise_dtypes=True).then_inc(v["bconst"], 1)
            nc.gpsimd.iota(v["ahead"][:], [[-1, CH]], base=CH, channel_multiplier=0,
                           allow_small_or_imprecise_dtypes=True).then_inc(v["bconst"], 1)
            nc.gpsimd.memset(v["own"][:], 1.0).then_inc(v["bconst"], 1)
            nc.gpsimd.memset(v["later"][:], 1.0).then_inc(v["bconst"], 1)
            pool.wait_ge(v["bconst"], 4)
            nc.gpsimd.memset(v["later"][:, :, 0:1], 0.0).then_inc(v["bconst"], 1)
            nc.gpsimd.affine_select(v["own"][:], v["own"][:], [[-STATES, GC], [0, 2 * BC]], ALU.is_ge, 0.0,
                                    base=0, channel_multiplier=1).then_inc(v["bconst"], 1)
            pool.wait_ge(v["bconst"], 6)
            nc.gpsimd.affine_select(v["own"][:], v["own"][:], [[STATES, GC], [0, 2 * BC]], ALU.is_ge, 0.0,
                                    base=STATES - 1, channel_multiplier=-1).then_inc(v["bconst"], 1)

            def row_scales(n, par):
                pool.wait_ge(args_done, 3 * (n + 1))
                nc.gpsimd.tensor_tensor(st[:], st[:], neg_half[:], ALU.pow).then_inc(st_done, 1)
                pool.wait_ge(st_done, ST * n + 1)
                wait(pool, zt_done, n)
                nc.gpsimd.tensor_tensor(minus[:, 1], minus[:, 0], st[:, 1], ALU.mult
                                        ).then_inc(st_done, 1)
                pool.wait_ge(st_done, ST * n + 2)
                nc.gpsimd.tensor_copy(ln_scale[:, bass.ds(n * CA, CA)], st[:, 0]).then_inc(st_done, 1)
                for c in range(CA):
                    nc.gpsimd.tensor_scalar(zn[:, c], xa[:, par, c], st[:, 1, c:c + 1],
                                            minus[:, 1, c:c + 1], ALU.mult, ALU.add
                                            ).then_inc(zn_done, 1)
                nc.gpsimd.tensor_copy(ln_mean[:, bass.ds(n * CA, CA)], mv[:, par, :, 0]).then_inc(st_done, 1)

            row_scales(0, 0)

            def step(n, par, k):
                if valid(n + 1, UA):
                    row_scales(n + 1, 1 - par)
                if valid(n - 1, UA):
                    wait(pool, xt_done, n - 1)
                    for j in range(KB):
                        pool.wait_ge(conv_done, DT * (n - 1) + 4 * (j + 1))
                        nc.gpsimd.tensor_tensor(xv[:, j], conv[:, j], conv[:, KB + j], ALU.mult
                                                ).then_inc(xv_done, 1)
                    pool.wait_ge(conv_done, DT * n)
                    pool.wait_ge(x2_prod, KB * n)
                    for j in range(KB):
                        nc.gpsimd.tensor_tensor(x2c[:, 1 - par, j], x2c[:, 1 - par, j], x2_tap[:, j], ALU.add
                                                ).then_inc(x2_done, 1)

            run_steps(pool, step, plan)

        @block.scalar
        def _(act):
            act.wait_ge(small_in, 16 * 6)
            act.wait_ge(consts, 5)

            def powers(steps):
                for i in steps:
                    wait(act, tap_sum, i - POWERS + 1)
                    s, kb = divmod(i, KB)
                    nc.scalar.activation(pole_pow[:, i % POWERS], back[:], ACT.Exp,
                                         scale=lpc[:, kb, s:s + 1]).then_inc(tap_exp, 1)

            powers(range(POWERS))

            def gate_rows(n):
                act.wait_ge(xt_done, n + 1)
                nc.scalar.activation(seq[:, :, bass.ds(n * CA, CA)].rearrange("p h c -> p c h"),
                                     ps_x[:], ACT.Copy).then_inc(xs_done, 1)

            def step(n, par, k):
                u = n - 1
                if valid(u - 1, UA):
                    act.wait_ge(z_copy, 2 * ZB * u)
                    wait(act, x2_done, KB * (u - 1))
                    for j in range(KB):
                        nc.scalar.activation(x2_tap[:, j], zbuf[:, par, j, 0:TA], ACT.Copy,
                                             scale=sw[:, j, 0:1]).then_inc(x2_prod, 1)
                if valid(n, UA):
                    act.wait_ge(zt_done, n + 1)
                    wait(act, z_mm, ZB * (n - 1))
                    nc.scalar.activation(zt[0][:, par], ps_t[:], ACT.Copy).then_inc(zh_done, 1)
                if is_step(n) and n == 0:
                    powers(range(POWERS, KB * STATES))
                if valid(u, UA):
                    first = is_step(n) and u % (UA // B) == 0
                    wait(act, conv_done, DT * (u - 1))
                    wait(act, x2_prod, KB * (u - 1))
                    halo = zero_halo[:] if first else zbuf[:, par, :, TA:]
                    wait(act, z_copy, 2 * ZB * u)
                    nc.scalar.activation(zbuf[:, 1 - par, :, 0:TAPS - 1], halo, ACT.Copy
                                         ).then_inc(halo_done, 1)
                for i in range(ZB):
                    if valid(u - 1, UA) and i == 3:
                        gate_rows(u - 1)
                    if valid(u, UA):
                        m = order[i]
                        act.wait_ge(z_mm, ZB * u + i + 1)
                        nc.scalar.activation(zbuf[:, 1 - par, m, TAPS - 1:], ps_z[:, i % 3], ACT.Copy
                                             ).then_inc(z_copy, 1)
                        if i == 0:
                            wait(act, xv_done, KB * u)
                        if i == 4:
                            wait(act, x2_out[1 - par], 16 * (k - 1 + par))
                        nc.scalar.activation(conv_of(m, 1 - par), ps_z[:, i % 3], ACT.Identity,
                                             scale=sw[:, m, 2:3], bias=sbias[:, m:m + 1]
                                             ).then_inc(z_copy, 1)
                    if valid(u - 1, UA) and i == 3:
                        act.wait_ge(x2_done, KB * u)
                        act.dma_start(x2_dram[:, :, bass.ds((u - 1) * TA, TA)], x2c[:, par]
                                      ).then_inc(x2_out[par], 16)

            run_steps(act, step, plan)

        @block.vector
        def _(dve):
            nc.vector.memset(taps[:], 0.0).then_inc(taps_ready, 1)

            def row_stats(n, par, k):
                dve.wait_ge(x_in[par], 16 * (k + 1))
                wait(dve, st_done, ST * (n - 1))
                for c in range(CA):
                    nc.vector.bn_stats(stats[:, c], xa[:, par, c]).then_inc(stats_done, 1)
                aggregate_after(dve, nc.vector, mark[:], stats_done, 2 * CA * n + CA)
                for c in range(CA):
                    nc.vector.bn_aggr(mv[:, par, c], stats[:, c]).then_inc(stats_done, 1)
                dve.wait_ge(stats_done, 2 * CA * n + 2 * CA)
                wait(dve, st_done, ST * n)
                wait(dve, zn_done, CA * n)
                nc.vector.tensor_scalar(st[:, 0], mv[:, par, :, 1], EPS_LN, None, ALU.add
                                        ).then_inc(args_done, 1)
                nc.vector.tensor_scalar(st[:, 1], mv[:, par, :, 1], 1.0 + EPS_RMS, EPS_RMS * EPS_LN,
                                        ALU.mult, ALU.add).then_inc(args_done, 1)
                nc.vector.tensor_scalar(minus[:, 0], mv[:, par, :, 0], -1.0, None, ALU.mult
                                        ).then_inc(args_done, 1)

            row_stats(0, 0, 0)
            dve.wait_ge(small_in, 16 * 6)
            dve.wait_ge(win_in, 16)
            for k in range(KB):
                nc.vector.tensor_scalar(win[:, k], win[:, k], pre[:, k:k + 1], None, ALU.mult
                                        ).then_inc(win_fold, 1)
            dve.wait_ge(win_fold, KB)
            nc.vector.tensor_copy(win_r[0][:], win[:]).then_inc(win_fold, 1)
            dve.wait_ge(win_fold, KB + 1)
            nc.vector.tensor_tensor(win_r[1][:], win[:], win_r[0][:].bitcast(F32), ALU.subtract
                                    ).then_inc(win_fold, 1)

            def long_taps():
                dve.wait_ge(taps_ready, 1)
                for i in range(KB * STATES):
                    s, kb = divmod(i, KB)
                    dve.wait_ge(tap_exp, i + 1)
                    wait(dve, tap_sum, i - KB + 1)
                    nc.vector.scalar_tensor_tensor(taps[:, kb, 0:CH], pole_pow[:, i % POWERS],
                                                   rc[:, kb, s:s + 1], taps[:, kb, 0:CH],
                                                   ALU.mult, ALU.add).then_inc(tap_sum, 1)
                dve.wait_ge(tap_sum, KB * STATES)
                for k in range(KB):
                    nc.vector.tensor_tensor(taps[:, k, CH - 1:CH], taps[:, k, CH - 1:CH],
                                            dsk[:, k:k + 1], ALU.add).then_inc(taps_ready, 1)

            def step(n, par, k):
                if valid(n + 1, UA):
                    row_stats(n + 1, 1 - par, k + par)
                if valid(n, UA):
                    dve.wait_ge(zh_done, n + 1)
                    nc.vector.tensor_tensor(zt[1][:, par], ps_t[:], zt[0][:, par].bitcast(F32),
                                            ALU.subtract).then_inc(zl_done, 1)
                u = n - 1
                if is_step(n) and n == 0:
                    long_taps()
                if valid(u, UA):
                    dve.wait_ge(halo_done, n)
                    for i in range(0, ZB, 2):
                        for tap, (j, m) in ((t, (j, order[j])) for t in ((1, 0) if i < 2 * KB else (1,))
                                            for j in (i, i + 1)):
                            if tap:
                                dve.wait_ge(z_copy, 2 * ZB * u + 2 * j + 2)
                            else:
                                dve.wait_ge(conv_done, DT * u + i + j + 1)
                            nc.vector.scalar_tensor_tensor(conv_of(m, 1 - par),
                                                           zbuf[:, 1 - par, m, tap:TA + tap],
                                                           sw[:, m, tap:tap + 1], conv_of(m, 1 - par),
                                                           ALU.mult, ALU.add).then_inc(conv_done, 1)

            run_steps(dve, step, plan)

        @block.tensor
        def _(pe):
            pe.wait_ge(consts, 5)

            def turn_rows(n):
                pe.wait_ge(zn_done, CA * (n + 1))
                wait(pe, zl_done, n)
                for b in range(KB):
                    for c in range(CA):
                        mm = nc.tensor.transpose(ps_t[:, b, c * P:(c + 1) * P],
                                                 zn[:, c, b * P:(b + 1) * P], ident[:])
                mm.then_inc(zt_done, 1)

            def step(n, par, k):
                rows_late = is_step(n) and n == 1
                if valid(n, UA) and not rows_late:
                    turn_rows(n)
                u = n - 1
                if valid(u, UA):
                    if is_step(n) and u == 0:
                        pe.wait_ge(win_fold, KB + 2)
                    pe.wait_ge(zl_done, u + 1)
                for i in range(ZB):
                    if rows_late and i == TX_AT:
                        turn_rows(n)
                    if valid(u - 1, UA) and i == TX_AT:
                        pe.wait_ge(xv_done, KB * u)
                        wait(pe, xs_done, u - 1)
                        for c in range(CA):
                            for b in range(KB):
                                mm = nc.tensor.transpose(ps_x[:, c, b * P:(b + 1) * P],
                                                         xv[:, b, c * P:(c + 1) * P], ident[:])
                        mm.then_inc(xt_done, 1)
                    if valid(u, UA):
                        m = order[i]
                        wait(pe, z_copy, 2 * (ZB * u + i - 2))
                        passes = [(a, b, kk) for a, b in ((0, 0), (0, 1), (1, 0)) for kk in range(KB)]
                        for j, (a, b, kk) in enumerate(passes):
                            mm = nc.tensor.matmul(ps_z[:, i % 3], win_r[a][:, kk, m * P:(m + 1) * P],
                                                  zt[b][:, 1 - par, kk], start=(j == 0),
                                                  stop=(j == len(passes) - 1))
                        mm.then_inc(z_mm, 1)

            run_steps(pe, step, plan)


def phase_b(nc, sb, ps, sem, v):
    seq, taps_dram = v["seq"], v["taps_dram"]
    lpg, rg, lpb_first, poles_in, bconst = (v[n] for n in "lpg rg lpb_first poles_in bconst".split())
    to_end, ahead, own, later = (v[n] for n in "to_end ahead own later".split())
    with ExitStack() as ctx:
        lpb = sb(ctx, "lpb", [P, (GROUPS - FIRST) * P])
        pole_chunk = sb(ctx, "pole_chunk", [P, GROUPS])
        collect = sb(ctx, "collect", [P, 2, P])
        collect_r = [sb(ctx, f"collect_{s}", [P, 2, P], F32R) for s in "hl"]
        seq_r = [sb(ctx, f"seq_{s}", [P, 2, GC * COLS], F32R) for s in "hl"]
        spread = sb(ctx, "spread", [P, 2, CH])
        decay = sb(ctx, "decay", [P, 2, 2 * GC * BC])
        inflow = sb(ctx, "inflow", [P, 2, 2 * GC, BC])
        state = sb(ctx, "state", [P, 2, 2 * GC * BC])
        toep = sb(ctx, "toep", [P, 2, GC, CH])
        raw = sb(ctx, "raw", [P, KB, FF])
        post = sb(ctx, "post", [P, KB])
        ps_s = [ps(ctx, f"ps_s{i}", [P, 2 * GC, BC]) for i in range(2)]
        ps_y = [ps(ctx, f"ps_y{i}", [P, 2 * GC * BC]) for i in range(2)]

        poles_more = [sem(ctx, f"poles_more{i}") for i in range(3)]
        toep_in = [sem(ctx, f"toep_in{i}") for i in range(2)]
        raw_in = sem(ctx, "raw_in")
        split = sem(ctx, "split")
        inflow_clear = sem(ctx, "inflow_clear")
        pole_done = sem(ctx, "pole_done")
        collect_done = sem(ctx, "collect_done")
        high_done = sem(ctx, "high_done")
        low_done = sem(ctx, "low_done")
        spread_done = sem(ctx, "spread_done")
        decay_done = sem(ctx, "decay_done")
        s_mm = sem(ctx, "s_mm")
        toep_mm = sem(ctx, "toep_mm")
        y_mm = sem(ctx, "y_mm")
        inflow_done = sem(ctx, "inflow_done")
        scan_done = sem(ctx, "scan_done")
        y_done = sem(ctx, "y_done")
        plan = (0, 1, (2, GROUPS // 2 - 1), GROUPS // 2 - 1)
        pole_pieces = (0, 3 * P, 16 * P, (GROUPS - FIRST) * P)
        folded = ((v["l2_w"], v["wl2"], 0), (v["l1_w"], v["wl1"], REST))

        block = ctx.enter_context(nc.Block())

        @block.sync
        def _(sp):
            def load(g, par):
                src = bass.AP(taps_dram.tensor, 2 * CH * GC * g, [[1, P], [2 * CH, GC], [1, CH]])
                wait(sp, toep_mm, g - 1)
                sp.dma_start(toep[:, par], src).then_inc(toep_in[par], 16)

            def load_poles(i):
                start, end = pole_pieces[i:i + 2]
                sp.dma_start(lpb[:, start:end],
                             bass.AP(v["lp_flat"].tensor, FIRST * P + start, [[0, P], [1, end - start]])
                             ).then_inc(poles_more[i], 16)

            load(0, 0)
            load(1, 1)
            load_poles(0)

            def step(g, par, k):
                if not (is_step(g) and g == 0) and valid(g + 1, GROUPS):
                    load(g + 1, 1 - par)
                if is_step(g) and g in (1, 2):
                    load_poles(g)

            run_steps(sp, step, plan)
            for i in range(2):
                sp.wait_ge(v["x2_out"][i], 16 * UA // 2)
            sp.dma_start(v["x2s"][:], v["x2_dram"][:, :, 0:TC]).then_inc(v["x2_in"], 16)
            sp.wait_ge(v["x2_in"], 16)

        @block.gpsimd
        def _(pool):
            wout, wl3, wrest, wstack = v["wout"], v["wl3"], v["wrest"], v["wstack"]
            raw_out = raw[:, :, 0:D]
            raw_l3 = raw[:].rearrange("p k f -> p (k f)")[:, 0:FULL * D].rearrange("p (m o) -> p m o", o=D)
            raw_stack = raw[0:3 * REST, 0, 0:D]
            count, loads = 0, 0
            pool.dma_start(post[:], v["post_w"]).then_inc(raw_in, 16)
            loads += 16
            pool.wait_ge(raw_in, loads)
            for src, dst, at in folded:
                pool.dma_start(raw[:], src.rearrange("(k p) f -> p k f", p=P)).then_inc(raw_in, 16)
                loads += 16
                pool.wait_ge(raw_in, loads)
                for kk in range(KB):
                    nc.gpsimd.tensor_scalar(raw[:, kk], raw[:, kk], post[:, kk:kk + 1], 1.0,
                                            ALU.mult, ALU.mult).then_inc(split, 1)
                count += KB
                pool.wait_ge(split, count)
                parts = ((raw[:, :, 0:FULL * P], [w[:] for w in dst]),
                         (raw[:, :, FULL * P:], [w[:, :, at:at + REST] for w in wrest]))
                for piece, (high, low) in parts:
                    nc.gpsimd.tensor_copy(high, piece).then_inc(split, 1)
                    count += 1
                    pool.wait_ge(split, count)
                    nc.gpsimd.tensor_tensor(low, piece, high.bitcast(F32), ALU.subtract
                                            ).then_inc(split, 1)
                    count += 1
                pool.wait_ge(split, count)
            pieces = [(v["out_w"].rearrange("(k p) o -> p k o", p=P), raw_out,
                       wout[0][:], wout[1][:])]
            pieces.append((v["l3_w"][0:FULL * P].rearrange("(m p) o -> p m o", p=P), raw_l3,
                           wl3[0][:], wl3[1][:]))
            for src, stage, high, low in pieces:
                pool.dma_start(stage, src).then_inc(raw_in, 16)
                loads += 16
                pool.wait_ge(raw_in, loads)
                nc.gpsimd.tensor_copy(high, stage).then_inc(split, 1)
                count += 1
                pool.wait_ge(split, count)
                nc.gpsimd.tensor_tensor(low, stage, high.bitcast(F32), ALU.subtract).then_inc(split, 1)
                count += 1
                pool.wait_ge(split, count)

            for q in range(3):
                pool.dma_start(raw_stack[q * REST:(q + 1) * REST], v["l3_w"][FULL * P:]
                               ).then_inc(raw_in, 16)
                loads += 16
            pool.wait_ge(raw_in, loads)
            nc.gpsimd.tensor_copy(wstack[:], raw_stack).then_inc(split, 1)
            count += 1
            pool.wait_ge(split, count)
            mid = slice(REST, 2 * REST)
            nc.gpsimd.tensor_tensor(wstack[mid], raw_stack[mid], wstack[mid].bitcast(F32), ALU.subtract
                                    ).then_inc(split, 1)
            count += 1
            pool.wait_ge(split, count)

        @block.scalar
        def _(act):
            act.wait_ge(poles_in, 48)
            act.wait_ge(bconst, 7)
            nc.scalar.activation(pole_chunk[:], lpg[:], ACT.Exp, scale=float(CH)).then_inc(pole_done, 1)
            act.wait_ge(pole_done, 1)

            def gather(g, par):
                if is_step(g) and g < FIRST:
                    poles = lpb_first[:, g * P:(g + 1) * P]
                else:
                    for i in range(1 if is_step(g) and (g - FIRST) * P < pole_pieces[1] else 3):
                        act.wait_ge(poles_more[i], 16)
                    poles = lpb[:, bass.ds((g - FIRST) * P, P)]
                wait(act, s_mm, g - 1)
                nc.scalar.activation(collect[:, par], poles, ACT.Exp,
                                     scale=to_end[:, 0:1]).then_inc(collect_done, 1)
                nc.scalar.activation(seq_r[0][:, par], seq[:, bass.ds(g * GC, GC), :].rearrange("p h c -> p (h c)"),
                                     ACT.Copy).then_inc(high_done, 1)
                act.wait_ge(collect_done, g + 1)
                nc.scalar.activation(collect_r[0][:, par], collect[:, par], ACT.Copy).then_inc(high_done, 1)

            def powers(g, par):
                wait(act, scan_done, g - 1)
                nc.scalar.activation(decay[:, par], later[:].rearrange("p c j -> p (c j)"), ACT.Copy,
                                     scale=pole_chunk[:, bass.ds(g, 1)]).then_inc(decay_done, 1)
                wait(act, y_mm, g - 1)
                nc.scalar.activation(spread[:, par], ahead[:], ACT.Exp, scale=lpg[:, bass.ds(g, 1)]
                                     ).then_inc(spread_done, 1)

            gather(0, 0)
            gather(1, 1)
            powers(0, 0)

            def take(g, par):
                act.wait_ge(y_mm, g + 1)
                nc.scalar.activation(seq[:, bass.ds(g * GC, GC), :], ps_y[par][:], ACT.Copy
                                     ).then_inc(y_done, 1)

            def step(g, par, k):
                if valid(g + 2, GROUPS):
                    gather(g + 2, par)
                if valid(g + 1, GROUPS):
                    powers(g + 1, 1 - par)
                if valid(g - 1, GROUPS):
                    take(g - 1, 1 - par)

            run_steps(act, step, plan)
            take(GROUPS - 1, 1)

        @block.vector
        def _(dve):
            dve.wait_ge(poles_in, 48)
            dve.wait_ge(bconst, 7)
            for i in range(2):
                nc.vector.memset(inflow[:, i, :, 0:1], 0.0).then_inc(inflow_clear, 1)
            dve.wait_ge(inflow_clear, 2)

            def low_parts(g, par):
                dve.wait_ge(high_done, 2 * (g + 1))
                for low, src, high in ((seq_r[1], seq[:, bass.ds(g * GC, GC), :].rearrange("p h c -> p (h c)"),
                                        seq_r[0]), (collect_r[1], collect[:, par], collect_r[0])):
                    nc.vector.tensor_tensor(low[:, par], src, high[:, par].bitcast(F32), ALU.subtract
                                            ).then_inc(low_done, 1)

            low_parts(0, 0)
            low_parts(1, 1)

            def step(g, par, k):
                dve.wait_ge(s_mm, g + 1)
                wait(dve, scan_done, g - 1)
                nc.vector.scalar_tensor_tensor(inflow[:, par, :, 1:BC], ps_s[par][:, :, 0:BC - 1],
                                               rg[:, bass.ds(g, 1)], own[:, :, 0:BC - 1],
                                               ALU.mult, ALU.mult).then_inc(inflow_done, 1)
                dve.wait_ge(inflow_done, g + 1)
                dve.wait_ge(decay_done, g + 1)
                wait(dve, y_mm, g - 1)
                nc.vector.tensor_tensor_scan(state[:, par], decay[:, par],
                                             inflow[:, par].rearrange("p c j -> p (c j)"), 0.0,
                                             ALU.mult, ALU.add).then_inc(scan_done, 1)
                if valid(g + 2, GROUPS):
                    low_parts(g + 2, par)

            run_steps(dve, step, plan)

        @block.tensor
        def _(pe):
            def states_of(g, par):
                pe.wait_ge(low_done, 2 * (g + 1))
                wait(pe, inflow_done, g - 1)
                for j, (a, b) in enumerate(((0, 0), (0, 1), (1, 0))):
                    mm = nc.tensor.matmul(ps_s[par][:].rearrange("p c j -> p (c j)"),
                                          collect_r[a][:, par], seq_r[b][:, par],
                                          start=(j == 0), stop=(j == 2))
                mm.then_inc(s_mm, 1)

            states_of(0, 0)

            def step(g, par, k):
                if valid(g + 1, GROUPS):
                    states_of(g + 1, 1 - par)
                pe.wait_ge(toep_in[par], 16 * (k + 1))
                wait(pe, y_done, g - 1)
                for c in range(GC):
                    mm = nc.tensor.matmul(ps_y[par][:, c * COLS:(c + 1) * COLS], toep[:, par, c],
                                          seq[:, bass.ds(g * GC + c, 1), :].rearrange("p h c -> p (h c)"),
                                          start=(c == 0), stop=False, skip_group_check=True)
                mm.then_inc(toep_mm, 1)
                pe.wait_ge(spread_done, g + 1)
                pe.wait_ge(scan_done, g + 1)
                nc.tensor.matmul(ps_y[par][:], spread[:, par], state[:, par], start=False, stop=True,
                                 skip_group_check=True).then_inc(y_mm, 1)

            run_steps(pe, step, plan)


def phase_c(nc, sb, ps, sem, v):
    ident, neg_half, seq = v["ident"], v["neg_half"], v["seq"]
    ln_scale, ln_mean, mark = v["ln_scale"], v["ln_mean"], v["mark"]
    wout, wl1, wl2, wl3 = v["wout"], v["wl1"], v["wl2"], v["wl3"]
    wrest, wstack = v["wrest"], v["wstack"]
    x2_dram, lora_dram = v["x2_dram"], v["lora_dram"]
    plan = (0, 1, (2, UCB // 2), UCB // 2, UCB // 2 + 1, (UCB // 2 + 2, UC // 2 - 1), UC // 2 - 1, UC // 2)
    PASSES = ((0, 0), (0, 1), (1, 0))
    PASSES_T = ((0, 0), (1, 0), (0, 1))
    ACT_HIGHS = FB - 2
    T3_AT = FB // 2
    RING = 4
    HIDS = 3
    with ExitStack() as ctx:
        we1_high, we2_high = (sb(ctx, name, shape, F32R) for name, shape in
                              (("we1_h", [P, KB, H]), ("we2_h", [P, HB, D])))
        with ExitStack() as weights_made:
            base1 = sb(weights_made, "base1", [P, KB, H])
            base2 = sb(weights_made, "base2", [P, HB, D])
        we1 = [we1_high, sb(ctx, "we1_l", [P, KB, H], F32R)]
        we2 = [we2_high, sb(ctx, "we2_l", [P, HB, D], F32R)]
        b1s = sb(ctx, "b1s", [P, HB])
        b2s = sb(ctx, "b2s", [P, CC, D])
        scale_s = sb(ctx, "scale_s", [P, 1])
        xs = sb(ctx, "xs", [P, 2, CC, D])
        x2s = v["x2s"]
        ys = sb(ctx, "ys", [P, CC, D])
        yf = sb(ctx, "yf", [P, KB, TC])
        yt = [sb(ctx, f"yt_{s}", [P, KB, TC], F32R) for s in "hl"]
        yrow = sb(ctx, "yrow", [P, 2, CC, D])
        rows = sb(ctx, "rows", [P, CC, D])
        zt = [sb(ctx, f"mt_{s}", [P, KB, TC], F32R) for s in "hl"]
        xt = [sb(ctx, f"xt_{s}", [P, KB, TC], F32R) for s in "hl"]
        gate = sb(ctx, "gate", [P, 2, TC])
        prod = sb(ctx, "prod", [P, 2, TC])
        pt = [sb(ctx, f"pt_{s}", [P, FULL, TC], F32R) for s in "hl"]
        pstack = sb(ctx, "pstack", [3 * REST, TC], F32R)
        x1 = sb(ctx, "x1", [P, 2, CC, D])
        hid = sb(ctx, "hid", [P, HIDS, TC])
        ht_high = sb(ctx, "ht_h", [P, HB, TC], F32R)
        with ExitStack() as weights_made:
            even = sb(weights_made, "even", [P, 2 * LORA, D])
        ht = [ht_high, sb(ctx, "ht_l", [P, HB, TC], F32R)]
        frow = sb(ctx, "frow", [P, CC, D])
        orow = sb(ctx, "orow", [P, CC, D])
        odd = sb(ctx, "odd", [P, KB, 2 * LORA])
        bn = sb(ctx, "bn", [P, 3, CC, 6])
        mva = sb(ctx, "mva", [P, CC, 2])
        mvx = sb(ctx, "mvx", [P, CC, 2])
        mvf = sb(ctx, "mvf", [P, CC, 2])
        sc = sb(ctx, "sc", [P, 4, CC])
        sums = sb(ctx, "sums", [P, CC])
        mark_act = sb(ctx, "mark_act", [P, 1])
        ps_t = ps(ctx, "ps_rt", [P, KB, TC])
        ps_o = ps(ctx, "ps_o", [P, CC, D])
        ps_m = ps(ctx, "ps_m", [P, CC, D])
        ps_w = ps(ctx, "ps_w", [P, CC, D])
        ring = [ps(ctx, f"ps_ring{i}", [P, 2, TC]) for i in range(RING)]

        x_in = [sem(ctx, f"cx_in{i}") for i in range(2)]
        names = """rows_out consts_in base1_in base2_in y_copied yt_mm yf_done yh_done yl_done o_mm yrow_u yrow_done
                   squared rms_arg rms_done zm_done zt_mm zh_done zl_done ml_mm gate_done prod_done
                   ph_done high_here pl_done stacked m_mm a_done a_stat a_var a_scale x1_hat x1_done x_stat x_var x_scale
                   xn_done xt_mm xh_done xl_done h_mm hid_done hh_done hl_even hl_odd w2_mm f_done
                   f_stat f_var f_scale f_norm out_done lora_out even1_in even2_in odd_done weight_add
                   weight_high low1_even low1_odd weight_low2"""
        S = {n: sem(ctx, "c_" + n) for n in names.split()}
        S["x2_in"] = v["x2_in"]

        x_rows = v["x"].rearrange("(n c p) d -> n p c d", c=CC, p=P)
        out_rows = v["out"].rearrange("(n c p) d -> n p c d", c=CC, p=P)
        PIECES = LORA + KB
        ADDS = 2 * LORA * KB

        def row_unit(t, n):
            return t[bass.ds(n, 1)].rearrange("n p c d -> (n p) c d")

        def piece(i):
            if i < LORA:
                span = slice(i * D, (i + 1) * D)
                return base1[:, :, span], we1[0][:, :, span], we1[1][:, :, span]
            return [w.rearrange("p (r j) o -> p j r o", j=KB)[:, i - LORA]
                    for w in (base2[:], we2[0][:], we2[1][:])]

        def product_views(m):
            if m < FULL:
                return pt[0][:, m], prod[:, m % 2], pt[1][:, m]
            return pstack[0:REST], prod[0:REST, m % 2], pstack[2 * REST:]

        def makes_weights(n):
            return is_step(n) and 0 <= n - 1 < UC and (n - 1) % UCB == 0

        block = ctx.enter_context(nc.Block())

        @block.sync
        def _(sp):
            sp.dma_start(xs[:, 0], x_rows[0]).then_inc(x_in[0], 16)
            sp.dma_start(b1s[:], v["b1"]).then_inc(S["consts_in"], 16)
            for c in range(CC):
                sp.dma_start(b2s[:, c], bass.AP(v["b2"].tensor, 0, [[0, P], [1, D]])
                             ).then_inc(S["consts_in"], 16)
            sp.dma_start(scale_s[:], bass.AP(v["scale"].tensor, 0, [[0, P], [1, 1]])
                         ).then_inc(S["consts_in"], 16)

            def store(n):
                sp.wait_ge(S["out_done"], n + 1)
                sp.dma_start(row_unit(out_rows, n), orow[:]).then_inc(S["rows_out"], 16)

            def step(n, par, k):
                if valid(n + 1, UC):
                    sp.wait_ge(S["yf_done"], n + 1)
                    sp.dma_start(x2s[:], x2_dram[:, :, bass.ds((n + 1) * TC, TC)]).then_inc(S["x2_in"], 16)
                if valid(n - 3, UC):
                    store(n - 3)
                if valid(n + 1, UC):
                    wait(sp, S["x1_done"], n)
                    sp.dma_start(xs[:, 1 - par], row_unit(x_rows, n + 1)).then_inc(x_in[1 - par], 16)
                if makes_weights(n):
                    made = (n - 1) // UCB
                    wait(sp, S["h_mm"], HB * (n - 1))
                    sp.dma_start(base1[:], v["w1"].rearrange("(k p) h -> p k h", p=P)).then_inc(S["base1_in"], 16)
                    sp.wait_ge(S["xn_done"], CC * n)
                    sp.dma_start(lora_dram, rows[1:1 + 4 * LORA, 0, :]).then_inc(S["lora_out"], 16)
                    sp.wait_ge(S["lora_out"], 16 * (made + 1))
                    wait(sp, S["w2_mm"], n - 1)
                    for bank, done in ((0, "even1_in"), (LORA, "even2_in")):
                        sp.dma_start(even[:, bank:bank + LORA],
                                     bass.AP(lora_dram.tensor, 2 * bank * D, [[0, P], [2 * D, LORA], [1, D]])
                                     ).then_inc(S[done], 16)
                    sp.dma_start(base2[:], v["w2"].rearrange("(m p) o -> p m o", p=P)).then_inc(S["base2_in"], 16)

            run_steps(sp, step, plan)
            store(UC - 1)
            sp.wait_ge(S["rows_out"], 16 * UC)

        @block.gpsimd
        def _(pool):
            def copy_y(n):
                wait(pool, S["yt_mm"], n)
                nc.gpsimd.tensor_copy(ys[:], seq[:, :, bass.ds(n * CC, CC)].rearrange("p h c -> p c h")
                                      ).then_inc(S["y_copied"], 1)

            def inverse_root(var, to, done, n):
                pool.wait_ge(S[var], n + 1)
                nc.gpsimd.tensor_tensor(sc[:, to], sc[:, to], neg_half[:, 0, 0:CC], ALU.pow
                                        ).then_inc(S[done], 1)

            nc.gpsimd.tensor_copy(ys[:, 0], seq[:, :, 0]).then_inc(S["y_copied"], 1)

            def add_out(n, par):
                pool.wait_ge(S["f_norm"], CC * (n + 1))
                wait(pool, S["rows_out"], 16 * n)
                nc.gpsimd.tensor_tensor(orow[:], frow[:], x1[:, par], ALU.add).then_inc(S["out_done"], 1)

            def step(n, par, k):
                if valid(n - 3, UC):
                    add_out(n - 3, 1 - par)
                if valid(n, UC):
                    inverse_root("rms_arg", 3, "rms_done", n)
                if valid(n - 1, UC):
                    inverse_root("a_var", 0, "a_scale", n - 1)
                if valid(n - 1, UC):
                    inverse_root("x_var", 1, "x_scale", n - 1)
                if valid(n + 1, UC):
                    copy_y(n + 1)
                if valid(n - 2, UC):
                    inverse_root("f_var", 2, "f_scale", n - 2)
                if makes_weights(n):
                    for q in range(1, LORA, 2):
                        pool.wait_ge(S["weight_high"], PIECES * ((n - 1) // UCB) + q + 1)
                        src, high, low = piece(q)
                        nc.gpsimd.tensor_tensor(low, src, high.bitcast(F32), ALU.subtract
                                                ).then_inc(S["low1_odd"], 1)
                    pool.wait_ge(S["weight_add"], ADDS * ((n - 1) // UCB + 1))
                if valid(n - 1, UC):
                    for m in range(0, HB, 2):
                        pool.wait_ge(S["hh_done"], HB * (n - 1) + m + 1)
                        nc.gpsimd.tensor_tensor(ht[1][:, m], hid[:, m % HIDS], ht[0][:, m].bitcast(F32),
                                                ALU.subtract).then_inc(S["hl_even"], 1)
                if makes_weights(n):
                    made = (n - 1) // UCB
                    pool.wait_ge(S["weight_high"], PIECES * (made + 1))
                    src, high, low = piece(PIECES - 1)
                    nc.gpsimd.tensor_tensor(low, src, high.bitcast(F32), ALU.subtract
                                            ).then_inc(S["weight_low2"], 1)

            run_steps(pool, step, plan)
            add_out(UC - 1, (UC - 1) % 2)

        @block.scalar
        def _(act):
            nc.scalar.activation(ys[:, 1], seq[:, :, 1], ACT.Copy).then_inc(S["y_copied"], 1)
            act.wait_ge(S["consts_in"], 16 * (CC + 2))

            def high_parts(made, pieces):
                for i in pieces:
                    adds = KB * (i + 1) if i < LORA else LORA * (KB + i - LORA + 1)
                    act.wait_ge(S["weight_add"], ADDS * made + adds)
                    src, high, low = piece(i)
                    nc.scalar.activation(high, src, ACT.Copy).then_inc(S["weight_high"], 1)

            def load_table(function):
                nc.scalar.activation(mark_act[:], neg_half[:, 0, 0:1], function)

            def step(n, par, k):
                if valid(n, UC):
                    act.wait_ge(S["yrow_done"], n + 1)
                    wait(act, S["rms_arg"], n)
                    wait(act, S["xt_mm"], n - 1)
                    for c in range(CC):
                        nc.scalar.activation(rows[:, c], yrow[:, par, c], ACT.Square,
                                             accum_out=sums[:, c:c + 1]).then_inc(S["squared"], 1)
                    act.wait_ge(S["rms_done"], n + 1)
                    for c in range(CC):
                        nc.scalar.activation(rows[:, c], yrow[:, par, c], ACT.Copy,
                                             scale=sc[:, 3, c:c + 1]).then_inc(S["zm_done"], 1)
                    act.wait_ge(S["zt_mm"], n + 1)
                    wait(act, S["ml_mm"], FB * n)
                    nc.scalar.activation(zt[0][:], ps_t[:], ACT.Copy).then_inc(S["zh_done"], 1)
                    load_table(ACT.Gelu_apprx_tanh)

                def product_high(m):
                    act.wait_ge(S["prod_done"], FB * n + m + 1)
                    if m == 0:
                        wait(act, S["m_mm"], n)
                    high, src = product_views(m)[:2]
                    nc.scalar.activation(high, src, ACT.Copy).then_inc(S["ph_done"], 1)

                def mlp_gate(m):
                    act.wait_ge(S["ml_mm"], FB * n + m + 1)
                    wait(act, S["prod_done"], FB * n + m - 1)
                    rows_of = slice(0, P) if m < FULL else slice(REST, 2 * REST)
                    nc.scalar.activation(gate[rows_of, m % 2], ring[m % RING][rows_of, 0],
                                         ACT.Gelu_apprx_tanh).then_inc(S["gate_done"], 1)
                    if m == FB - 1:
                        load_table(ACT.Gelu)
                    elif m > 0:
                        product_high(m - 1)

                if valid(n, UC):
                    for m in range(T3_AT):
                        mlp_gate(m)
                if valid(n - 1, UC):
                    act.wait_ge(S["xt_mm"], n)
                    wait(act, S["h_mm"], HB * (n - 1))
                    nc.scalar.activation(xt[0][:], ps_t[:], ACT.Copy).then_inc(S["xh_done"], 1)
                if valid(n, UC):
                    for m in range(T3_AT, FB):
                        mlp_gate(m)
                if makes_weights(n):
                    made = (n - 1) // UCB
                    wait(act, S["h_mm"], HB * (n - 1))
                    wait(act, S["w2_mm"], n - 1)
                    high_parts(made, range(LORA))
                if valid(n - 1, UC):
                    wait(act, S["w2_mm"], n - 1)
                    for m in range(HB):
                        b = HB * (n - 1) + m
                        act.wait_ge(S["h_mm"], b + 1)
                        half = HB // 2 * (n - 1)
                        if m < HIDS:
                            wait(act, S["hl_even"], half)
                            wait(act, S["hl_odd"], half)
                        else:
                            act.wait_ge(S["hl_odd" if (m - HIDS) % 2 else "hl_even"],
                                        half + (m - HIDS) // 2 + 1)
                        nc.scalar.activation(hid[:, m % HIDS], ring[(m + 2) % RING][:, 0], ACT.Gelu,
                                             bias=b1s[:, m:m + 1]).then_inc(S["hid_done"], 1)
                        if makes_weights(n) and m == HIDS - 1:
                            high_parts(made, range(LORA, PIECES))

            run_steps(act, step, plan)

        @block.vector
        def _(dve):
            def measure(src, kind, stat):
                for c in range(CC):
                    nc.vector.bn_stats(bn[:, kind, c], src[:, c]).then_inc(S[stat], 1)

            def aggregate(kind, mv, stat, var, n):
                aggregate_after(dve, nc.vector, mark[:], S[stat], 2 * CC * n + CC)
                for c in range(CC):
                    nc.vector.bn_aggr(mv[:, c], bn[:, kind, c]).then_inc(S[stat], 1)
                dve.wait_ge(S[stat], 2 * CC * (n + 1))
                nc.vector.tensor_scalar(sc[:, kind], mv[:, :, 1], EPS_LN, None, ALU.add
                                        ).then_inc(S[var], 1)

            def split_low(low, src, high, done):
                nc.vector.tensor_tensor(low, src, high.bitcast(F32), ALU.subtract).then_inc(S[done], 1)

            def gate_y(n, part):
                if part == 0:
                    dve.wait_ge(S["yt_mm"], n + 1)
                    dve.wait_ge(S["x2_in"], 16 * (n + 1))
                    wait(dve, S["yl_done"], n)
                    back = ps_t[:].rearrange("p b (c t) -> p (b c) t", t=CH)[:, :, ::-1]
                    nc.vector.tensor_tensor(yf[:].rearrange("p b (c t) -> p (b c) t", t=CH), back,
                                            x2s[:].rearrange("p b (c t) -> p (b c) t", t=CH), ALU.mult
                                            ).then_inc(S["yf_done"], 1)
                elif part == 1:
                    dve.wait_ge(S["yf_done"], n + 1)
                    wait(dve, S["o_mm"], n)
                    nc.vector.tensor_copy(yt[0][:], yf[:]).then_inc(S["yh_done"], 1)
                else:
                    dve.wait_ge(S["yh_done"], n + 1)
                    split_low(yt[1][:], yf[:], yt[0][:], "yl_done")

            def normalize_f(n):
                dve.wait_ge(S["f_scale"], n + 1)
                for c in range(CC):
                    nc.vector.tensor_scalar(frow[:, c], frow[:, c], mvf[:, c, 0:1], sc[:, 2, c:c + 1],
                                            ALU.subtract, ALU.mult).then_inc(S["f_norm"], 1)

            def step(n, par, k):
                if valid(n - 3, UC):
                    normalize_f(n - 3)
                old = 1 - par
                u = n - 1
                if valid(n, UC):
                    dve.wait_ge(x_in[par], 16 * (k + 1))
                    wait(dve, S["x1_hat"], CC * (n - 1))
                    for c in range(CC):
                        nc.vector.tensor_scalar(yrow[:, par, c], xs[:, par, c],
                                                ln_mean[:, bass.ds(n * CC + c, 1)],
                                                ln_scale[:, bass.ds(n * CC + c, 1)],
                                                ALU.subtract, ALU.mult).then_inc(S["yrow_u"], 1)
                if valid(u, UC):
                    dve.wait_ge(S["m_mm"], u + 1)
                    wait(dve, S["zm_done"], CC * (u + 1))
                    nc.vector.tensor_tensor(yrow[:, old], ps_m[:], yrow[:, old], ALU.add
                                            ).then_inc(S["a_done"], 1)
                if valid(n, UC):
                    dve.wait_ge(S["yrow_u"], CC * (n + 1))
                    dve.wait_ge(S["o_mm"], n + 1)
                    nc.vector.tensor_tensor(yrow[:, par], ps_o[:], yrow[:, par], ALU.add
                                            ).then_inc(S["yrow_done"], 1)
                if valid(u, UC):
                    dve.wait_ge(S["a_done"], u + 1)
                    wait(dve, S["x1_hat"], CC * u)
                    measure(yrow[:, old], 0, "a_stat")
                if valid(n, UC):
                    dve.wait_ge(S["squared"], CC * (n + 1))
                    wait(dve, S["zm_done"], CC * n)
                    nc.vector.tensor_scalar(sc[:, 3], sums[:], 1.0 / D, EPS_RMS, ALU.mult, ALU.add
                                            ).then_inc(S["rms_arg"], 1)
                if valid(u, UC):
                    aggregate(0, mva, "a_stat", "a_var", u)
                if valid(u, UC):
                    dve.wait_ge(S["a_scale"], u + 1)
                    wait(dve, S["out_done"], u - 1)
                    for c in range(CC):
                        nc.vector.tensor_scalar(x1[:, old, c], yrow[:, old, c], mva[:, c, 0:1],
                                                sc[:, 0, c:c + 1], ALU.subtract, ALU.mult
                                                ).then_inc(S["x1_hat"], 1)
                    dve.wait_ge(S["x1_hat"], CC * (u + 1))
                    nc.vector.tensor_tensor(x1[:, old], x1[:, old], xs[:, old], ALU.add
                                            ).then_inc(S["x1_done"], 1)
                if valid(n, UC):
                    dve.wait_ge(S["zh_done"], n + 1)
                    split_low(zt[1][:], ps_t[:], zt[0][:], "zl_done")
                if valid(u, UC):
                    dve.wait_ge(S["x1_done"], u + 1)
                    wait(dve, S["xn_done"], CC * u)
                    measure(x1[:, old], 1, "x_stat")
                if valid(u, UC):
                    aggregate(1, mvx, "x_stat", "x_var", u)
                if valid(u, UC):
                    dve.wait_ge(S["x_scale"], u + 1)
                    if valid(n, UC):
                        dve.wait_ge(S["zt_mm"], n + 1)
                    else:
                        wait(dve, S["xt_mm"], u)
                    for c in range(CC):
                        nc.vector.tensor_scalar(rows[:, c], x1[:, old, c], mvx[:, c, 0:1],
                                                sc[:, 1, c:c + 1], ALU.subtract, ALU.mult
                                                ).then_inc(S["xn_done"], 1)
                if valid(n - 2, UC):
                    w = n - 2
                    dve.wait_ge(S["w2_mm"], w + 1)
                    wait(dve, S["out_done"], w)
                    nc.vector.tensor_tensor(frow[:], ps_w[:], b2s[:], ALU.add).then_inc(S["f_done"], 1)
                    dve.wait_ge(S["f_done"], w + 1)
                    wait(dve, S["f_norm"], CC * w)
                    measure(frow[:], 2, "f_stat")
                    aggregate(2, mvf, "f_stat", "f_var", w)

                def mlp_product(m):
                    b = FB * n + m
                    dve.wait_ge(S["gate_done"], b + 1)
                    wait(dve, S["pl_done"], b - 1)
                    if m < FULL:
                        value, gated = ring[m % RING][:, 1], gate[:, m % 2]
                    else:
                        value, gated = ring[m % RING][0:REST, 0], gate[REST:2 * REST, m % 2]
                    nc.vector.tensor_tensor(product_views(m)[1], value, gated, ALU.mult
                                            ).then_inc(S["prod_done"], 1)
                    if m > 0:
                        product_low(m - 1)
                    if m == FB - 1:
                        product_low(m)

                def product_low(m):
                    high, src, low = product_views(m)
                    if m < ACT_HIGHS:
                        dve.wait_ge(S["ph_done"], ACT_HIGHS * n + m + 1)
                    else:
                        dve.wait_ge(S["prod_done"], FB * n + m + 1)
                        nc.vector.tensor_copy(high, src).then_inc(S["high_here"], 1)
                        dve.wait_ge(S["high_here"], (FB - ACT_HIGHS) * n + m - ACT_HIGHS + 1)
                    if m == FULL:
                        nc.vector.tensor_copy(pstack[REST:2 * REST], src).then_inc(S["stacked"], 1)
                    split_low(low, src, high, "pl_done")

                if valid(n, UC):
                    for m in range(T3_AT):
                        mlp_product(m)
                if valid(u, UC):
                    dve.wait_ge(S["xh_done"], u + 1)
                    split_low(xt[1][:], ps_t[:], xt[0][:], "xl_done")
                    if makes_weights(n):
                        scaled_odd((n - 1) // UCB)
                if valid(n, UC):
                    for m in range(T3_AT, FB):
                        if makes_weights(n) and m == FB - 1:
                            dve.wait_ge(S["even1_in"], 16 * ((n - 1) // UCB + 1))
                            dve.wait_ge(S["base1_in"], 16 * ((n - 1) // UCB + 1))
                            w1_pieces((n - 1) // UCB, range(LORA // 2))
                        mlp_product(m)
                if valid(n + 1, UC) and not valid(u, UC):
                    for part in range(3):
                        gate_y(n + 1, part)
                if makes_weights(n):
                    made = (n - 1) // UCB
                    w1_pieces(made, range(LORA // 2, LORA))
                    dve.wait_ge(S["even2_in"], 16 * (made + 1))
                    dve.wait_ge(S["base2_in"], 16 * (made + 1))
                    span = D // LORA
                    for i in range(LORA, PIECES):
                        for q in range(LORA):
                            add_rank_one(piece(i)[0][:, :, q * span:(q + 1) * span],
                                         even[:, LORA + q].rearrange("p (a r) -> p r a", r=LORA),
                                         odd[:, i - LORA, LORA + q:LORA + q + 1])
                if valid(u, UC):
                    for m in range(HB):
                        b = HB * u + m
                        dve.wait_ge(S["hid_done"], b + 1)
                        if m == 0:
                            wait(dve, S["w2_mm"], u)
                        nc.vector.tensor_copy(ht[0][:, m], hid[:, m % HIDS]).then_inc(S["hh_done"], 1)
                        if m % 2:
                            dve.wait_ge(S["hh_done"], b + 1)
                            split_low(ht[1][:, m], hid[:, m % HIDS], ht[0][:, m], "hl_odd")
                        if valid(n + 1, UC) and m in (1, 3, 5):
                            gate_y(n + 1, m // 2)
                if makes_weights(n):
                    for i in range(LORA, PIECES - 1):
                        low_part(made, i, "weight_low2")

            def scaled_odd(made):
                dve.wait_ge(S["xl_done"], UCB * made + 1)
                cols = [t[:, :, 2:2 + 4 * LORA:2].bitcast(F32) for t in xt]
                nc.vector.tensor_tensor(odd[:], cols[0], cols[1], ALU.add).then_inc(S["odd_done"], 1)
                dve.wait_ge(S["odd_done"], 2 * made + 1)
                nc.vector.tensor_scalar(odd[:], odd[:], scale_s[:, 0:1], None, ALU.mult
                                        ).then_inc(S["odd_done"], 1)
                dve.wait_ge(S["odd_done"], 2 * made + 2)

            def w1_pieces(made, pieces):
                for q in pieces:
                    for kb in range(KB):
                        add_rank_one(base1[:, kb, q * D:(q + 1) * D], even[:, q], odd[:, kb, q:q + 1])
                for q in pieces:
                    if q % 2 == 0:
                        low_part(made, q, "low1_even")

            def add_rank_one(weights, row, col):
                nc.vector.scalar_tensor_tensor(weights, row, col, weights, ALU.mult, ALU.add
                                               ).then_inc(S["weight_add"], 1)

            def low_part(made, i, done):
                dve.wait_ge(S["weight_high"], PIECES * made + i + 1)
                src, high, low = piece(i)
                split_low(low, src, high, done)

            for part in range(3):
                gate_y(0, part)
            dve.wait_ge(S["consts_in"], 16 * (CC + 2))
            run_steps(dve, step, plan)
            normalize_f(UC - 1)

        @block.tensor
        def _(pe):
            def product(out, lhs, rhs, blocks, only=None, closed=True, passes=PASSES, low_ready=None):
                todo = [(a, b, kk) for a, b in passes for kk in only or range(blocks)]
                opens = only is None or only[0] == 0
                closes = closed and (only is None or only[-1] == blocks - 1)
                for j, (a, b, kk) in enumerate(todo):
                    if low_ready and j == len(todo) - blocks:
                        pe.wait_ge(*low_ready)
                    mm = nc.tensor.matmul(out, lhs(a, kk), rhs(b, kk), start=(opens and j == 0),
                                          stop=(closes and j == len(todo) - 1))
                return mm

            def chunk(c):
                return slice(c * P, (c + 1) * P)

            def transpose_unit(dst, src):
                for b in range(KB):
                    for c in range(CC):
                        mm = nc.tensor.transpose(dst[:, b, chunk(c)], src[:, c, b * P:(b + 1) * P], ident[:])
                return mm

            def mlp_block(n, m):
                if m >= RING:
                    pe.wait_ge(S["prod_done"], FB * n + m - RING + 1)
                else:
                    wait(pe, S["hid_done"], HB * (n - 1) - (0 if m else 1))
                if m == 0:
                    pe.wait_ge(S["zh_done"], n + 1)
                bank = ring[m % RING]
                if m < FULL:
                    for side, w in enumerate((wl1, wl2)):
                        mm = product(bank[:, side], lambda a, kk: w[a][:, kk, m * P:(m + 1) * P],
                                     lambda b, kk: zt[b][:, kk], KB, passes=PASSES_T,
                                     low_ready=(S["zl_done"], n + 1) if m == side == 0 else None)
                else:
                    mm = product(bank[0:2 * REST, 0], lambda a, kk: wrest[a][:, kk],
                                 lambda b, kk: zt[b][:, kk], KB)
                mm.then_inc(S["ml_mm"], 1)

            def ffn_down(c, only=None):
                return product(ps_w[:, c], lambda a, m: ht[a][:, m, chunk(c)],
                               lambda b, m: we2[b][:, m], HB, only)

            def turn_y(n):
                pe.wait_ge(S["y_copied"], n + 2)
                transpose_unit(ps_t, ys).then_inc(S["yt_mm"], 1)

            def step(n, par, k):
                u, w = n - 1, n - 2
                if valid(u, UC):
                    pe.wait_ge(S["pl_done"], FB * (u + 1))
                    wait(pe, S["a_done"], u)
                    pe.wait_ge(S["stacked"], u + 1)
                    for c in range(CC):
                        product(ps_m[:, c], lambda a, m: pt[a][:, m, chunk(c)],
                                lambda b, m: wl3[b][:, m], FULL, closed=False)
                        mm = nc.tensor.matmul(ps_m[:, c], pstack[:, chunk(c)], wstack[:],
                                              start=False, stop=True)
                    mm.then_inc(S["m_mm"], 1)
                if valid(n, UC):
                    pe.wait_ge(S["yl_done"], n + 1)
                    wait(pe, S["yrow_done"], n)
                    for c in range(CC):
                        mm = product(ps_o[:, c], lambda a, kk: yt[a][:, kk, chunk(c)],
                                     lambda b, kk: wout[b][:, kk], KB)
                    mm.then_inc(S["o_mm"], 1)
                if valid(w, UC):
                    pe.wait_ge(S["hl_even"], HB // 2 * (w + 1))
                    pe.wait_ge(S["hl_odd"], HB // 2 * (w + 1))
                    wait(pe, S["f_done"], w)
                    if is_step(n) and w % UCB == 0:
                        pe.wait_ge(S["weight_low2"], KB * (w // UCB + 1))
                    ffn_down(0)
                    ffn_down(1, range(HB // 2))
                if valid(n, UC):
                    pe.wait_ge(S["zm_done"], CC * (n + 1))
                    pe.wait_ge(S["yf_done"], n + 1)
                    transpose_unit(ps_t, rows).then_inc(S["zt_mm"], 1)
                if valid(w, UC):
                    ffn_down(1, range(HB // 2, HB)).then_inc(S["w2_mm"], 1)
                if valid(n, UC):
                    for m in range(T3_AT):
                        mlp_block(n, m)
                if valid(u, UC):
                    pe.wait_ge(S["xn_done"], CC * (u + 1))
                    if valid(n, UC):
                        pe.wait_ge(S["zl_done"], n + 1)
                    else:
                        wait(pe, S["xl_done"], u)
                    transpose_unit(ps_t, rows).then_inc(S["xt_mm"], 1)
                if valid(n, UC):
                    for m in range(T3_AT, FB):
                        mlp_block(n, m)
                if valid(n + 1, UC):
                    if valid(u, UC):
                        pe.wait_ge(S["xl_done"], u + 1)
                    else:
                        pe.wait_ge(S["zl_done"], n + 1)
                    turn_y(n + 1)
                if valid(u, UC):
                    pe.wait_ge(S["xl_done"], u + 1)
                    for m in range(HB):
                        if m >= RING:
                            pe.wait_ge(S["hid_done"], HB * u + m - RING + 1)
                        elif valid(n, UC):
                            pe.wait_ge(S["prod_done"], FB * n + FB - RING + m + 1)
                        else:
                            pe.wait_ge(S["hid_done"], HB * u)
                        if makes_weights(n):
                            q = m * P // D
                            pe.wait_ge(S["low1_odd" if q % 2 else "low1_even"],
                                       LORA // 2 * (u // UCB) + q // 2 + 1)
                        product(ring[(m + 2) % RING][:, 0], lambda a, kk: we1[a][:, kk, m * P:(m + 1) * P],
                                lambda b, kk: xt[b][:, kk], KB).then_inc(S["h_mm"], 1)

            turn_y(0)
            run_steps(pe, step, plan)


def arrays(inputs):
    import numpy as np

    def get(name):
        return np.asarray(inputs["L0_" + name])

    def by_partition(a, p=P):
        a = a.reshape((a.shape[0] // p, p) + a.shape[1:])
        return np.ascontiguousarray(np.moveaxis(a, 0, 1))

    poles = get("attn_log_poles").reshape(D, STATES)
    residues = get("attn_residues")
    laid = {
        "x": get("attn_u").reshape(TOKENS, D),
        "pre_w": by_partition(get("attn_pre_norm_w")),
        "in_w": get("attn_in_proj_w").T,
        "short_w": by_partition(get("attn_short_w").reshape(3 * D, TAPS)),
        "short_b": by_partition(get("attn_short_b")),
        "lp_chan": by_partition(poles),
        "lp_group": poles.reshape(GROUPS, P).T,
        "lp_flat": poles.reshape(1, D * STATES),
        "res_chan": by_partition(residues),
        "res_group": residues.reshape(GROUPS, P).T,
        "d_skip": by_partition(get("attn_D_skip")),
        "out_w": get("attn_out_proj_w").T,
        "post_w": by_partition(get("attn_post_norm_w")),
        "l1_w": get("attn_l1_w").T,
        "l2_w": get("attn_l2_w").T,
        "l3_w": get("attn_l3_w").T,
        "w1": get("ffn_W1").T,
        "b1": by_partition(get("ffn_b1")),
        "w2": get("ffn_W2").T,
        "b2": get("ffn_b2").reshape(1, D),
        "scale": get("ffn_scale").reshape(1, 1),
    }
    return {k: np.ascontiguousarray(a) for k, a in laid.items()}


def kernel(**inputs):
    import numpy as np
    import concourse.bacc as bacc
    from concourse.bass_utils import run_bass_kernel_spmd

    nc = bacc.Bacc("TRN2", target_bir_lowering=False, num_devices=1)
    laid = arrays(inputs)
    args = [nc.dram_tensor(f"in_{name}", a.shape, mybir.dt.from_np(a.dtype), kind="ExternalInput").ap()
            for name, a in laid.items()]
    out = nc.dram_tensor("out", (TOKENS, D), F32, kind="ExternalOutput").ap()
    build(nc, *args, out)
    ran = run_bass_kernel_spmd(nc, [{f"in_{name}": a for name, a in laid.items()}], core_ids=[0])
    return np.asarray(ran.results[0]["out"]).reshape(B, L, D)
```
